# Optimizing a Trainium2 kernel written in Bass

```python
import numpy as np
import jax
import jax.numpy as jnp

def _softmax(x, axis=-1):
    return jax.nn.softmax(x, axis=axis)

def _gelu(x):
    return jax.nn.gelu(x, approximate=True)

def _silu(x):
    return jax.nn.silu(x)

def _sigmoid(x):
    return jax.nn.sigmoid(x)

def _layernorm(x, axis=-1, eps=1e-05):
    m = jnp.mean(x, axis=axis, keepdims=True)
    v = jnp.var(x, axis=axis, keepdims=True)
    return (x - m) / jnp.sqrt(v + eps)

def _scatter_add(tgt, idx, src, axis=0):
    return tgt.at[idx].add(src)

def _segment_sum(src, seg, n):
    return jax.ops.segment_sum(src, seg, n)
kernel_name = 'mk_gnn_resnorm_d4_gnn_r64_cd98ef'

def setup_inputs(seed: int=0):
    np.random.seed(seed)
    _w = jnp.asarray

    def _rec_inputs():
        import jax
        import jax.numpy as jnp
        _gk = jax.random.key(seed)
        x = -0.000202 + 1 * jax.random.normal(jax.random.fold_in(_gk, 1), (100000, 64), jnp.float32)
        src = jax.random.randint(jax.random.fold_in(_gk, 2), (25000,), 0, 100000, jnp.int32)
        dst = jax.random.randint(jax.random.fold_in(_gk, 3), (25000,), 0, 100000, jnp.int32)
        _o = jnp.argsort(dst, stable=True)
        src = src[_o]
        dst = dst[_o]
        edge_attr_32 = 0.000216709 + 1.00012 * jax.random.normal(jax.random.fold_in(_gk, 12), (25000, 32), jnp.float32)
        edge_weight = jax.random.uniform(jax.random.fold_in(_gk, 14), (25000,), jnp.float32, 0.0, 0.999999)
        return (x, src, dst, edge_attr_32, edge_weight)
    x, src, dst, edge_attr_32, edge_weight = _rec_inputs()

    def _L0_gnn_setup():
        import jax, jax.numpy as jnp
        import numpy as np
        N = 100000
        E = 25000
        IN_C = 64
        HID = 2 * IN_C
        OUT_C = 64
        key = jax.random.key(seed)
        k1, k2, k3, k4, k5, k6 = jax.random.split(key, 6)
        node_features = jax.random.normal(k1, (N, IN_C), dtype=jnp.float32)
        edge_index = jax.random.randint(k2, (2, E), 0, N, dtype=jnp.int64)
        W1 = jax.random.normal(k3, (IN_C, HID), dtype=jnp.float32) / np.sqrt(IN_C)
        b1 = jax.random.normal(k4, (HID,), dtype=jnp.float32) * 0.01
        W2 = jax.random.normal(k5, (HID, OUT_C), dtype=jnp.float32) / np.sqrt(HID)
        b2 = jax.random.normal(k6, (OUT_C,), dtype=jnp.float32) * 0.01
        return {'node_features': node_features, 'edge_index': edge_index, 'W1': W1, 'b1': b1, 'W2': W2, 'b2': b2}
    _L0_gnn_all = _L0_gnn_setup()
    _L0_gnn_in = {k: v for k, v in _L0_gnn_all.items() if k in ('W1', 'b1', 'W2', 'b2')}
    del _L0_gnn_all

    def _L1_gnn_setup():
        import jax, jax.numpy as jnp
        import numpy as np
        N = 50000
        E = 25000
        LAT, HID, OUT = (64, 128, 64)

        def _add_self_loops(edge_index, edge_attr, n):
            loop = jnp.arange(n, dtype=edge_index.dtype)
            src = jnp.concatenate([edge_index[0], loop])
            dst = jnp.concatenate([edge_index[1], loop])
            ew = jnp.concatenate([edge_attr, jnp.ones((n,), edge_attr.dtype)])
            return (src, dst, ew)

        def _gcn_conv(x, W, b, src, dst, ew, n):
            h = x @ W
            deg = jax.ops.segment_sum(ew, dst, num_segments=n)
            dinv = jnp.where(deg > 0, jax.lax.rsqrt(deg), 0.0)
            norm = dinv[src] * ew * dinv[dst]
            out = jax.ops.segment_sum(norm[:, None] * h[src], dst, num_segments=n)
            return out + b
        key = jax.random.key(seed)
        k = jax.random.split(key, 8)
        z = jax.random.normal(k[0], (N, LAT), jnp.float32)
        edge_index = jax.random.randint(k[1], (2, E), 0, N, dtype=jnp.int32)
        edge_attr = jax.random.uniform(k[2], (E,), jnp.float32)
        W1 = jax.random.normal(k[3], (LAT, HID), jnp.float32) / np.sqrt(LAT)
        b1 = jnp.zeros((HID,), jnp.float32)
        W2 = jax.random.normal(k[4], (HID, OUT), jnp.float32) / np.sqrt(HID)
        b2 = jnp.zeros((OUT,), jnp.float32)
        return {'z': z, 'edge_index': edge_index, 'edge_attr': edge_attr, 'W1': W1, 'b1': b1, 'W2': W2, 'b2': b2}
    _L1_gnn_all = _L1_gnn_setup()
    _L1_gnn_in = {k: v for k, v in _L1_gnn_all.items() if k in ('W1', 'b1', 'W2', 'b2')}
    del _L1_gnn_all

    def _L2_gnn_setup():
        import jax, jax.numpy as jnp
        import numpy as np
        N_NODES = 50000
        N_EDGES = 12500
        D = 64

        def _leaky_relu(x, slope=0.2):
            return jnp.where(x >= 0, x, slope * x)
        key = jax.random.key(seed)
        ks = jax.random.split(key, 6)
        feats = jax.random.normal(ks[0], (N_NODES, D), dtype=jnp.float32)
        src = jax.random.randint(ks[1], (N_EDGES,), 0, N_NODES, dtype=jnp.int32)
        dst = jax.random.randint(ks[2], (N_EDGES,), 0, N_NODES, dtype=jnp.int32)
        W = jax.random.normal(ks[3], (D, D), dtype=jnp.float32) * (1.0 / np.sqrt(D))
        attn_l = jax.random.normal(ks[4], (D,), dtype=jnp.float32) * (1.0 / np.sqrt(D))
        attn_r = jax.random.normal(ks[5], (D,), dtype=jnp.float32) * (1.0 / np.sqrt(D))
        bias = jnp.zeros((D,), dtype=jnp.float32)
        return {'feats': feats, 'src': src, 'dst': dst, 'W': W, 'attn_l': attn_l, 'attn_r': attn_r, 'bias': bias}
    _L2_gnn_all = _L2_gnn_setup()
    _L2_gnn_in = {k: v for k, v in _L2_gnn_all.items() if k in ('W', 'attn_l', 'attn_r', 'bias')}
    del _L2_gnn_all

    def _L3_gnn_setup():
        import jax, jax.numpy as jnp
        import numpy as np
        N_NODES = 50000
        N_EDGES = 12500
        D_NODE = 64
        D_EDGE = 32
        D_HID = 128

        def _mlp(x, W1, b1, W2, b2):
            return jax.nn.relu(x @ W1 + b1) @ W2 + b2
        key = jax.random.key(seed)
        ks = jax.random.split(key, 12)
        inp = {'nodes': jax.random.normal(ks[0], (N_NODES, D_NODE), dtype=jnp.float32), 'row': jax.random.randint(ks[1], (N_EDGES,), 0, N_NODES, dtype=jnp.int32), 'col': jax.random.randint(ks[2], (N_EDGES,), 0, N_NODES, dtype=jnp.int32), 'edge_features': jax.random.normal(ks[3], (N_EDGES, D_EDGE), dtype=jnp.float32)}
        d_in_msg = 2 * D_NODE + D_EDGE
        inp['mW1'] = jax.random.normal(ks[4], (d_in_msg, D_HID), dtype=jnp.float32) / np.sqrt(d_in_msg)
        inp['mb1'] = jnp.zeros((D_HID,), dtype=jnp.float32)
        inp['mW2'] = jax.random.normal(ks[5], (D_HID, D_NODE), dtype=jnp.float32) / np.sqrt(D_HID)
        inp['mb2'] = jnp.zeros((D_NODE,), dtype=jnp.float32)
        d_in_upd = 2 * D_NODE
        inp['uW1'] = jax.random.normal(ks[6], (d_in_upd, D_HID), dtype=jnp.float32) / np.sqrt(d_in_upd)
        inp['ub1'] = jnp.zeros((D_HID,), dtype=jnp.float32)
        inp['uW2'] = jax.random.normal(ks[7], (D_HID, D_NODE), dtype=jnp.float32) / np.sqrt(D_HID)
        inp['ub2'] = jnp.zeros((D_NODE,), dtype=jnp.float32)
        return inp
    _L3_gnn_all = _L3_gnn_setup()
    _L3_gnn_in = {k: v for k, v in _L3_gnn_all.items() if k in ('mW1', 'mb1', 'mW2', 'mb2', 'uW1', 'ub1', 'uW2', 'ub2')}
    del _L3_gnn_all
    return {'x': x, 'src': src, 'dst': dst, 'edge_attr_32': edge_attr_32, 'edge_weight': edge_weight, 'L0_gnn_W1': _L0_gnn_in['W1'], 'L0_gnn_b1': _L0_gnn_in['b1'], 'L0_gnn_W2': _L0_gnn_in['W2'], 'L0_gnn_b2': _L0_gnn_in['b2'], 'L1_gnn_W1': _L1_gnn_in['W1'], 'L1_gnn_b1': _L1_gnn_in['b1'], 'L1_gnn_W2': _L1_gnn_in['W2'], 'L1_gnn_b2': _L1_gnn_in['b2'], 'L2_gnn_W': _L2_gnn_in['W'], 'L2_gnn_attn_l': _L2_gnn_in['attn_l'], 'L2_gnn_attn_r': _L2_gnn_in['attn_r'], 'L2_gnn_bias': _L2_gnn_in['bias'], 'L3_gnn_mW1': _L3_gnn_in['mW1'], 'L3_gnn_mb1': _L3_gnn_in['mb1'], 'L3_gnn_mW2': _L3_gnn_in['mW2'], 'L3_gnn_mb2': _L3_gnn_in['mb2'], 'L3_gnn_uW1': _L3_gnn_in['uW1'], 'L3_gnn_ub1': _L3_gnn_in['ub1'], 'L3_gnn_uW2': _L3_gnn_in['uW2'], 'L3_gnn_ub2': _L3_gnn_in['ub2']}

def reference(x, src, dst, edge_attr_32, edge_weight, L0_gnn_W1, L0_gnn_b1, L0_gnn_W2, L0_gnn_b2, L1_gnn_W1, L1_gnn_b1, L1_gnn_W2, L1_gnn_b2, L2_gnn_W, L2_gnn_attn_l, L2_gnn_attn_r, L2_gnn_bias, L3_gnn_mW1, L3_gnn_mb1, L3_gnn_mW2, L3_gnn_mb2, L3_gnn_uW1, L3_gnn_ub1, L3_gnn_uW2, L3_gnn_ub2):
    import jax
    import jax.numpy as jnp

    def _L0_gnn_ref(node_features, edge_index, W1, b1, W2, b2):
        import jax, jax.numpy as jnp
        import numpy as np
        N = 100000
        E = 25000
        IN_C = 64
        HID = 2 * IN_C
        OUT_C = 64
        n = node_features.shape[0]
        h = jax.nn.relu(node_features @ W1 + b1)
        h = h @ W2
        loops = jnp.arange(n, dtype=edge_index.dtype)
        src = jnp.concatenate([edge_index[0], loops])
        dst = jnp.concatenate([edge_index[1], loops])
        deg = jax.ops.segment_sum(jnp.ones_like(dst, dtype=h.dtype), dst, num_segments=n)
        dinv = jnp.where(deg > 0, jax.lax.rsqrt(deg), 0.0)
        norm = dinv[src] * dinv[dst]
        msgs = h[src] * norm[:, None]
        out = jax.ops.segment_sum(msgs, dst, num_segments=n) + b2
        return out

    def _L1_gnn_ref(z, edge_index, edge_attr, W1, b1, W2, b2):
        import jax, jax.numpy as jnp
        import numpy as np
        N = 50000
        E = 25000
        LAT, HID, OUT = (64, 128, 64)

        def _add_self_loops(edge_index, edge_attr, n):
            loop = jnp.arange(n, dtype=edge_index.dtype)
            src = jnp.concatenate([edge_index[0], loop])
            dst = jnp.concatenate([edge_index[1], loop])
            ew = jnp.concatenate([edge_attr, jnp.ones((n,), edge_attr.dtype)])
            return (src, dst, ew)

        def _gcn_conv(x, W, b, src, dst, ew, n):
            h = x @ W
            deg = jax.ops.segment_sum(ew, dst, num_segments=n)
            dinv = jnp.where(deg > 0, jax.lax.rsqrt(deg), 0.0)
            norm = dinv[src] * ew * dinv[dst]
            out = jax.ops.segment_sum(norm[:, None] * h[src], dst, num_segments=n)
            return out + b
        n = z.shape[0]
        src, dst, ew = _add_self_loops(edge_index, edge_attr, n)
        hidden = jax.nn.relu(_gcn_conv(z, W1, b1, src, dst, ew, n))
        return _gcn_conv(hidden, W2, b2, src, dst, ew, n)

    def _L2_gnn_ref(feats, src, dst, W, attn_l, attn_r, bias):
        import jax, jax.numpy as jnp
        import numpy as np
        N_NODES = 50000
        N_EDGES = 12500
        D = 64

        def _leaky_relu(x, slope=0.2):
            return jnp.where(x >= 0, x, slope * x)
        n = feats.shape[0]
        h = _leaky_relu(feats)
        z = h @ W
        el = z @ attn_l
        er = z @ attn_r
        e = _leaky_relu(el[src] + er[dst])
        emax = jax.ops.segment_max(e, dst, num_segments=n)
        emax = jnp.where(jnp.isfinite(emax), emax, 0.0)
        ex = jnp.exp(e - emax[dst])
        denom = jax.ops.segment_sum(ex, dst, num_segments=n)
        denom = jnp.where(denom == 0, 1.0, denom)
        alpha = ex / denom[dst]
        msg = alpha[:, None] * z[src]
        rst = jax.ops.segment_sum(msg, dst, num_segments=n)
        return rst + bias

    def _L3_gnn_ref(nodes, row, col, edge_features, mW1, mb1, mW2, mb2, uW1, ub1, uW2, ub2):
        import jax, jax.numpy as jnp
        import numpy as np
        N_NODES = 50000
        N_EDGES = 12500
        D_NODE = 64
        D_EDGE = 32
        D_HID = 128

        def _mlp(x, W1, b1, W2, b2):
            return jax.nn.relu(x @ W1 + b1) @ W2 + b2
        msg_in = jnp.concatenate([nodes[row], nodes[col], edge_features], axis=-1)
        messages = _mlp(msg_in, mW1, mb1, mW2, mb2)
        aggregated = jax.ops.segment_sum(messages, col, num_segments=nodes.shape[0])
        upd_in = jnp.concatenate([nodes, aggregated], axis=-1)
        return _mlp(upd_in, uW1, ub1, uW2, ub2)
    edge_index = jnp.stack([src, dst])
    x = _layernorm(x + _L0_gnn_ref(x, edge_index, L0_gnn_W1, L0_gnn_b1, L0_gnn_W2, L0_gnn_b2), axis=-1)
    x = _layernorm(x + _L1_gnn_ref(x, edge_index, edge_weight, L1_gnn_W1, L1_gnn_b1, L1_gnn_W2, L1_gnn_b2), axis=-1)
    x = _layernorm(x + _L2_gnn_ref(x, src, dst, L2_gnn_W, L2_gnn_attn_l, L2_gnn_attn_r, L2_gnn_bias), axis=-1)
    x = _layernorm(x + _L3_gnn_ref(x, src, dst, edge_attr_32, L3_gnn_mW1, L3_gnn_mb1, L3_gnn_mW2, L3_gnn_mb2, L3_gnn_uW1, L3_gnn_ub1, L3_gnn_uW2, L3_gnn_ub2), axis=-1)
    return x

_drawn_inputs = setup_inputs


def setup_inputs(seed=0):
    import zlib

    import numpy as np

    out = dict(_drawn_inputs(seed))
    spreads = {'L1_gnn_b1': (0.0, 0.1),
     'L1_gnn_b2': (0.0, 0.1),
     'L2_gnn_bias': (0.0, 0.1),
     'L3_gnn_mb1': (0.0, 0.571),
     'L3_gnn_mb2': (0.0, 0.397),
     'L3_gnn_ub1': (0.0, 0.1),
     'L3_gnn_ub2': (0.0, 0.1)}
    factors = {'L0_gnn_b1': 8.0, 'L0_gnn_b2': 7.035, 'L2_gnn_attn_l': 3.937, 'L2_gnn_attn_r': 8.0}
    for name, (base, spread) in spreads.items():
        noise = np.random.default_rng([zlib.crc32(name.encode()), seed]).standard_normal(out[name].shape)
        drawn = base * np.exp(spread * noise) if base else spread * noise
        out[name] = jnp.asarray(drawn.astype(out[name].dtype))
    for name, factor in factors.items():
        out[name] = (out[name] * factor).astype(out[name].dtype)
    return out
```

```python
from contextlib import ExitStack

import concourse.bass as bass
from concourse import mybir

F32 = mybir.dt.float32
I32 = mybir.dt.int32
ALU = mybir.AluOpType
ACT = mybir.ActivationFunctionType
AX_X = mybir.AxisListType.X

N = 100000
E = 25000
D = 64
DE = 32
H = 128
R = 125
TB = 8
BLK = R * TB
BW = TB * D
TC = 4
CH = R * TC
CW = TC * D
NT = E // R
NC = E // CH
NB = N // BLK
NI = E // BLK
EPS = 1e-5
BIG = 3.0e38
FAR = 1.0e6


class Shared:

    def __init__(self, sem, base):
        self.sem, self.base = sem, base


class Unit:

    def __init__(self, n, real, stage, i, par, b2, b3):
        self.n, self.real, self.stage, self.i, self.par, self.b2, self.b3 = n, real, stage, i, par, b2, b3


def at_least(eng, sem, value):
    if isinstance(value, int) and value <= 0:
        return
    if isinstance(sem, Shared):
        sem, value = sem.sem, value + sem.base
    eng.wait_ge(sem, value)


def build(nc, t, out):
    ctx = ExitStack()
    with ctx:
        def sb(name, shape, dt=F32):
            return ctx.enter_context(nc.sbuf_tensor(name, shape, dt))

        def sem(name):
            return ctx.enter_context(nc.semaphore(name))

        def sems(prefix, names):
            return {n: sem(f"{prefix}_{n}") for n in names.split()}

        def dram(name, shape, dt=F32):
            return nc.dram_tensor(name, shape, dt, kind="Internal").ap()

        xs_d = dram("xs_rows", (E, D))
        xd_d = dram("xd_rows", (E, D))
        t0_d = dram("t0_h0", (E, D))
        t1_d = dram("t1_x1", (2 * E, D))
        t2_d = dram("t2_h2", (2 * E, D))
        t3_d = dram("t3_x2", (2 * E, D))
        t4_d = dram("t4_x3", (2 * E, D))
        info_d = dram("node_info", (N, 4))
        keep_d = dram("keep_row", (NC, CH))
        on_d = dram("on_row", (NC, CH))
        z_d = dram("z_cols", (NC, D + 2, CH))
        decay_d = dram("decay_row", (NC, CH))
        ex_d = dram("ex_row", (NC, CH))
        x3f_d = dram("x3_filled", (NC, D, CH))

        def chunks(ap):
            return ap.rearrange("(c k p) f -> c p k f", k=TC, p=R)

        def blocks(ap):
            return ap.rearrange("(b j p) f -> b p j f", j=TB, p=R)

        ident = sb("ident", [128, 128])
        w_top = [sb(f"w_top{s}", [128, H]) for s in range(3)]
        w_bot = [sb(f"w_bot{s}", [128, H]) for s in range(3)]
        w_dn = [sb(f"w_dn{s}", [H, 128]) for s in range(3)]
        b_up = sb("b_up", [H, 3])
        b_dn = sb("b_dn", [128, 3])
        b_row = sb("b_row", [128, 4, D])
        b_two = sb("b_two", [128, 3, 128])
        gat_w = sb("gat_w", [128, 128])
        gat_raw = sb("gat_raw", [128, D])
        gat_att = sb("gat_att", [128, D])
        gat_tmp = sb("gat_tmp", [128, D])
        w_msg = sb("w_msg", [128, H])
        w_edge = sb("w_edge", [128, H])
        w_msg2 = sb("w_msg2", [H, D])
        w_upd = sb("w_upd", [128, H])
        b_msg = sb("b_msg", [H, 1])
        b_msg2 = sb("b_msg2", [D, 1])
        mean6 = sb("mean6", [128, 8])
        eps = sb("eps", [128, 1])
        wide = sb("wide", [128, 8 * CH])
        info_fill = wide[0:R, 0:N // R * 4]

        src_i = sb("src_i", [R, NT], I32)
        dst_i = sb("dst_i", [R, NT], I32)
        ew_t = sb("ew_t", [R, NT])
        d0_t = sb("d0_t", [R, NT])
        d1_t = sb("d1_t", [R, NT])
        last_t = sb("last_t", [R, NT])
        w0_t = sb("w0_t", [R, NT])
        w1_t = sb("w1_t", [R, NT])
        gidx = sb("gidx", [R, NT], I32)
        gfl = sb("gfl", [R, NT])
        gbase = sb("gbase", [R, NT])
        slot_id = sb("slot_id", [R, NT])
        info_r = sb("info_r", [R, NT, 4])
        sidx = sb("sidx", [R, NT], I32)

        dst_c = sb("dst_c", [NC, CH + 2], I32)
        dstf_c = sb("dstf_c", [NC, CH + 2])
        ew_c = sb("ew_c", [NC, CH])
        one_c = sb("one_c", [NC, CH])
        keep_c = sb("keep_c", [NC, CH])
        last_c = sb("last_c", [NC, CH])
        on_c = sb("on_c", [NC, CH])
        s1_c = sb("s1_c", [NC, 2, CH])
        s2_c = sb("s2_c", [NC, 2, CH])
        s3_c = sb("s3_c", [NC, 2, CH])
        edge_c = sb("edge_c", [NC, 4])
        top = sb("top", [2, 2, NC + 1])
        carry_r = sb("carry_r", [2, NC + 1])
        carry_c = sb("carry_c", [NC, 2])

        x_in = [sb(f"x_in{i}", [R, BW]) for i in range(2)]
        x1_r_all = [sb(f"x1_r{i}", [128, BW]) for i in range(2)]
        x1_r = [b[0:R, :] for b in x1_r_all]
        x2_r_all = [sb(f"x2_r{i}", [128, BW]) for i in range(2)]
        x2_r = [b[0:R, :] for b in x2_r_all]
        x3_r_all = [sb(f"x3_r{i}", [128, BW]) for i in range(2)]
        x3_r = [b[0:R, :] for b in x3_r_all]
        x4_r_all = [sb(f"x4_r{i}", [128, BW]) for i in range(2)]
        x4_r = [b[0:R, :] for b in x4_r_all]
        h0_r_all = [sb(f"h0_r{i}", [128, BW]) for i in range(2)]
        h0_r = [b[0:R, :] for b in h0_r_all]
        h2_r_all = [sb(f"h2_r{i}", [128, BW]) for i in range(2)]
        h2_r = [b[0:R, :] for b in h2_r_all]
        xT = [sb(f"xT{i}", [128, CH]) for i in range(3)]
        hid = [sb(f"hid{i}", [128, 2, CH]) for i in range(2)]
        rT = [sb(f"rT{i}", [128, CH]) for i in range(2)]
        rc = sb("rc", [R, BW])
        sq = [sb(f"sq{i}", [R, BW]) for i in range(2)]
        y_r = sb("y_r", [R, BW])
        sq_b = sb("sq_b", [R, BW])
        mn = sb("mn", [R, TB])
        ss = [sb(f"ss{i}", [R, TB]) for i in range(2)]
        sd = [sb(f"sd{i}", [R, TB]) for i in range(2)]
        rs = sb("rs", [R, TB])
        ss_b, sd_b, rs_b = sb("ss_b", [R, TB]), sb("sd_b", [R, TB]), sb("rs_b", [R, TB])

        p_idx = [sb(f"p_idx{i}", [R, TB], I32) for i in range(2)]
        p_row = [sb(f"p_row{i}", [R, BW]) for i in range(2)]
        g_idx = [sb(f"g_idx{i}", [R, TC], I32) for i in range(4)]
        g_row = [sb(f"g_row{i}", [R, TC * 128]) for i in range(4)]
        o_idx = [sb(f"o_idx{i}", [R, TC], I32) for i in range(2)]

        l_src = [sb(f"l_src{i}", [R, CW]) for i in range(4)]
        l_a = [sb(f"l_a{i}", [R, TC * 128]) for i in range(4)]
        l_b = [sb(f"l_b{i}", [R, CW]) for i in range(4)]
        l_k = [sb(f"l_k{i}", [D + 1, CH]) for i in range(4)]
        l_m = [wide[0:D + 1, i * CH:(i + 1) * CH] for i in range(4, 8)]
        l_z = [wide[0:D + 1, i * CH:(i + 1) * CH] for i in range(4)]
        l_in = [b[:, 0:CH] for b in x1_r_all + x2_r_all]
        l_up = [b[:, 0:CH] for b in x3_r_all + x4_r_all]
        l_ea = [b[:, 0:CH] for b in h0_r_all + h2_r_all]
        m_r = [sb(f"m_r{i}", [R, TC * 128]) for i in range(2)]
        agg = [sb(f"agg{i}", [128, CH]) for i in range(2)]
        zx = [sb(f"zx{i}", [D + 2, CH]) for i in range(2)]
        lxT = [sb(f"lxT{i}", [128, CH]) for i in range(2)]
        lhid = [sb(f"lhid{i}", [128, CH]) for i in range(2)]
        lhid2 = [sb(f"lhid2{i}", [128, CH]) for i in range(2)]
        u_r = [sb(f"u_r{i}", [R, TC * 128]) for i in range(2)]
        v_r = sb("v_r", [R, CW])
        w_r = sb("w_r", [R, CW])
        n_r = [sb(f"n_r{i}", [R, CW]) for i in range(4)]
        lsq = sb("lsq", [R, CW])
        lmn, lss, lsd, lrs, lden = (sb(f"l_{x}", [R, TC]) for x in ("mn", "ss", "sd", "rs", "den"))
        zero1 = sb("zero1", [128, 1])

        bank = [ctx.enter_context(nc.psum_tensor(f"bank{i}", [128, 512], F32)) for i in range(4)]
        pair = [ctx.enter_context(nc.psum_tensor(f"pair{i}", [128, 2, 512], F32)) for i in range(2)]

        s_w = sem("weights_loaded")
        s_e = sem("edges_loaded")
        s_pad = sem("dst_padding_set")
        s_pool0 = sem("ident_steps")
        s_set = sem("sbuf_zeroed")
        s_prep = sem("dve_weight_steps")
        s_bt = sem("bias_transposed")
        s_c = sem("dve_scalar_steps")
        s_ct = sem("scalar_transposes")
        s_ca = sem("act_scalar_steps")
        s_rows = sem("scalar_rows_stored")
        s_init = sem("node_info_initialised")
        P = sems("pool", "copied idx0 idx1 xs0 xs1 xss0 xss1 sc0 sc1 inf0 inf1 xd0 xd1 xds0 xds1")
        Cn = sems("chain", "rowsT xT up hid dn res resT mean_sum mean centred h0 h0b h2 h2b sq ssum std rstd"
                           " rows y sq2 ssum2 std2 rstd2 rows2 in0 in1 out0 out1 s0st0 s0st1 s1st0 s1st1")

        ctx.enter_context(nc.allow_non_contiguous_dma(reason="bias columns and the chunks' neighbours, once"))
        block = ctx.enter_context(nc.Block())

        W1 = [t["L0_gnn_W1"], t["L1_gnn_W1"], t["L3_gnn_uW1"][0:D, :]]
        W2 = [t["L0_gnn_W2"], t["L1_gnn_W2"], t["L3_gnn_uW2"]]
        B1 = [t["L0_gnn_b1"], t["L1_gnn_b1"], t["L3_gnn_ub1"]]
        BR = [t["L0_gnn_b2"], t["L1_gnn_b2"], t["L2_gnn_bias"], t["L3_gnn_ub2"]]

        def column(ap):
            return ap.rearrange("(p a) -> p a", a=1)

        def everywhere(ap, p=128):
            return ap.rearrange("(a f) -> a f", a=1).to_broadcast([p, ap.shape[0]])

        weight_loads = []
        for s in range(3):
            weight_loads += [(w_top[s][0:D, :], W1[s]), (w_bot[s][D:128, :], W1[s]), (w_dn[s][:, 0:D], W2[s]),
                             (b_up[:, s:s + 1], column(B1[s]))]
        weight_loads += [(b_row[:, i, :], everywhere(BR[i])) for i in range(4)]
        weight_loads += [(gat_raw[0:D, :], t["L2_gnn_W"]), (gat_raw[D:128, :], t["L2_gnn_W"]),
                         (gat_att[0:D, :], everywhere(t["L2_gnn_attn_l"], D)),
                         (gat_att[D:128, :], everywhere(t["L2_gnn_attn_r"], D)),
                         (w_msg[:, :], t["L3_gnn_mW1"][0:128, :]), (w_edge[0:DE, :], t["L3_gnn_mW1"][128:160, :]),
                         (w_msg2[:, :], t["L3_gnn_mW2"]), (w_upd[0:D, :], t["L3_gnn_uW1"][D:128, :]),
                         (w_upd[D:128, :], t["L3_gnn_uW1"][0:D, :]),
                         (b_msg[:, :], column(t["L3_gnn_mb1"])), (b_msg2[:, :], column(t["L3_gnn_mb2"]))]
        ALL_W = 16 * len(weight_loads)
        dst2 = t["dst"].rearrange("(c j) -> c j", j=CH)
        edge_loads = [(dst_c[:, 1:CH + 1], dst2), (dst_c[1:NC, 0:1], dst2[0:NC - 1, CH - 1:CH]),
                      (dst_c[0:NC - 1, CH + 1:CH + 2], dst2[1:NC, 0:1]),
                      (ew_c[:, :], t["edge_weight"].rearrange("(c j) -> c j", j=CH)),
                      (src_i[:, :], t["src_by_tile"]), (dst_i[:, :], t["dst_by_tile"]),
                      (ew_t[:, :], t["edge_weight_by_tile"])]
        ALL_E = 16 * len(edge_loads)
        N_ONES = 3 + 4 + 4 + 4 + 2 + 2 + 2
        N_SET = 13

        STAGE = [1, 0, 2]
        LAST = NB + NI
        MS = (LAST + 5) // 2
        UNITS = 6 * MS
        W0 = NB // 2

        def unit(m, u):
            q, pos = u // 3, u % 3
            real = (not isinstance(m, int)) or 0 <= 6 * m + u < UNITS
            return Unit(m * 6 + u, real, STAGE[pos], m * 2 + q, q % 2, u % 2, u % 3)

        def node_slots(slot, eng, pairs_loop, straight_after):
            slot(0, -1)
            for u in range(6):
                slot(0, u)
            for lo, hi in pairs_loop:
                if isinstance(hi, int) and hi - lo > 1:
                    with eng.Fori(lo, hi, 1) as m:
                        for u in range(6):
                            slot(m, u)
                else:
                    for u in range(6):
                        slot(lo, u)
            for m in straight_after:
                for u in range(6):
                    slot(m, u)
            for u in range(5):
                slot(MS, u)

        def half(buf):
            return buf[:, :].rearrange("p (k f) -> p k f", f=128)[:, :, 0:D]

        def n_view(ap):
            return ap.rearrange("p (j f) -> p j f", f=D)

        def spread(col, n):
            return col.unsqueeze(2).to_broadcast([R, n, D])

        def row_bias(i, n):
            return b_row[0:R, i, :].unsqueeze(1).to_broadcast([R, n, D])

        def chunk_slots(slot, eng):
            for k in range(8):
                slot(k, k % 4, k // 4, True, k > 0)
            with eng.Fori(2, NC // 4, 1) as j:
                for q in range(4):
                    slot(j * 4 + q, q, j, True, True)
            for k in range(4 * (NC // 4), NC):
                slot(k, k % 4, k // 4, True, True)
            slot(NC, NC % 4, NC // 4, False, True)

        def before(k, q, h):
            return k - 1, (q - 1) % 4, (h if q else h - 1), (q - 1) % 2

        shared, counted = {}, {}

        def level_sems(names, twice=()):
            made = {}
            for name in names.split():
                if name not in shared:
                    shared[name], counted[name] = sem(f"level_{name}"), 0
                made[name] = Shared(shared[name], counted[name])
                counted[name] += NC * (2 if name in twice else 1)
            return made

        def in_turn(name, n, per_chunk):
            made = []
            for r in range(n):
                key = f"{name}{r}"
                if key not in shared:
                    shared[key], counted[key] = sem(f"level_{key}"), 0
                made.append(Shared(shared[key], counted[key]))
                counted[key] += per_chunk * len(range(r, NC, n))
            return made

        LA = level_sems("msg msgT agg aggT xdT xcol up hid dn t1 t2 t3 t4 t5 msum mean cen sq ssum std rstd rows")
        LB = level_sems("msg msgT agg aggT t1 t2 u uT ucol up hid dn rows")
        LC = level_sems("msg msgT agg aggT t1 t2 t3 t4 t5 sq ssum std rstd rows")
        LD = level_sems("lky1 lky2 lkyT col zx zc")
        LE = level_sems("msg agg aggT den den2 rden t1 t2 t3 sq ssum std rstd rows", twice=("msg",))
        LF = level_sems("msg msgT fill")
        LG = level_sems("srcT scol up hid dn msg agg up2 hid2 dn2 t1 t2 sq ssum std rstd rows")
        LD["c"], LD["ct"], LD["ca"] = sem("score_steps"), sem("score_transposes"), sem("score_exp")
        A_ld, A_st = in_turn("ld", 4, 48), in_turn("st", 4, 16)
        B_ld, B_ga, B_st = in_turn("ld", 4, 32), in_turn("ga", 4, 64), in_turn("st", 4, 16)
        C_ld, C_ga, C_st = in_turn("ld", 4, 48), in_turn("ga", 4, 64), in_turn("st", 4, 16)
        D_ld, D_ga, D_st = in_turn("ld", 4, 16), in_turn("ga", 4, 64), in_turn("zst", 2, 16)
        G_ld, G_st = in_turn("ld", 4, 64), in_turn("st", 4, 16)
        F_ld, F_st = in_turn("ld", 4, 32), in_turn("zst", 2, 16)
        M_ld, M_ga, M_sc = in_turn("ld", 4, 80), in_turn("ga", 4, 64), in_turn("sc", 2, 64)
        s_ones = sem("gat_ones_row")

        def all_stored(eng, st, k_total=NC, n=4):
            for r in range(n):
                at_least(eng, st[r], 16 * len(range(r, k_total, n)))

        @block.sync
        def _(sp):
            sp.wait_ge(s_pad, 1)
            for dst, src in edge_loads:
                sp.dma_start(dst, src).then_inc(s_e, 16)
            sp.wait_ge(s_set, N_SET)
            for dst, src in weight_loads:
                sp.dma_start(dst, src).then_inc(s_w, 16)
            sp.dma_start(info_d.rearrange("(p a) c -> p (a c)", p=R), info_fill).then_inc(s_init, 16)
            sp.wait_ge(s_c, C_ROWS)
            sp.dma_start(keep_d, keep_c[:, :]).then_inc(s_rows, 16)
            sp.dma_start(on_d, on_c[:, :]).then_inc(s_rows, 16)

            dense_in = t["x"].rearrange("(b p j) f -> b p (j f)", p=R, j=TB)
            dense_out = out.rearrange("(b p j) f -> b p (j f)", p=R, j=TB)
            xs_v = blocks(xs_d)
            in_sem, out_sem = [Cn["in0"], Cn["in1"]], [Cn["out0"], Cn["out1"]]
            s0_sem, s1_sem = [Cn["s0st0"], Cn["s0st1"]], [Cn["s1st0"], Cn["s1st1"]]

            def load(i, par, half, iso, first=False):
                if iso:
                    b, h0_read, xs_stored = i - NB, i - (NB + 1), (half - (NB // 2 - 1)) * 16
                    if not isinstance(i, int):
                        b = sp.snap(b)
                if iso:
                    at_least(sp, Cn["h0"], h0_read)
                if not first:
                    sp.wait_ge(Cn["rowsT"], i * 3 - 4)
                if iso:
                    sp.wait_ge([P["xss0"], P["xss1"]][par], xs_stored)
                    sp.dma_start(n_view(x_in[par][:, :]), xs_v[b]).then_inc(in_sem[par], 16)
                else:
                    sp.dma_start(x_in[par][:, :], dense_in[i]).then_inc(in_sem[par], 16)

            def store_dense(i, par):
                sp.wait_ge(Cn["rows"], i * 3 + 3)
                sp.dma_start(dense_out[i - 4], x4_r[par][:, :]).then_inc(out_sem[par], 16)

            def store_s0(i, par):
                b = i - NB
                sp.wait_ge(Cn["h0b"], b + 1)
                sp.dma_start(blocks(t0_d)[b], n_view(h0_r[par][:, :])).then_inc(s0_sem[par], 16)
                sp.wait_ge(Cn["rows"], i * 3 + 2)
                sp.dma_start(blocks(t1_d[E:2 * E, :])[b], n_view(x1_r[par][:, :])).then_inc(s0_sem[par], 16)

            def store_s1(i, par):
                b = i - NB - 2
                sp.wait_ge(Cn["h2b"], b + 1)
                sp.dma_start(blocks(t2_d[E:2 * E, :])[b], n_view(h2_r[par][:, :])).then_inc(s1_sem[par], 16)
                sp.wait_ge(Cn["rows"], i * 3 + 1)
                sp.dma_start(blocks(t3_d[E:2 * E, :])[b], n_view(x2_r[par][:, :])).then_inc(s1_sem[par], 16)
                sp.wait_ge(Cn["rows2"], i + 1)
                sp.dma_start(blocks(t4_d[E:2 * E, :])[b], n_view(x3_r[par][:, :])).then_inc(s1_sem[par], 16)

            def iteration(i):
                if i + 1 < LAST:
                    load(i + 1, (i + 1) % 2, (i + 1) // 2, i + 1 >= NB, first=i + 1 < 2)
                j = i - 1
                if NB <= j < LAST:
                    store_s0(j, j % 2)
                if NB + 2 <= j < LAST + 2:
                    store_s1(j, j % 2)
                if 4 <= j < NB + 4:
                    store_dense(j, j % 2)

            for i in range(-1, 6):
                iteration(i)
            with sp.Fori(3, NB // 2 - 1, 1) as m:
                for q in range(2):
                    load(m * 2 + (q + 1), (q + 1) % 2, None, False)
                    store_dense(m * 2 + (q - 1), (q - 1) % 2)
            for i in range(NB - 2, NB + 6):
                iteration(i)
            with sp.Fori(NB // 2 + 3, LAST // 2 - 1, 1) as m:
                for q in range(2):
                    load(m * 2 + (q + 1), (q + 1) % 2, m + (q + 1) // 2, True)
                    store_s0(m * 2 + (q - 1), (q - 1) % 2)
                    store_s1(m * 2 + (q - 1), (q - 1) % 2)
            for i in range(2 * (LAST // 2 - 1), LAST + 4):
                iteration(i)

            sp.wait_ge(s_ones, N_ONES)
            sp.wait_ge(s_rows, 32)
            for r in range(2):
                sp.wait_ge([P["xds0"], P["xds1"]][r], 16 * len(range(r, NI, 2)))
                sp.wait_ge(s0_sem[r], 32 * len(range(r, NI, 2)))

            def rows_of(table):
                return chunks(table[0:E, :])

            def level(loads, ld, used, st, done, where, width):
                def ld_chunk(k, q, first):
                    pairs = loads(k, q)
                    if not first:
                        for s in used:
                            at_least(sp, s, k - 3)
                    for to, frm in pairs:
                        sp.dma_start(to, frm).then_inc(ld[q].sem, 16)

                def st_chunk(k, q):
                    to, frm = where(k, q)
                    at_least(sp, done, k + 1)
                    sp.dma_start(to, frm).then_inc(st[q % len(st)].sem, 16)

                for k in range(4):
                    ld_chunk(k, k, True)
                for k in range(4):
                    st_chunk(k, k)
                    ld_chunk(k + 4, k, False)
                with sp.Fori(1, NC // 4 - 1, 1) as j:
                    for q in range(4):
                        st_chunk(j * 4 + q, q)
                        ld_chunk(j * 4 + (q + 4), q, False)
                for k in range(4 * (NC // 4 - 1), NC):
                    st_chunk(k, k % 4)
                    if k + 4 < NC:
                        ld_chunk(k + 4, k % 4, False)

            def bc(row_d, k, p):
                return row_d[k].rearrange("(a f) -> a f", a=1).to_broadcast([p, CH]) if isinstance(k, int) \
                    else row_d[k].rearrange("(a f) -> a f", a=1).to_broadcast([p, CH])

            def v4(ap):
                return ap.rearrange("p (k f) -> p k f", f=D)

            level(lambda k, q: [(v4(l_src[q][:, :]), chunks(t0_d)[k]), (half(l_a[q]), chunks(xd_d)[k]),
                                (l_k[q][0:D, :], bc(keep_d, k, D))],
                  A_ld, [LA["rows"]], A_st, LA["rows"], lambda k, q: (rows_of(t1_d)[k], v4(n_r[q][:, :])), CW)
            all_stored(sp, A_st)
            level(lambda k, q: [(half(l_a[q]), rows_of(t1_d)[k]), (l_k[q][0:D, :], bc(keep_d, k, D))],
                  B_ld, [LB["rows"]], B_st, LB["rows"], lambda k, q: (rows_of(t2_d)[k], v4(n_r[q][:, :])), CW)
            all_stored(sp, B_st)
            level(lambda k, q: [(half(l_a[q]), rows_of(t2_d)[k]), (v4(l_b[q][:, :]), rows_of(t1_d)[k]),
                                (l_k[q][0:D, :], bc(keep_d, k, D))],
                  C_ld, [LC["rows"]], C_st, LC["rows"], lambda k, q: (rows_of(t3_d)[k], v4(n_r[q][:, :])), CW)
            all_stored(sp, C_st)
            level(lambda k, q: [(half(l_a[q]), rows_of(t3_d)[k])],
                  D_ld, [LD["lky2"]], D_st, LD["zc"], lambda k, q: (z_d[k], zx[q % 2][:, :]), CW)
            for r in range(2):
                at_least(sp, D_st[r], 16 * len(range(r, NC, 2)))
            sp.dma_start(s1_c[:, 0, :], z_d[:, D, :]).then_inc(s_rows, 16)
            sp.dma_start(s1_c[:, 1, :], z_d[:, D + 1, :]).then_inc(s_rows, 16)
            sp.wait_ge(LD["c"], D_ROWS)
            sp.dma_start(decay_d, s2_c[:, 0, :]).then_inc(s_rows, 16)
            sp.dma_start(ex_d, s2_c[:, 1, :]).then_inc(s_rows, 16)
            sp.wait_ge(s_rows, 96)
            sp.wait_ge(s_ones, N_ONES)
            level(lambda k, q: [(l_z[q][0:D, :], z_d[k, 0:D, :]), (l_m[q][:, :], bc(ex_d, k, D + 1)),
                                (l_k[q][:, :], bc(decay_d, k, D + 1)), (v4(l_b[q][:, :]), rows_of(t3_d)[k])],
                  G_ld, [LE["rows"]], G_st, LE["rows"], lambda k, q: (rows_of(t4_d)[k], v4(n_r[q][:, :])), CW)
            all_stored(sp, G_st)
            def mirror(eng, k):
                return (NC - 1) - k if isinstance(k, int) else eng.snap(k * -1 + (NC - 1))

            level(lambda k, q: [(half(l_a[q]), rows_of(t4_d)[mirror(sp, k)]),
                                (l_k[q][0:D, :], bc(on_d, mirror(sp, k), D))],
                  F_ld, [LF["fill"]], F_st, LF["fill"],
                  lambda k, q: (x3f_d[mirror(sp, k)], agg[q % 2][0:D, :]), CW)
            for r in range(2):
                at_least(sp, F_st[r], 16 * len(range(r, NC, 2)))

            def ld_m(k, q, first):
                if not first:
                    at_least(sp, LG["rows"], k - 3)
                for to, frm in [(l_in[q][D:128, :], x3f_d[k]), (l_up[q][D:128, :], x3f_d[k]),
                                (l_ea[q][0:DE, :], t["edge_attr_cols"].rearrange("f (c j) -> c f j", j=CH)[k]),
                                (l_k[q][0:D, :], bc(keep_d, k, D)), (v4(l_b[q][:, :]), rows_of(t4_d)[k])]:
                    sp.dma_start(to, frm).then_inc(M_ld[q].sem, 16)

            for k in range(4):
                ld_m(k, k, True)
            for k in range(4):
                ld_m(k + 4, k, False)
            with sp.Fori(1, NC // 4 - 1, 1) as j:
                for q in range(4):
                    ld_m(j * 4 + (q + 4), q, False)
            for k in range(4 * (NC // 4), NC):
                ld_m(k, k % 4, False)

        @block.gpsimd
        def _(pool):
            g = nc.gpsimd
            g.memset(ident[:, :], 0.0).then_inc(s_pool0, 1)
            pool.wait_ge(s_pool0, 1)
            g.affine_select(out=ident[:, :], in_=ident[:, :], compare_op=ALU.not_equal, fill=1.0, base=0,
                            pattern=[[-1, 128]], channel_multiplier=1).then_inc(s_pool0, 1)
            g.iota(slot_id[:, :], pattern=[[R, NT]], base=0, channel_multiplier=1,
                   allow_small_or_imprecise_dtypes=True).then_inc(s_pool0, 1)
            g.iota(gbase[:, :], pattern=[[R, NT]], base=E, channel_multiplier=1,
                   allow_small_or_imprecise_dtypes=True).then_inc(s_pool0, 1)
            pool.wait_ge(s_e, ALL_E)
            n_nodes, n_rows = pool.to_reg(N), pool.to_reg(2 * E)

            bound = pool.alloc_register("row_bound")

            def settle(rows):
                pool.reg_add(bound, rows, -1)

            def over_units(body, total):
                body(0, 0, 0)
                body(1, 1, 0)
                with pool.Fori(1, total // 2, 1) as j:
                    for q in range(2):
                        body(j * 2 + q, q, j)
                for b in range(2 * (total // 2), total):
                    body(b, b % 2, b // 2)

            copied = [0]

            def rows_by_index(idx, sem_got, sem_stored, to_d, base):
                def body(b, par, half):
                    at_least(pool, sem_stored[par], half * 16)
                    g.tensor_copy(p_idx[par][:, :], idx[:, bass.ds(b * TB, TB)]).then_inc(P["copied"], 1)
                    pool.wait_ge(P["copied"], b + (base + 1))
                    settle(n_nodes)
                    for j in range(TB):
                        g.indirect_dma_start(
                            out=p_row[par][:, j * D:(j + 1) * D], out_offset=None, in_=t["x"],
                            in_offset=bass.IndirectOffsetOnAxis(ap=p_idx[par][:, j:j + 1], axis=0),
                            bounds_check=bound, oob_is_err=False).then_inc(sem_got[par], 16)
                    pool.wait_ge(sem_got[par], (half + 1) * (16 * TB))
                    pool.dma_start(blocks(to_d)[b], n_view(p_row[par][:, :])).then_inc(sem_stored[par], 16)
                over_units(body, NI)

            rows_by_index(src_i, [P["xs0"], P["xs1"]], [P["xss0"], P["xss1"]], xs_d, 0)

            pool.wait_ge(s_init, 16)
            pool.wait_ge(s_c, C_INFO)
            sc = [P["sc0"], P["sc1"]]

            def scatter_info(b, par, half):
                at_least(pool, sc[par], half * (16 * TB))
                g.tensor_copy(p_idx[par][:, :], sidx[:, bass.ds(b * TB, TB)]).then_inc(P["copied"], 1)
                g.tensor_copy(p_row[par][:, 0:TB * 4], info_r[:, :, :].rearrange("p t c -> p (t c)")
                              [:, bass.ds(b * (TB * 4), TB * 4)]).then_inc(P["copied"], 1)
                pool.wait_ge(P["copied"], b * 2 + (NI + 2))
                settle(n_nodes)
                for j in range(TB):
                    g.indirect_dma_start(
                        out=info_d, out_offset=bass.IndirectOffsetOnAxis(ap=p_idx[par][:, j:j + 1], axis=0),
                        in_=p_row[par][:, 4 * j:4 * j + 4], in_offset=None,
                        bounds_check=bound, oob_is_err=False).then_inc(sc[par], 16)

            for r in range(2):
                pool.wait_ge([P["xss0"], P["xss1"]][r], 16 * len(range(r, NI, 2)))
            over_units(scatter_info, NI)
            for r in range(2):
                pool.wait_ge(sc[r], 16 * TB * len(range(r, NI, 2)))

            got = [P["inf0"], P["inf1"]]

            def gather_info(b, par, half):
                g.tensor_copy(p_idx[par][:, :], src_i[:, bass.ds(b * TB, TB)]).then_inc(P["copied"], 1)
                pool.wait_ge(P["copied"], b * 2 + (3 * NI + 1))
                settle(n_nodes)
                for j in range(TB):
                    g.indirect_dma_start(
                        out=p_row[par][:, 4 * j:4 * j + 4], out_offset=None, in_=info_d,
                        in_offset=bass.IndirectOffsetOnAxis(ap=p_idx[par][:, j:j + 1], axis=0),
                        bounds_check=bound, oob_is_err=False).then_inc(got[par], 16)
                pool.wait_ge(got[par], (half + 1) * (16 * TB))
                g.tensor_copy(info_r[:, :, :].rearrange("p t c -> p (t c)")[:, bass.ds(b * (TB * 4), TB * 4)],
                              p_row[par][:, 0:TB * 4]).then_inc(P["copied"], 1)

            over_units(gather_info, NI)
            pool.wait_ge(P["copied"], 5 * NI)
            rows_by_index(dst_i, [P["xd0"], P["xd1"]], [P["xds0"], P["xds1"]], xd_d, 5 * NI)

            def gather_level(table, ga, used, n_before):
                def body(k, q, h):
                    used(k)
                    g.tensor_copy(g_idx[q][:, :], gidx[:, bass.ds(k * TC, TC)]).then_inc(P["copied"], 1)
                    pool.wait_ge(P["copied"], k + (7 * NI - NI + n_before + 1))
                    settle(n_rows)
                    for j in range(TC):
                        g.indirect_dma_start(
                            out=g_row[q][:, j * 128:j * 128 + D], out_offset=None, in_=table,
                            in_offset=bass.IndirectOffsetOnAxis(ap=g_idx[q][:, j:j + 1], axis=0),
                            bounds_check=bound, oob_is_err=False).then_inc(ga[q].sem, 16)
                for k in range(4):
                    body(k, k, 0)
                with pool.Fori(1, NC // 4, 1) as j:
                    for q in range(4):
                        body(j * 4 + q, q, j)
                for k in range(4 * (NC // 4), NC):
                    body(k, k % 4, k // 4)

            for r in range(2):
                pool.wait_ge([Cn["s0st0"], Cn["s0st1"]][r], 32 * len(range(r, NI, 2)))
                pool.wait_ge([Cn["s1st0"], Cn["s1st1"]][r], 48 * len(range(r, NI, 2)))
            pool.wait_ge(s_c, C_ALL)
            pool.wait_ge(s_ones, N_ONES)
            all_stored(pool, A_st)
            gather_level(t1_d, B_ga, lambda k: at_least(pool, LB["msg"], k - 3), 0)
            all_stored(pool, B_st)
            gather_level(t2_d, C_ga, lambda k: at_least(pool, LC["msg"], k - 3), NC)
            all_stored(pool, C_st)
            gather_level(t3_d, D_ga, lambda k: at_least(pool, LD["lky1"], k - 3), 2 * NC)
            all_stored(pool, G_st)

            out_sem = [Cn["out0"], Cn["out1"]]
            for r in range(2):
                pool.wait_ge(out_sem[r], 16 * len(range(r, NB, 2)))

            def m_gather(k, q):
                at_least(pool, LG["srcT"], k - 3)
                g.tensor_copy(g_idx[q][:, :], gidx[:, bass.ds(k * TC, TC)]).then_inc(P["copied"], 1)
                for j in range(TC):
                    if j == 0:
                        pool.wait_ge(P["copied"], m_copies(k, True))
                        settle(n_rows)
                    g.indirect_dma_start(
                        out=g_row[q][:, j * 128:j * 128 + D], out_offset=None, in_=t4_d,
                        in_offset=bass.IndirectOffsetOnAxis(ap=g_idx[q][:, j:j + 1], axis=0),
                        bounds_check=bound, oob_is_err=False).then_inc(M_ga[q].sem, 16)

            M_LAG = 4
            BASE = 6 * NI + 3 * NC

            def m_copies(k, gather):
                if gather:
                    if isinstance(k, int):
                        return BASE + k + 1 + max(0, k - M_LAG)
                    return k * 2 + (BASE + 1 - M_LAG)
                if isinstance(k, int):
                    return BASE + (k + 1) + min(NC, k + 1 + M_LAG)
                return k * 2 + (BASE + 2 + M_LAG)

            def m_scatter(k, q, h):
                par = q % 2
                if isinstance(k, int):
                    at_least(pool, M_sc[par], 64 * (k // 2))
                else:
                    at_least(pool, M_sc[par], h * 128 + (q // 2) * 64)
                g.tensor_copy(o_idx[par][:, :], sidx[:, bass.ds(k * TC, TC)]).then_inc(P["copied"], 1)
                pool.wait_ge(P["copied"], m_copies(k, False))
                at_least(pool, LG["rows"], k + 1)
                settle(n_nodes)
                for j in range(TC):
                    g.indirect_dma_start(
                        out=out, out_offset=bass.IndirectOffsetOnAxis(ap=o_idx[par][:, j:j + 1], axis=0),
                        in_=n_r[q][:, j * D:(j + 1) * D], in_offset=None,
                        bounds_check=bound, oob_is_err=False).then_inc(M_sc[par].sem, 16)

            for k in range(8):
                m_gather(k, k % 4)
                if k >= M_LAG:
                    m_scatter(k - M_LAG, k % 4, 0)
            with pool.Fori(2, NC // 4, 1) as j:
                for q in range(4):
                    m_gather(j * 4 + q, q)
                    m_scatter(j * 4 + (q - M_LAG), q, j - 1)
            for k in range(4 * (NC // 4), NC + M_LAG):
                if k < NC:
                    m_gather(k, k % 4)
                m_scatter(k - M_LAG, k % 4, 0)
            for r in range(2):
                at_least(pool, M_sc[r], 64 * len(range(r, NC, 2)))

        @block.tensor
        def _(pe):
            T = nc.tensor
            pe.wait_ge(s_pool0, 2)

            def turn(dst, src, rows, cols):
                return T.transpose(dst, src, ident[0:rows, 0:rows])

            def summaries(n, wait_sem, v, done):
                pe.wait_ge(wait_sem, v)
                turn(bank[3][0:n, 0:NC], edge_c[:, 0:n], NC, n)
                turn(bank[3][0:n, 64:64 + NC], edge_c[:, 2:2 + n], NC, n).then_inc(done, 1)

            summaries(2, s_c, C_SUM, s_ct)
            pe.wait_ge(s_c, C_CARRY)
            turn(bank[3][0:NC, 128:130], carry_r[0:2, 0:NC], 2, NC).then_inc(s_ct, 1)
            pe.wait_ge(s_c, C_DINV)
            order = [s3_c[:, 0, :], s3_c[:, 1, :], last_c[:, :], s2_c[:, 0, :]]
            for a, what in enumerate(order):
                for k in range(TC):
                    mm = turn(bank[a % 4][0:R, k * NC:(k + 1) * NC], what[:, k * R:(k + 1) * R], NC, R)
                mm.then_inc(s_ct, 1)
            pe.wait_ge(s_c, C_INFO)
            pe.wait_ge(s_prep, PREP_TWO)
            for s in range(3):
                T.transpose(bank[s][:, 0:128], b_two[:, s, :], ident[:, :]).then_inc(s_bt, 1)

            pe.wait_ge(s_prep, PREP_ALL)
            rows_in = {0: x_in, 1: x1_r, 2: x3_r}

            def slot(m, u):
                a = unit(m, u + 1)
                if a.real:
                    if a.stage == 0 and not (isinstance(a.i, int) and a.i >= LAST):
                        pe.wait_ge([Cn["in0"], Cn["in1"]][a.par], (m + (u + 1) // 3 // 2) * 16 + 16
                                   if not isinstance(m, int) else 16 * (a.i // 2 + 1))
                    if a.stage == 1:
                        at_least(pe, Cn["rows"], a.n - 4 if not isinstance(a.n, int) or a.i >= 2 else 0)
                    if a.stage == 2:
                        at_least(pe, Cn["rows2"], a.i - 1)
                    at_least(pe, Cn["xT"], a.n)
                    for k in range(4):
                        mm = turn(bank[0][:, k * R:(k + 1) * R], rows_in[a.stage][a.par][:, 128 * k:128 * k + 128], R, 128)
                    mm.then_inc(Cn["rowsT"], 1)
                a = unit(m, u - 2)
                if a.real:
                    pe.wait_ge(Cn["res"], a.n + 1)
                    at_least(pe, Cn["rows"], a.n - 1)
                    for k in range(4):
                        mm = turn(bank[2 + a.b2][0:R, 128 * k:128 * k + 128], rT[a.b2][:, k * R:(k + 1) * R], 128, R)
                    mm.then_inc(Cn["resT"], 1)
                a = unit(m, u)
                if a.real:
                    pe.wait_ge(Cn["xT"], a.n + 1)
                    at_least(pe, Cn["hid"], a.n - 1)
                    T.matmul(pair[a.b2][:, 0, 0:CH], w_top[a.stage][:, :], xT[a.b3][:, :], start=True, stop=True)
                    T.matmul(pair[a.b2][:, 1, 0:CH], w_bot[a.stage][:, :], xT[a.b3][:, :], start=True, stop=True)\
                     .then_inc(Cn["up"], 1)
                a = unit(m, u - 1)
                if a.real:
                    pe.wait_ge(Cn["hid"], a.n + 1)
                    at_least(pe, Cn["res"], a.n)
                    T.matmul(bank[1][0:D, 0:CH], w_dn[a.stage][:, 0:D], hid[a.b2][:, 0, :], start=True, stop=True)
                    T.matmul(bank[1][D:128, 0:CH], w_dn[a.stage][:, 0:D], hid[a.b2][:, 1, :], start=True, stop=True)\
                     .then_inc(Cn["dn"], 1)

            node_slots(slot, pe, [(1, LAST // 2)], range(LAST // 2, MS))

            MT, XT, HT, OT, AT, UT = bank[0], bank[1], pair[0][:, 0, :], bank[2], bank[3], pair[0][:, 1, :]
            HT2 = pair[1][:, 0, :]
            MS_ = pair[1][:, 1, :]

            def tiles_to_cols(dst, src):
                for k in range(TC):
                    mm = turn(dst[:, k * R:(k + 1) * R], src[:, k * 128:(k + 1) * 128], R, 128)
                return mm

            def cols_to_tiles(dst, src):
                for k in range(TC):
                    mm = turn(dst[0:R, k * 128:(k + 1) * 128], src[:, k * R:(k + 1) * R], 128, R)
                return mm

            def down_rows(dst, h, w):
                for k in range(TC):
                    mm = T.matmul(dst[0:R, 128 * k:128 * k + 128], h[:, k * R:(k + 1) * R], w[:, :], start=True, stop=True)
                return mm

            pe.wait_ge(Cn["rows"], UNITS)
            pe.wait_ge(s_ones, N_ONES)

            def slot_a(k, q, h, front, back):
                p = q % 2
                if front:
                    at_least(pe, A_ld[q], h * 48 + 48)
                    at_least(pe, LA["xcol"], k)
                    tiles_to_cols(XT, l_a[q]).then_inc(LA["xdT"].sem, 1)
                    at_least(pe, LA["msg"], k + 1)
                    at_least(pe, LA["agg"], k)
                    tiles_to_cols(MT, m_r[p]).then_inc(LA["msgT"].sem, 1)
                if back:
                    kb, qb, hb, pb = before(k, q, h)
                    at_least(pe, LA["agg"], kb + 1)
                    at_least(pe, LA["t2"], kb)
                    cols_to_tiles(AT, agg[pb]).then_inc(LA["aggT"].sem, 1)
                if front:
                    at_least(pe, LA["xcol"], k + 1)
                    at_least(pe, LA["hid"], k)
                    T.matmul(HT[:, 0:CH], w_top[0][:, :], lxT[p][:, :], start=True, stop=True).then_inc(LA["up"].sem, 1)
                if back:
                    at_least(pe, LA["hid"], kb + 1)
                    at_least(pe, LA["t1"], kb)
                    down_rows(OT, lhid[pb], w_dn[0]).then_inc(LA["dn"].sem, 1)
            chunk_slots(slot_a, pe)
            at_least(pe, LA["rows"], NC)

            def slot_b(k, q, h, front, back):
                p = q % 2
                if front:
                    at_least(pe, LB["msg"], k + 1)
                    at_least(pe, LB["agg"], k)
                    tiles_to_cols(MT, m_r[p]).then_inc(LB["msgT"].sem, 1)
                    at_least(pe, LB["agg"], k + 1)
                    at_least(pe, LB["t2"], k)
                    cols_to_tiles(AT, agg[p]).then_inc(LB["aggT"].sem, 1)
                if back:
                    kb, qb, hb, pb = before(k, q, h)
                    at_least(pe, LB["u"], kb + 1)
                    at_least(pe, LB["ucol"], kb)
                    tiles_to_cols(UT, u_r[pb]).then_inc(LB["uT"].sem, 1)
                    at_least(pe, LB["ucol"], kb + 1)
                    T.matmul(HT[:, 0:CH], w_top[1][:, :], lxT[pb][:, :], start=True, stop=True).then_inc(LB["up"].sem, 1)
                    at_least(pe, LB["hid"], kb + 1)
                    at_least(pe, LB["rows"], kb)
                    down_rows(OT, lhid[pb], w_dn[1]).then_inc(LB["dn"].sem, 1)
            chunk_slots(slot_b, pe)
            at_least(pe, LB["rows"], NC)

            def slot_c(k, q, h, front, back):
                p = q % 2
                if front:
                    at_least(pe, LC["msg"], k + 1)
                    at_least(pe, LC["agg"], k)
                    tiles_to_cols(MT, m_r[p]).then_inc(LC["msgT"].sem, 1)
                    at_least(pe, LC["agg"], k + 1)
                    at_least(pe, LC["t2"], k)
                    cols_to_tiles(AT, agg[p]).then_inc(LC["aggT"].sem, 1)
            chunk_slots(slot_c, pe)
            at_least(pe, LC["rows"], NC)

            def slot_d(k, q, h, front, back):
                p = q % 2
                if front:
                    at_least(pe, LD["lky1"], k + 1)
                    at_least(pe, LD["lky2"], k + 1)
                    at_least(pe, LD["col"], k)
                    tiles_to_cols(MT, m_r[p]).then_inc(LD["lkyT"].sem, 1)
                if back:
                    kb, qb, hb, pb = before(k, q, h)
                    at_least(pe, LD["col"], kb + 1)
                    at_least(pe, LD["zc"], kb)
                    T.matmul(HT[0:128, 0:CH], gat_w[:, :], lxT[pb][:, :], start=True, stop=True).then_inc(LD["zx"].sem, 1)
            chunk_slots(slot_d, pe)
            summaries(1, LD["c"], D_SUM1, LD["ct"])
            pe.wait_ge(LD["c"], D_CARRY1)
            turn(bank[3][0:NC, 128:129], carry_r[0:1, 1:NC + 1], 1, NC).then_inc(LD["ct"], 1)
            summaries(1, LD["c"], D_SUM2, LD["ct"])
            pe.wait_ge(LD["c"], D_CARRY2)
            turn(bank[3][0:NC, 128:129], carry_r[0:1, 0:NC], 1, NC).then_inc(LD["ct"], 1)
            pe.wait_ge(LD["c"], D_ROWS)

            def slot_g(k, q, h, front, back):
                p = q % 2
                if front:
                    at_least(pe, LE["agg"], k + 1)
                    at_least(pe, LE["t1"], k)
                    cols_to_tiles(AT, agg[p]).then_inc(LE["aggT"].sem, 1)
            chunk_slots(slot_g, pe)
            at_least(pe, LE["rows"], NC)

            def slot_f(k, q, h, front, back):
                p = q % 2
                if front:
                    at_least(pe, LF["msg"], k + 1)
                    at_least(pe, LF["fill"], k)
                    tiles_to_cols(MT, m_r[p]).then_inc(LF["msgT"].sem, 1)
            chunk_slots(slot_f, pe)
            at_least(pe, LF["fill"], NC)

            def slot_m(k, q, h, front, back):
                p = q % 2
                if front:
                    at_least(pe, M_ga[q], h * 64 + 64)
                    at_least(pe, LG["scol"], k)
                    tiles_to_cols(MT, g_row[q]).then_inc(LG["srcT"].sem, 1)
                if back:
                    kb, qb, hb, pb = before(k, q, h)
                    at_least(pe, LG["agg"], kb + 1)
                    at_least(pe, LG["hid2"], kb)
                    T.matmul(HT2[:, 0:CH], w_upd[:, :], l_up[qb][:, :], start=True, stop=True).then_inc(LG["up2"].sem, 1)
                if front:
                    at_least(pe, M_ld[q], h * 80 + 80)
                    at_least(pe, LG["scol"], k + 1)
                    at_least(pe, LG["hid"], k)
                    T.matmul(HT[:, 0:CH], w_msg[:, :], l_in[q][:, :], start=True, stop=False)
                    T.matmul(HT[:, 0:CH], w_edge[:, :], l_ea[q][:, :], start=False, stop=True).then_inc(LG["up"].sem, 1)
                if back:
                    at_least(pe, LG["hid2"], kb + 1)
                    at_least(pe, LG["t1"], kb)
                    down_rows(OT, lhid2[pb], w_dn[2]).then_inc(LG["dn2"].sem, 1)
                if front:
                    at_least(pe, LG["hid"], k + 1)
                    at_least(pe, LG["msg"], k)
                    T.matmul(XT[0:D, 0:CH], w_msg2[:, :], lhid[p][:, :], start=True, stop=True).then_inc(LG["dn"].sem, 1)
            chunk_slots(slot_m, pe)

        @block.scalar
        def _(act):
            A = nc.scalar
            act.wait_ge(s_set, N_SET)
            act.wait_ge(s_c, C_DD)
            A.activation(s3_c[:, :, :], s2_c[:, :, :], ACT.Sqrt).then_inc(s_ca, 1)
            act.wait_ge(s_w, ALL_W)
            act.wait_ge(s_prep, PREP_ALL)

            def root(dst, src):
                return A.activation(dst, src, ACT.Sqrt, bias=eps[0:R, :], scale=1.0 / D)

            def slot(m, u):
                a = unit(m, u - 3)
                if a.real:
                    at_least(act, Cn["rstd"], a.n - 1)
                    act.wait_ge(Cn["ssum"], a.n + 1)
                    root(sd[a.b2][:, :], ss[a.b2][:, :]).then_inc(Cn["std"], 1)
                a = unit(m, u + 1)
                if a.real:
                    act.wait_ge(Cn["rowsT"], a.n + 1)
                    at_least(act, Cn["res"], a.n - 2)
                    A.activation(xT[a.b3][:, :], bank[0][:, 0:CH], ACT.Copy).then_inc(Cn["xT"], 1)
                a = unit(m, u - 5)
                if a.real and a.stage == 1:
                    act.wait_ge(Cn["ssum2"], a.i + 1)
                    at_least(act, Cn["rstd2"], a.i)
                    root(sd_b[:, :], ss_b[:, :]).then_inc(Cn["std2"], 1)
                a = unit(m, u - 2)
                if a.real:
                    at_least(act, Cn["ssum"], a.n - 1)
                    if a.stage == 0:
                        act.wait_ge(Cn["centred"], a.i + 1)
                        A.activation(sq[a.b2][:, :], rc[:, :], ACT.Square).then_inc(Cn["sq"], 1)
                    else:
                        act.wait_ge(Cn["resT"], a.n + 1)
                        A.activation(sq[a.b2][:, :], bank[2 + a.b2][0:R, :], ACT.Square).then_inc(Cn["sq"], 1)
                a = unit(m, u)
                if a.real:
                    act.wait_ge(Cn["up"], a.n + 1)
                    at_least(act, Cn["dn"], a.n - 1)
                    A.activation(hid[a.b2][:, :, :], pair[a.b2][:, :, 0:CH], ACT.Relu,
                                 bias=b_up[:, a.stage:a.stage + 1]).then_inc(Cn["hid"], 1)
                a = unit(m, u - 3)
                if a.real and a.stage == 1:
                    act.wait_ge(Cn["y"], a.i + 1)
                    at_least(act, Cn["ssum2"], a.i)
                    A.activation(sq_b[:, :], y_r[:, :], ACT.Square).then_inc(Cn["sq2"], 1)

            node_slots(slot, act, [(1, MS - 1)], [MS - 1])

            MT, XT, HT, OT, AT, UT = bank[0], bank[1], pair[0][:, 0, :], bank[2], bank[3], pair[0][:, 1, :]
            HT2 = pair[1][:, 0, :]

            def norm(S, kb):
                at_least(act, S["cen"] if S is LA else S["t5"] if S is LC else S["t3"] if S is LE else S["t2"], kb + 1)
                at_least(act, S["ssum"], kb)
                A.activation(lsq[:, :], w_r[:, :] if S is not LA else v_r[:, :], ACT.Square).then_inc(S["sq"].sem, 1)
                at_least(act, S["ssum"], kb + 1)
                at_least(act, S["rstd"], kb)
                root(lsd[:, :], lss[:, :]).then_inc(S["std"].sem, 1)

            def slot_a(k, q, h, front, back):
                p = q % 2
                if front:
                    at_least(act, LA["xdT"], k + 1)
                    at_least(act, LA["up"], k - 1)
                    A.activation(lxT[p][0:D, :], XT[0:D, 0:CH], ACT.Copy).then_inc(LA["xcol"].sem, 1)
                    at_least(act, LA["up"], k + 1)
                    at_least(act, LA["dn"], k - 1)
                    A.activation(lhid[p][:, :], HT[:, 0:CH], ACT.Relu, bias=b_up[:, 0:1]).then_inc(LA["hid"].sem, 1)
                if back:
                    norm(LA, before(k, q, h)[0])
            act.wait_ge(s_ones, N_ONES)
            chunk_slots(slot_a, act)

            def slot_b(k, q, h, front, back):
                if back:
                    kb, qb, hb, pb = before(k, q, h)
                    at_least(act, LB["uT"], kb + 1)
                    at_least(act, LB["up"], kb - 1)
                    A.activation(lxT[pb][0:D, :], UT[0:D, 0:CH], ACT.Copy).then_inc(LB["ucol"].sem, 1)
                    at_least(act, LB["up"], kb + 1)
                    at_least(act, LB["dn"], kb - 1)
                    A.activation(lhid[pb][:, :], HT[:, 0:CH], ACT.Relu, bias=b_up[:, 1:2]).then_inc(LB["hid"].sem, 1)
                    at_least(act, LB["dn"], kb + 1)
                    at_least(act, B_st[qb], hb * 16)
                    A.activation(n_r[qb][:, :].rearrange("p (k f) -> p k f", f=D),
                                 OT[0:R, :].rearrange("p (k f) -> p k f", f=128)[:, :, 0:D], ACT.Copy)\
                     .then_inc(LB["rows"].sem, 1)
            at_least(act, LA["rows"], NC)
            all_stored(act, A_st)
            chunk_slots(slot_b, act)

            def slot_c(k, q, h, front, back):
                if back:
                    norm(LC, before(k, q, h)[0])
            chunk_slots(slot_c, act)

            def slot_d(k, q, h, front, back):
                p = q % 2
                if front:
                    at_least(act, LD["lkyT"], k + 1)
                    at_least(act, LD["zx"], k - 1)
                    A.activation(lxT[p][:, :], MT[:, 0:CH], ACT.Copy).then_inc(LD["col"].sem, 1)
                if back:
                    kb, qb, hb, pb = before(k, q, h)
                    at_least(act, LD["zx"], kb + 1)
                    if isinstance(kb, int):
                        at_least(act, D_st[pb], 16 * (kb // 2))
                    else:
                        at_least(act, D_st[pb], hb * 32 + (qb // 2) * 16)
                    A.activation(zx[pb][:, :], HT[0:D + 2, 0:CH], ACT.Copy).then_inc(LD["zc"].sem, 1)
            at_least(act, LC["rows"], NC)
            chunk_slots(slot_d, act)
            act.wait_ge(LD["c"], D_EXP)
            A.activation(s2_c[:, :, :], s3_c[:, :, :], ACT.Exp).then_inc(LD["ca"], 1)

            def slot_g(k, q, h, front, back):
                if back:
                    norm(LE, before(k, q, h)[0])
            chunk_slots(slot_g, act)

            def slot_m(k, q, h, front, back):
                p = q % 2
                if front:
                    at_least(act, LG["srcT"], k + 1)
                    at_least(act, LG["up"], k - 3)
                    A.activation(l_in[q][0:D, :], MT[0:D, 0:CH], ACT.Copy).then_inc(LG["scol"].sem, 1)
                if back:
                    kb, qb, hb, pb = before(k, q, h)
                    at_least(act, LG["up2"], kb + 1)
                    at_least(act, LG["dn2"], kb - 1)
                    A.activation(lhid2[pb][:, :], HT2[:, 0:CH], ACT.Relu, bias=b_up[:, 2:3]).then_inc(LG["hid2"].sem, 1)
                if front:
                    at_least(act, LG["up"], k + 1)
                    at_least(act, LG["dn"], k - 1)
                    A.activation(lhid[p][:, :], HT[:, 0:CH], ACT.Relu, bias=b_msg[:, :]).then_inc(LG["hid"].sem, 1)
                    at_least(act, LG["dn"], k + 1)
                    at_least(act, LG["agg"], k - 3)
                    A.activation(l_m[q][0:D, :], XT[0:D, 0:CH], ACT.Identity, bias=b_msg2[:, :]).then_inc(LG["msg"].sem, 1)
                if back:
                    norm(LG, kb)
            at_least(act, LE["rows"], NC)
            at_least(act, LF["fill"], NC)
            chunk_slots(slot_m, act)

        @block.vector
        def _(dve):
            V = nc.vector
            c = [0, 0]

            def step(ins):
                c[0] += 1
                ins.then_inc(s_c, 1)
                dve.wait_ge(s_c, c[0])

            def prep(ins):
                c[1] += 1
                ins.then_inc(s_prep, 1)
                dve.wait_ge(s_prep, c[1])

            V.memset(dst_c[:, :], -1).then_inc(s_pad, 1)
            zeroed = [w_top[s] for s in range(3)] + [w_bot[s] for s in range(3)] + [w_dn[s] for s in range(3)] \
                + [gat_w, w_edge]
            for w in zeroed:
                V.memset(w[:, :], 0.0).then_inc(s_set, 1)
            V.memset(eps[:, :], EPS).then_inc(s_set, 1)
            V.memset(info_fill, 1.0).then_inc(s_ones, 1)
            dve.wait_ge(s_ones, 1)
            V.memset(info_fill.rearrange("p (a c) -> p a c", c=4)[:, :, 0:1], -1.0).then_inc(s_set, 1)

            dve.wait_ge(s_e, ALL_E)
            V.memset(one_c[:, :], 1.0).then_inc(s_c, 1)
            c[0] += 1
            step(V.tensor_copy(dstf_c[:, :], dst_c[:, :]))
            V.tensor_tensor(keep_c[:, :], dstf_c[:, 0:CH], dstf_c[:, 1:CH + 1], ALU.is_equal).then_inc(s_c, 1)
            V.tensor_tensor(on_c[:, :], dstf_c[:, 1:CH + 1], dstf_c[:, 2:CH + 2], ALU.is_equal).then_inc(s_c, 1)
            c[0] += 2
            dve.wait_ge(s_c, c[0])
            assert c[0] == C_ROWS
            step(V.tensor_scalar(last_c[:, :], on_c[:, :], -1.0, 1.0, ALU.mult, ALU.add))
            V.tensor_tensor_scan(s1_c[:, 0, :], keep_c[:, :], one_c[:, :], 0.0, ALU.mult, ALU.add).then_inc(s_c, 1)
            V.tensor_tensor_scan(s1_c[:, 1, :], keep_c[:, :], ew_c[:, :], 0.0, ALU.mult, ALU.add).then_inc(s_c, 1)
            V.tensor_reduce(edge_c[:, 0:1], keep_c[:, :], AX_X, ALU.min).then_inc(s_c, 1)
            V.tensor_reduce(edge_c[:, 1:2], keep_c[:, :], AX_X, ALU.min).then_inc(s_c, 1)
            c[0] += 4
            dve.wait_ge(s_c, c[0])
            step(V.tensor_copy(edge_c[:, 2:4], s1_c[:, :, CH - 1]))
            assert c[0] == C_SUM
            dve.wait_ge(s_ct, 1)
            step(V.tensor_copy(top[:, :, 0:NC], bank[3][0:2, 0:128].rearrange("p (a b) -> p a b", a=2)[:, :, 0:NC]))
            step(V.memset(carry_r[:, :], 0.0))
            step(V.tensor_tensor_scan(carry_r[0:2, 1:NC + 1], top[:, 0, 0:NC], top[:, 1, 0:NC], 0.0, ALU.mult, ALU.add))
            assert c[0] == C_CARRY
            dve.wait_ge(s_ct, 2)
            step(V.tensor_copy(carry_c[:, :], bank[3][0:NC, 128:130]))
            V.tensor_tensor_scan(s1_c[:, 0, :], keep_c[:, :], one_c[:, :], carry_c[:, 0:1], ALU.mult, ALU.add).then_inc(s_c, 1)
            V.tensor_tensor_scan(s1_c[:, 1, :], keep_c[:, :], ew_c[:, :], carry_c[:, 1:2], ALU.mult, ALU.add).then_inc(s_c, 1)
            c[0] += 2
            dve.wait_ge(s_c, c[0])
            step(V.tensor_scalar(s1_c[:, :, :], s1_c[:, :, :], 1.0, None, ALU.add))
            step(V.tensor_scalar(s2_c[:, :, :], s1_c[:, :, :], 1e-30, None, ALU.max))
            assert c[0] == C_DD
            dve.wait_ge(s_ca, 1)
            step(V.reciprocal(s3_c[:, :, :], s3_c[:, :, :]))
            step(V.tensor_scalar(s1_c[:, :, :], s1_c[:, :, :], 0.0, None, ALU.is_gt))
            step(V.tensor_tensor(s3_c[:, :, :], s3_c[:, :, :], s1_c[:, :, :], ALU.mult))
            step(V.tensor_scalar(s2_c[:, 0, :], on_c[:, :], FAR, None, ALU.mult))
            step(V.tensor_tensor(s2_c[:, 0, :], s2_c[:, 0, :], dstf_c[:, 1:CH + 1], ALU.add))
            assert c[0] == C_DINV

            def tiled(a):
                return bank[a][0:R, 0:NT].rearrange("p (k c) -> p c k", k=TC)

            def in_tiles(ap):
                return ap.rearrange("p (c k) -> p c k", k=TC)

            dve.wait_ge(s_ct, 6)
            dve.wait_ge(s_pool0, 4)
            V.tensor_copy(in_tiles(d0_t[:, :]), tiled(0)).then_inc(s_c, 1)
            V.tensor_copy(in_tiles(d1_t[:, :]), tiled(1)).then_inc(s_c, 1)
            V.tensor_copy(in_tiles(last_t[:, :]), tiled(2)).then_inc(s_c, 1)
            V.tensor_copy(in_tiles(sidx[:, :]), tiled(3)).then_inc(s_c, 1)
            V.tensor_copy(info_r[:, :, 0], slot_id[:, :]).then_inc(s_c, 1)
            V.memset(info_r[:, :, 3], 0.0).then_inc(s_c, 1)
            c[0] += 6
            dve.wait_ge(s_c, c[0])
            V.tensor_copy(info_r[:, :, 1], d0_t[:, :]).then_inc(s_c, 1)
            V.tensor_copy(info_r[:, :, 2], d1_t[:, :]).then_inc(s_c, 1)
            c[0] += 2
            assert c[0] == C_INFO

            dve.wait_ge(s_w, ALL_W)

            def centre(view, n, width, m):
                prep(V.tensor_reduce(m, view, AX_X, ALU.add))
                prep(V.tensor_scalar(m, m, -1.0 / width, None, ALU.mult))
                prep(V.tensor_tensor(view, view, m.unsqueeze(2).to_broadcast([128, n, width]), ALU.add))

            centre(b_row[:, 1:4, :], 3, D, mean6[:, 0:3])
            for s in (1, 2):
                centre(w_dn[s][:, 0:D].unsqueeze(1), 1, D, mean6[:, 2 + s:3 + s])
            prep(V.tensor_tensor(gat_tmp[:, :], gat_raw[:, :], gat_att[:, :], ALU.mult))
            prep(V.tensor_reduce(gat_w[0:D, D:D + 1], gat_tmp[0:D, :], AX_X, ALU.add))
            prep(V.tensor_reduce(gat_w[D:128, D + 1:D + 2], gat_tmp[D:128, :], AX_X, ALU.add))
            centre(gat_raw[:, :].unsqueeze(1), 1, D, mean6[:, 5:6])
            prep(V.tensor_copy(gat_w[0:D, 0:D], gat_raw[0:D, :]))
            for s, i in enumerate((0, 1, 3)):
                prep(V.tensor_copy(b_two[:, s, 0:D], b_row[:, i, :]))
                prep(V.tensor_copy(b_two[:, s, D:128], b_row[:, i, :]))
            assert c[1] == PREP_TWO
            dve.wait_ge(s_bt, 3)
            for s in range(3):
                prep(V.tensor_copy(b_dn[:, s:s + 1], bank[s][:, 0:1]))
            for i in (0, 1):
                V.memset(x1_r[i][:, :], 0.0).then_inc(s_prep, 1)
                V.memset(x3_r[i][:, :], 0.0).then_inc(s_prep, 1)
                c[1] += 2
            assert c[1] == PREP_ALL

            iso_sem0, iso_sem1 = [Cn["s0st0"], Cn["s0st1"]], [Cn["s1st0"], Cn["s1st1"]]

            def pR(a):
                return bank[2 + a.b2][0:R, :]

            def slot_of(mode):
                def slot(m, u):
                    known = mode is None

                    def iso0(i):
                        return NB <= i < LAST if known else mode == "iso"

                    def iso1(i):
                        return NB + 2 <= i < LAST + 2 if known else mode == "iso"

                    def half_after(i, q, first):
                        return (i - 2 - first) // 2 + 1 if known else m + (q - (first + 2 - first % 2) // 2 + 1 - 0)

                    a = unit(m, u - 3)
                    if a.real:
                        qq = (u - 3) // 3 // 2
                        at_m = m + qq
                        dve.wait_ge(Cn["std"], a.n + 1)
                        V.reciprocal(rs[:, :], sd[a.b2][:, :]).then_inc(Cn["rstd"], 1)
                        dve.wait_ge(Cn["rstd"], a.n + 1)
                        dst = {0: x1_r, 1: x2_r, 2: x4_r}[a.stage][a.par]
                        if a.stage == 0:
                            if not known or a.i >= 2:
                                dve.wait_ge(Cn["rowsT"], a.n)
                            if (known and NB <= a.i - 2 < LAST) or mode == "iso":
                                v = 32 * ((a.i - 2 - NB) // 2 + 1) if known else (at_m - NB // 2) * 32
                                dve.wait_ge(iso_sem0[a.par], v)
                        if a.stage == 1:
                            if (known and NB + 2 <= a.i - 2 < LAST + 2) or mode == "iso":
                                v = 48 * ((a.i - 2 - NB - 2) // 2 + 1) if known else (at_m - NB // 2 - 1) * 48
                                dve.wait_ge(iso_sem1[a.par], v)
                        if a.stage == 2:
                            if (known and 4 <= a.i - 2 < NB + 4) or mode == "dense":
                                v = 16 * ((a.i - 6) // 2 + 1) if known else (at_m - 2) * 16
                                dve.wait_ge([Cn["out0"], Cn["out1"]][a.par], v)
                        val = rc[:, :] if a.stage == 0 else pR(a)
                        V.tensor_tensor(n_view(dst[:, :]), n_view(val), spread(rs[:, :], TB), ALU.mult)\
                         .then_inc(Cn["rows"], 1)
                        if a.stage == 1:
                            dve.wait_ge(Cn["rows"], a.n + 1)
                            at_least(dve, Cn["rows2"], a.i)
                            V.tensor_tensor(n_view(y_r[:, :]), n_view(x2_r[a.par][:, :]), row_bias(2, TB), ALU.add)\
                             .then_inc(Cn["y"], 1)
                    a = unit(m, u - 2)
                    if a.real and a.stage == 0:
                        dve.wait_ge(Cn["resT"], a.n + 1)
                        V.tensor_reduce(mn[:, :], n_view(pR(a)), AX_X, ALU.add).then_inc(Cn["mean_sum"], 1)
                        dve.wait_ge(Cn["mean_sum"], a.i + 1)
                        V.tensor_scalar(mn[:, :], mn[:, :], -1.0 / D, None, ALU.mult).then_inc(Cn["mean"], 1)
                        dve.wait_ge(Cn["mean"], a.i + 1)
                        V.tensor_tensor(n_view(rc[:, :]), n_view(pR(a)), spread(mn[:, :], TB), ALU.add)\
                         .then_inc(Cn["centred"], 1)
                    at_m = m + (u - 2) // 3 // 2
                    if a.real and a.stage == 0 and iso0(a.i):
                        if not known or a.i - 2 >= NB:
                            v = 32 * ((a.i - 2 - NB) // 2 + 1) if known else (at_m - NB // 2) * 32
                            dve.wait_ge(iso_sem0[a.par], v)
                        V.tensor_tensor(h0_r[a.par][:, :], pR(a), x_in[a.par][:, :], ALU.subtract).then_inc(Cn["h0"], 1)
                        dve.wait_ge(Cn["h0"], a.i - NB + 1)
                        V.tensor_tensor(n_view(h0_r[a.par][:, :]), n_view(h0_r[a.par][:, :]), row_bias(0, TB),
                                        ALU.subtract).then_inc(Cn["h0b"], 1)
                    a = unit(m, u - 4)
                    if a.real and a.stage == 1:
                        dve.wait_ge(Cn["sq2"], a.i + 1)
                        at_least(dve, Cn["std2"], a.i)
                        V.tensor_reduce(ss_b[:, :], n_view(sq_b[:, :]), AX_X, ALU.add).then_inc(Cn["ssum2"], 1)
                    a = unit(m, u - 2)
                    if a.real:
                        dve.wait_ge(Cn["sq"], a.n + 1)
                        at_least(dve, Cn["std"], a.n - 1)
                        V.tensor_reduce(ss[a.b2][:, :], n_view(sq[a.b2][:, :]), AX_X, ALU.add).then_inc(Cn["ssum"], 1)
                    at_m = m + (u - 2) // 3 // 2
                    if a.real and a.stage == 1 and iso1(a.i):
                        if not known or a.i - 2 >= NB + 2:
                            v = 48 * ((a.i - 2 - NB - 2) // 2 + 1) if known else (at_m - NB // 2 - 1) * 48
                            dve.wait_ge(iso_sem1[a.par], v)
                        V.tensor_tensor(h2_r[a.par][:, :], pR(a), x1_r[a.par][:, :], ALU.subtract).then_inc(Cn["h2"], 1)
                        dve.wait_ge(Cn["h2"], a.i - NB - 1)
                        V.tensor_tensor(n_view(h2_r[a.par][:, :]), n_view(h2_r[a.par][:, :]), row_bias(1, TB),
                                        ALU.subtract).then_inc(Cn["h2b"], 1)
                    a = unit(m, u - 5)
                    if a.real and a.stage == 1:
                        dve.wait_ge(Cn["std2"], a.i + 1)
                        V.reciprocal(rs_b[:, :], sd_b[:, :]).then_inc(Cn["rstd2"], 1)
                        dve.wait_ge(Cn["rstd2"], a.i + 1)
                        if not known or a.i >= 2:
                            dve.wait_ge(Cn["rowsT"], a.n + 3)
                        at_m = m + (u - 5) // 3 // 2
                        if (known and NB + 2 <= a.i - 2 < LAST + 2) or mode == "iso":
                            v = 48 * ((a.i - 2 - NB - 2) // 2 + 1) if known else (at_m - NB // 2 - 1) * 48
                            dve.wait_ge(iso_sem1[a.par], v)
                        V.tensor_tensor(n_view(x3_r[a.par][:, :]), n_view(y_r[:, :]), spread(rs_b[:, :], TB), ALU.mult)\
                         .then_inc(Cn["rows2"], 1)
                    a = unit(m, u - 1)
                    if a.real:
                        dve.wait_ge(Cn["dn"], a.n + 1)
                        at_least(dve, Cn["resT"], a.n - 1)
                        V.scalar_tensor_tensor(rT[a.b2][:, :], bank[1][:, 0:CH], b_dn[:, a.stage:a.stage + 1],
                                               xT[a.b3][:, :], ALU.add, ALU.add).then_inc(Cn["res"], 1)
                return slot

            def run(mode, lo, hi):
                s = slot_of(mode)
                with dve.Fori(lo, hi, 1) as m:
                    for u in range(6):
                        s(m, u)

            known = slot_of(None)
            known(0, -1)
            for m in range(0, 4):
                for u in range(6):
                    known(m, u)
            run("dense", 4, NB // 2)
            for m in range(NB // 2, NB // 2 + 4):
                for u in range(6):
                    known(m, u)
            run("iso", NB // 2 + 4, LAST // 2)
            for m in range(LAST // 2, MS):
                for u in range(6):
                    known(m, u)
            for u in range(5):
                known(MS, u)

            dve.wait_ge(P["copied"], 5 * NI)
            step(V.tensor_scalar(gfl[:, :], info_r[:, :, 0], 0.0, None, ALU.is_ge))
            step(V.tensor_tensor(w0_t[:, :], info_r[:, :, 0], gbase[:, :], ALU.subtract))
            step(V.tensor_tensor(w0_t[:, :], w0_t[:, :], gfl[:, :], ALU.mult))
            step(V.tensor_tensor(gidx[:, :], w0_t[:, :], gbase[:, :], ALU.add))
            step(V.tensor_copy(w0_t[:, :], info_r[:, :, 1]))
            step(V.tensor_tensor(w1_t[:, :], info_r[:, :, 2], ew_t[:, :], ALU.mult))
            assert c[0] == C_ALL
            for i in range(2):
                V.memset(lxT[i][:, :], 0.0).then_inc(s_ones, 1)
            for r in range(2):
                dve.wait_ge(iso_sem0[r], 32 * len(range(r, NI, 2)))
                dve.wait_ge(iso_sem1[r], 48 * len(range(r, NI, 2)))
            for buf in l_ea + l_a + g_row + m_r + u_r + agg:
                V.memset(buf[:, :], 0.0).then_inc(s_ones, 1)

            dve.wait_ge(s_ones, N_ONES)

            def v4(ap):
                return ap.rearrange("p (k f) -> p k f", f=D)

            def tile_scalar(tt, k):
                return tt[:, bass.ds(k * TC, TC)].unsqueeze(2).to_broadcast([R, TC, D])

            def finish(S, kb, qb, hb, val, st):
                at_least(dve, S["sq"], kb + 1)
                V.tensor_reduce(lss[:, :], v4(lsq[:, :]), AX_X, ALU.add).then_inc(S["ssum"].sem, 1)
                at_least(dve, S["std"], kb + 1)
                V.reciprocal(lrs[:, :], lsd[:, :]).then_inc(S["rstd"].sem, 1)
                at_least(dve, S["rstd"], kb + 1)
                if st is not None:
                    at_least(dve, st[qb], hb * 16)
                V.tensor_tensor(v4(n_r[qb][:, :]), v4(val), spread(lrs[:, :], TC), ALU.mult).then_inc(S["rows"].sem, 1)

            def scan(S, k, q, data, width, name_done, first, msg_sem):
                at_least(dve, msg_sem, k + 1)
                init = 0.0 if first else agg[(q - 1) % 2][0:width, CH - 1:CH]
                V.tensor_tensor_scan(agg[q % 2][0:width, :], l_k[q][0:width, :], data, init,
                                     ALU.mult, ALU.add).then_inc(name_done.sem, 1)

            MT, XT, OT, AT = bank[0], bank[1], bank[2], bank[3]
            OTv = OT[0:R, :].rearrange("p (k f) -> p k f", f=128)[:, :, 0:D]
            ATv = AT[0:R, :].rearrange("p (k f) -> p k f", f=128)[:, :, 0:D]

            def slot_a(k, q, h, front, back):
                p = q % 2
                if front:
                    at_least(dve, A_ld[q], h * 48 + 48)
                    at_least(dve, LA["msgT"], k - 1)
                    V.tensor_tensor(half(m_r[p]), v4(l_src[q][:, :]), tile_scalar(w0_t, k), ALU.mult)\
                     .then_inc(LA["msg"].sem, 1)
                if back:
                    kb, qb, hb, pb = before(k, q, h)
                    at_least(dve, LA["dn"], kb + 1)
                    at_least(dve, LA["rows"], kb)
                    V.tensor_tensor(v4(v_r[:, :]), OTv, tile_scalar(d0_t, kb), ALU.mult).then_inc(LA["t1"].sem, 1)
                    at_least(dve, LA["t1"], kb + 1)
                    at_least(dve, LA["aggT"], kb + 1)
                    V.tensor_tensor(v4(w_r[:, :]), v4(v_r[:, :]), ATv, ALU.add).then_inc(LA["t2"].sem, 1)
                    at_least(dve, LA["t2"], kb + 1)
                    V.tensor_tensor(v4(v_r[:, :]), v4(w_r[:, :]), tile_scalar(d0_t, kb), ALU.mult).then_inc(LA["t3"].sem, 1)
                    at_least(dve, LA["t3"], kb + 1)
                    V.tensor_tensor(v4(w_r[:, :]), v4(v_r[:, :]), half(l_a[qb]), ALU.add).then_inc(LA["t4"].sem, 1)
                    at_least(dve, LA["t4"], kb + 1)
                    V.tensor_tensor(v4(w_r[:, :]), v4(w_r[:, :]), row_bias(0, TC), ALU.add).then_inc(LA["t5"].sem, 1)
                    at_least(dve, LA["t5"], kb + 1)
                    V.tensor_reduce(lmn[:, :], v4(w_r[:, :]), AX_X, ALU.add).then_inc(LA["msum"].sem, 1)
                    at_least(dve, LA["msum"], kb + 1)
                    V.tensor_scalar(lmn[:, :], lmn[:, :], -1.0 / D, None, ALU.mult).then_inc(LA["mean"].sem, 1)
                    at_least(dve, LA["mean"], kb + 1)
                    V.tensor_tensor(v4(v_r[:, :]), v4(w_r[:, :]), spread(lmn[:, :], TC), ALU.add).then_inc(LA["cen"].sem, 1)
                if front:
                    at_least(dve, LA["aggT"], k - 1)
                    scan(LA, k, q, MT[0:D, 0:CH], D, LA["agg"], isinstance(k, int) and k == 0, LA["msgT"])
                if back:
                    finish(LA, kb, qb, hb, v_r[:, :], A_st)
            chunk_slots(slot_a, dve)

            def slot_b(k, q, h, front, back):
                p = q % 2
                if front:
                    at_least(dve, B_ga[q], h * 64 + 64)
                    at_least(dve, LB["msgT"], k - 1)
                    V.tensor_tensor(half(m_r[p]), half(g_row[q]), tile_scalar(w1_t, k), ALU.mult)\
                     .then_inc(LB["msg"].sem, 1)
                    at_least(dve, B_ld[q], h * 32 + 32)
                    at_least(dve, LB["aggT"], k - 1)
                    scan(LB, k, q, MT[0:D, 0:CH], D, LB["agg"], isinstance(k, int) and k == 0, LB["msgT"])
                    at_least(dve, LB["u"], k)
                    V.tensor_tensor(v4(v_r[:, :]), half(l_a[q]), tile_scalar(d1_t, k), ALU.mult).then_inc(LB["t1"].sem, 1)
                    at_least(dve, LB["t1"], k + 1)
                    at_least(dve, LB["aggT"], k + 1)
                    V.tensor_tensor(v4(w_r[:, :]), v4(v_r[:, :]), ATv, ALU.add).then_inc(LB["t2"].sem, 1)
                    at_least(dve, LB["t2"], k + 1)
                    at_least(dve, LB["uT"], k - 1)
                    V.tensor_tensor(half(u_r[p]), v4(w_r[:, :]), tile_scalar(d1_t, k), ALU.mult).then_inc(LB["u"].sem, 1)
            at_least(dve, LA["rows"], NC)
            chunk_slots(slot_b, dve)
            at_least(dve, LB["rows"], NC)
            all_stored(dve, B_st)

            def slot_c(k, q, h, front, back):
                p = q % 2
                if front:
                    at_least(dve, C_ga[q], h * 64 + 64)
                    at_least(dve, LC["msgT"], k - 1)
                    V.tensor_tensor(half(m_r[p]), half(g_row[q]), tile_scalar(w1_t, k), ALU.mult)\
                     .then_inc(LC["msg"].sem, 1)
                    at_least(dve, C_ld[q], h * 48 + 48)
                if back:
                    kb, qb, hb, pb = before(k, q, h)
                    V.tensor_tensor(v4(v_r[:, :]), half(l_a[qb]), tile_scalar(d1_t, kb), ALU.mult).then_inc(LC["t1"].sem, 1)
                    at_least(dve, LC["t1"], kb + 1)
                    at_least(dve, LC["aggT"], kb + 1)
                    at_least(dve, LC["rows"], kb)
                    V.tensor_tensor(v4(w_r[:, :]), v4(v_r[:, :]), ATv, ALU.add).then_inc(LC["t2"].sem, 1)
                    at_least(dve, LC["t2"], kb + 1)
                    V.tensor_tensor(v4(v_r[:, :]), v4(w_r[:, :]), tile_scalar(d1_t, kb), ALU.mult).then_inc(LC["t3"].sem, 1)
                    at_least(dve, LC["t3"], kb + 1)
                    V.tensor_tensor(w_r[:, :], v_r[:, :], l_b[qb][:, :], ALU.add).then_inc(LC["t4"].sem, 1)
                    at_least(dve, LC["t4"], kb + 1)
                    V.tensor_tensor(v4(w_r[:, :]), v4(w_r[:, :]), row_bias(1, TC), ALU.add).then_inc(LC["t5"].sem, 1)
                if front:
                    at_least(dve, LC["aggT"], k - 1)
                    scan(LC, k, q, MT[0:D, 0:CH], D, LC["agg"], isinstance(k, int) and k == 0, LC["msgT"])
                if back:
                    finish(LC, kb, qb, hb, w_r[:, :], C_st)
            chunk_slots(slot_c, dve)
            at_least(dve, LC["rows"], NC)

            def slot_d(k, q, h, front, back):
                p = q % 2
                if front:
                    mv = m_r[p][:, :].rearrange("p (k f) -> p k f", f=128)
                    at_least(dve, D_ga[q], h * 64 + 64)
                    at_least(dve, LD["lkyT"], k - 1)
                    V.scalar_tensor_tensor(mv[:, :, 0:D], half(g_row[q]), 0.2, half(g_row[q]),
                                           ALU.mult, ALU.max).then_inc(LD["lky1"].sem, 1)
                    at_least(dve, D_ld[q], h * 16 + 16)
                    V.scalar_tensor_tensor(mv[:, :, D:128], half(l_a[q]), 0.2, half(l_a[q]),
                                           ALU.mult, ALU.max).then_inc(LD["lky2"].sem, 1)
            chunk_slots(slot_d, dve)

            dc = [0]

            def dstep(ins):
                dc[0] += 1
                ins.then_inc(LD["c"], 1)
                dve.wait_ge(LD["c"], dc[0])

            dve.wait_ge(s_rows, 64)
            el, er, s3a, s3b = s1_c[:, 0, :], s1_c[:, 1, :], s3_c[:, 0, :], s3_c[:, 1, :]
            dstep(V.tensor_tensor(er, er, last_c[:, :], ALU.mult))
            dstep(V.tensor_tensor_scan(s3a[:, ::-1], on_c[:, ::-1], er[:, ::-1], 0.0, ALU.mult, ALU.add))
            dstep(V.tensor_reduce(edge_c[:, 0:1], on_c[:, :], AX_X, ALU.min))
            dstep(V.tensor_copy(edge_c[:, 2:3], s3a[:, 0:1]))
            assert dc[0] == D_SUM1
            dve.wait_ge(LD["ct"], 1)
            dstep(V.tensor_copy(top[0:1, :, 0:NC], bank[3][0:1, 0:128].rearrange("p (a b) -> p a b", a=2)[:, :, 0:NC]))
            dstep(V.memset(carry_r[:, :], 0.0))
            dstep(V.tensor_tensor_scan(carry_r[0:1, 0:NC][:, ::-1], top[0:1, 0, 0:NC][:, ::-1],
                                       top[0:1, 1, 0:NC][:, ::-1], 0.0, ALU.mult, ALU.add))
            assert dc[0] == D_CARRY1
            dve.wait_ge(LD["ct"], 2)
            dstep(V.tensor_copy(carry_c[:, 0:1], bank[3][0:NC, 128:129]))
            dstep(V.tensor_tensor_scan(s3a[:, ::-1], on_c[:, ::-1], er[:, ::-1], carry_c[:, 0:1], ALU.mult, ALU.add))
            dstep(V.tensor_tensor(s3b, el, s3a, ALU.add))
            dstep(V.scalar_tensor_tensor(el, s3b, 0.2, s3b, ALU.mult, ALU.max))
            dstep(V.tensor_scalar(er, keep_c[:, :], -1.0, BIG, ALU.add, ALU.mult))
            dstep(V.tensor_tensor_scan(s3a, er, el, -BIG, ALU.add, ALU.max))
            dstep(V.tensor_reduce(edge_c[:, 0:1], er, AX_X, ALU.min))
            dstep(V.tensor_copy(edge_c[:, 2:3], s3a[:, CH - 1:CH]))
            assert dc[0] == D_SUM2
            dve.wait_ge(LD["ct"], 3)
            dstep(V.tensor_copy(top[0:1, :, 0:NC], bank[3][0:1, 0:128].rearrange("p (a b) -> p a b", a=2)[:, :, 0:NC]))
            dstep(V.memset(carry_r[:, :], -BIG))
            dstep(V.tensor_tensor_scan(carry_r[0:1, 1:NC + 1], top[0:1, 0, 0:NC], top[0:1, 1, 0:NC], -BIG, ALU.add, ALU.max))
            assert dc[0] == D_CARRY2
            dve.wait_ge(LD["ct"], 4)
            dstep(V.tensor_copy(carry_c[:, 0:1], bank[3][0:NC, 128:129]))
            mx = dstf_c[:, 0:CH + 1]
            dstep(V.tensor_copy(mx[:, 0:1], carry_c[:, 0:1]))
            dstep(V.tensor_tensor_scan(mx[:, 1:CH + 1], er, el, carry_c[:, 0:1], ALU.add, ALU.max))
            dstep(V.tensor_tensor(s3a, mx[:, 0:CH], mx[:, 1:CH + 1], ALU.subtract))
            dstep(V.tensor_scalar(s3a, s3a, 0.0, None, ALU.min))
            dstep(V.tensor_tensor(s3b, el, mx[:, 1:CH + 1], ALU.subtract))
            assert dc[0] == D_EXP
            dve.wait_ge(LD["ca"], 1)
            dstep(V.tensor_tensor(s2_c[:, 0, :], s2_c[:, 0, :], keep_c[:, :], ALU.mult))
            assert dc[0] == D_ROWS

            AT65 = AT[0:R, :].rearrange("p (k f) -> p k f", f=128)

            def slot_g(k, q, h, front, back):
                if front:
                    at_least(dve, G_ld[q], h * 64 + 64)
                    V.tensor_tensor(l_z[q][0:D, :], l_z[q][0:D, :], l_m[q][0:D, :], ALU.mult).then_inc(LE["msg"].sem, 1)
                    V.tensor_copy(l_z[q][D:D + 1, :], l_m[q][D:D + 1, :]).then_inc(LE["msg"].sem, 1)
                    at_least(dve, LE["aggT"], k - 1)
                    at_least(dve, LE["msg"], k * 2 + 2)
                    init = 0.0 if isinstance(k, int) and k == 0 else agg[(q - 1) % 2][0:D + 1, CH - 1:CH]
                    at_least(dve, LE["agg"], k)
                    V.tensor_tensor_scan(agg[q % 2][0:D + 1, :], l_k[q][:, :], l_z[q][:, :], init,
                                         ALU.mult, ALU.add).then_inc(LE["agg"].sem, 1)
                if back:
                    kb, qb, hb, pb = before(k, q, h)
                    at_least(dve, LE["aggT"], kb + 1)
                    V.tensor_scalar(lden[:, :], AT65[:, :, D], 0.0, None, ALU.is_equal).then_inc(LE["den"].sem, 1)
                    at_least(dve, LE["den"], kb + 1)
                    V.tensor_tensor(lmn[:, :], AT65[:, :, D], lden[:, :], ALU.add).then_inc(LE["den2"].sem, 1)
                    at_least(dve, LE["den2"], kb + 1)
                    V.reciprocal(lden[:, :], lmn[:, :]).then_inc(LE["rden"].sem, 1)
                    at_least(dve, LE["rden"], kb + 1)
                    V.tensor_tensor(v4(v_r[:, :]), AT65[:, :, 0:D], spread(lden[:, :], TC), ALU.mult).then_inc(LE["t1"].sem, 1)
                    at_least(dve, LE["t1"], kb + 1)
                    at_least(dve, LE["rows"], kb)
                    V.tensor_tensor(w_r[:, :], v_r[:, :], l_b[qb][:, :], ALU.add).then_inc(LE["t2"].sem, 1)
                    at_least(dve, LE["t2"], kb + 1)
                    V.tensor_tensor(v4(w_r[:, :]), v4(w_r[:, :]), row_bias(2, TC), ALU.add).then_inc(LE["t3"].sem, 1)
                    finish(LE, kb, qb, hb, w_r[:, :], G_st)
            chunk_slots(slot_g, dve)
            at_least(dve, LE["rows"], NC)

            def slot_f(k, q, h, front, back):
                p = q % 2
                if front:
                    live = tile_scalar(last_t, (NC - 1) - k if isinstance(k, int) else dve.snap(k * -1 + (NC - 1)))
                    at_least(dve, F_ld[q], h * 32 + 32)
                    at_least(dve, LF["msgT"], k - 1)
                    V.tensor_tensor(half(m_r[p]), half(l_a[q]), live, ALU.mult)\
                     .then_inc(LF["msg"].sem, 1)
                    at_least(dve, LF["msgT"], k + 1)
                    if isinstance(k, int):
                        at_least(dve, F_st[p], 16 * (k // 2))
                    else:
                        at_least(dve, F_st[p], h * 32 + (q // 2) * 16)
                    first = isinstance(k, int) and k == 0
                    at_least(dve, LF["fill"], k)
                    V.tensor_tensor_scan(agg[p][0:D, ::-1], l_k[q][0:D, ::-1], MT[0:D, 0:CH][:, ::-1],
                                         0.0 if first else agg[1 - p][0:D, 0:1], ALU.mult, ALU.add).then_inc(LF["fill"].sem, 1)
            chunk_slots(slot_f, dve)
            for r in range(2):
                at_least(dve, F_st[r], 16 * len(range(r, NC, 2)))

            def slot_m(k, q, h, front, back):
                p = q % 2
                if back:
                    kb, qb, hb, pb = before(k, q, h)
                    at_least(dve, LG["dn2"], kb + 1)
                    V.tensor_tensor(v4(v_r[:, :]), OTv, v4(l_b[qb][:, :]), ALU.add).then_inc(LG["t1"].sem, 1)
                    at_least(dve, LG["t1"], kb + 1)
                    at_least(dve, LG["rows"], kb)
                    V.tensor_tensor(v4(w_r[:, :]), v4(v_r[:, :]), row_bias(3, TC), ALU.add).then_inc(LG["t2"].sem, 1)
                if front:
                    at_least(dve, LG["msg"], k + 1)
                    at_least(dve, LG["agg"], k)
                    init = 0.0 if isinstance(k, int) and k == 0 else l_up[(q - 1) % 4][0:D, CH - 1:CH]
                    V.tensor_tensor_scan(l_up[q][0:D, :], l_k[q][0:D, :], l_m[q][0:D, :], init,
                                         ALU.mult, ALU.add).then_inc(LG["agg"].sem, 1)
                if back:
                    if isinstance(kb, int):
                        at_least(dve, M_sc[pb], 64 * ((kb - 4) // 2 + 1))
                    else:
                        at_least(dve, M_sc[pb], hb * 128 + ((qb // 2) * 64 - 64))
                    finish(LG, kb, qb, hb, w_r[:, :], None)
            chunk_slots(slot_m, dve)


C_ROWS = 4
C_SUM = 10
C_CARRY = 13
C_DD = 18
C_DINV = 23
C_INFO = 31
C_ALL = 37
PREP_TWO = 22
PREP_ALL = 29
D_SUM1, D_CARRY1, D_SUM2, D_CARRY2, D_EXP, D_ROWS = 4, 7, 15, 18, 24, 25

_INS = ["x", "dst", "edge_weight",
        "L0_gnn_W1", "L0_gnn_b1", "L0_gnn_W2", "L0_gnn_b2", "L1_gnn_W1", "L1_gnn_b1", "L1_gnn_W2", "L1_gnn_b2",
        "L2_gnn_W", "L2_gnn_attn_l", "L2_gnn_attn_r", "L2_gnn_bias", "L3_gnn_mW1", "L3_gnn_mb1", "L3_gnn_mW2",
        "L3_gnn_mb2", "L3_gnn_uW1", "L3_gnn_ub1", "L3_gnn_uW2", "L3_gnn_ub2"]


def kernel(**inputs):
    import numpy as _np
    import concourse.bacc as _bacc
    from concourse import mybir as _mybir
    from concourse.bass_utils import run_bass_kernel_spmd as _run

    given = {n: _np.asarray(inputs[n]) for n in _INS}
    for n, name in (("src", "src_by_tile"), ("dst", "dst_by_tile"), ("edge_weight", "edge_weight_by_tile")):
        given[name] = _np.asarray(inputs[n]).reshape(NT, R).T
    given["edge_attr_cols"] = _np.asarray(inputs["edge_attr_32"]).T
    nc = _bacc.Bacc("TRN2", target_bir_lowering=False, num_devices=1)
    arrays, t = {}, {}
    for name, a in given.items():
        a = _np.ascontiguousarray(a)
        arrays[f"in_{name}"] = a
        t[name] = nc.dram_tensor(f"in_{name}", a.shape, _mybir.dt.from_np(a.dtype), kind="ExternalInput").ap()
    out = nc.dram_tensor("out_rows", (N, D), F32, kind="ExternalOutput").ap()
    build(nc, t, out)
    r = _run(nc, [arrays], core_ids=[0])
    return r.results[0]["out_rows"]
```

```python
from contextlib import ExitStack

import concourse.bass as bass
from concourse import mybir

F32 = mybir.dt.float32
I32 = mybir.dt.int32
ALU = mybir.AluOpType
ACT = mybir.ActivationFunctionType
AX_X = mybir.AxisListType.X

N = 100000
E = 25000
D = 64
DE = 32
H = 128
R = 125
TB = 8
BLK = R * TB
BW = TB * D
TC = 4
CH = R * TC
CW = TC * D
NT = E // R
NC = E // CH
NB = N // BLK
NI = E // BLK
EPS = 1e-5
BIG = 3.0e38
FAR = 1.0e6


class Shared:

    def __init__(self, sem, base):
        self.sem, self.base = sem, base


class Unit:

    def __init__(self, n, real, stage, i, par, b2, b3):
        self.n, self.real, self.stage, self.i, self.par, self.b2, self.b3 = n, real, stage, i, par, b2, b3


def at_least(eng, sem, value):
    if isinstance(value, int) and value <= 0:
        return
    if isinstance(sem, Shared):
        sem, value = sem.sem, value + sem.base
    eng.wait_ge(sem, value)


def build(nc, t, out):
    ctx = ExitStack()
    with ctx:
        def sb(name, shape, dt=F32):
            return ctx.enter_context(nc.sbuf_tensor(name, shape, dt))

        def sem(name):
            return ctx.enter_context(nc.semaphore(name))

        def sems(prefix, names):
            return {n: sem(f"{prefix}_{n}") for n in names.split()}

        def dram(name, shape, dt=F32):
            return nc.dram_tensor(name, shape, dt, kind="Internal").ap()

        xs_d = dram("xs_rows", (E, D))
        xd_d = dram("xd_rows", (E, D))
        t0_d = dram("t0_h0", (E, D))
        t1_d = dram("t1_x1", (2 * E, D))
        t2_d = dram("t2_h2", (2 * E, D))
        t3_d = dram("t3_x2", (2 * E, D))
        t4_d = dram("t4_x3", (2 * E, D))
        info_d = dram("node_info", (N, 4))
        keep_d = dram("keep_row", (NC, CH))
        on_d = dram("on_row", (NC, CH))
        z_d = dram("z_cols", (NC, D + 2, CH))
        decay_d = dram("decay_row", (NC, CH))
        ex_d = dram("ex_row", (NC, CH))
        x3f_d = dram("x3_filled", (NC, D, CH))

        def chunks(ap):
            return ap.rearrange("(c k p) f -> c p k f", k=TC, p=R)

        def blocks(ap):
            return ap.rearrange("(b j p) f -> b p j f", j=TB, p=R)

        ident = sb("ident", [128, 128])
        w_top = [sb(f"w_top{s}", [128, H]) for s in range(3)]
        w_bot = [sb(f"w_bot{s}", [128, H]) for s in range(3)]
        w_dn = [sb(f"w_dn{s}", [H, 128]) for s in range(3)]
        b_up = sb("b_up", [H, 3])
        b_dn = sb("b_dn", [128, 3])
        b_row = sb("b_row", [128, 4, D])
        b_two = sb("b_two", [128, 3, 128])
        gat_w = sb("gat_w", [128, 128])
        gat_raw = sb("gat_raw", [128, D])
        gat_att = sb("gat_att", [128, D])
        gat_tmp = sb("gat_tmp", [128, D])
        w_msg = sb("w_msg", [128, H])
        w_edge = sb("w_edge", [128, H])
        w_msg2 = sb("w_msg2", [H, D])
        w_upd = sb("w_upd", [128, H])
        b_msg = sb("b_msg", [H, 1])
        b_msg2 = sb("b_msg2", [D, 1])
        mean6 = sb("mean6", [128, 8])
        eps = sb("eps", [128, 1])
        wide = sb("wide", [128, 8 * CH])
        info_fill = wide[0:R, 0:N // R * 4]

        src_i = sb("src_i", [R, NT], I32)
        dst_i = sb("dst_i", [R, NT], I32)
        ew_t = sb("ew_t", [R, NT])
        d0_t = sb("d0_t", [R, NT])
        d1_t = sb("d1_t", [R, NT])
        last_t = sb("last_t", [R, NT])
        w0_t = sb("w0_t", [R, NT])
        w1_t = sb("w1_t", [R, NT])
        gidx = sb("gidx", [R, NT], I32)
        gfl = sb("gfl", [R, NT])
        gbase = sb("gbase", [R, NT])
        slot_id = sb("slot_id", [R, NT])
        info_r = sb("info_r", [R, NT, 4])
        sidx = sb("sidx", [R, NT], I32)

        dst_c = sb("dst_c", [NC, CH + 2], I32)
        dstf_c = sb("dstf_c", [NC, CH + 2])
        ew_c = sb("ew_c", [NC, CH])
        one_c = sb("one_c", [NC, CH])
        keep_c = sb("keep_c", [NC, CH])
        last_c = sb("last_c", [NC, CH])
        on_c = sb("on_c", [NC, CH])
        s1_c = sb("s1_c", [NC, 2, CH])
        s2_c = sb("s2_c", [NC, 2, CH])
        s3_c = sb("s3_c", [NC, 2, CH])
        edge_c = sb("edge_c", [NC, 4])
        top = sb("top", [2, 2, NC + 1])
        carry_r = sb("carry_r", [2, NC + 1])
        carry_c = sb("carry_c", [NC, 2])

        x_in = [sb(f"x_in{i}", [R, BW]) for i in range(2)]
        x1_r_all = [sb(f"x1_r{i}", [128, BW]) for i in range(2)]
        x1_r = [b[0:R, :] for b in x1_r_all]
        x2_r_all = [sb(f"x2_r{i}", [128, BW]) for i in range(2)]
        x2_r = [b[0:R, :] for b in x2_r_all]
        x3_r_all = [sb(f"x3_r{i}", [128, BW]) for i in range(2)]
        x3_r = [b[0:R, :] for b in x3_r_all]
        x4_r_all = [sb(f"x4_r{i}", [128, BW]) for i in range(2)]
        x4_r = [b[0:R, :] for b in x4_r_all]
        h0_r_all = [sb(f"h0_r{i}", [128, BW]) for i in range(2)]
        h0_r = [b[0:R, :] for b in h0_r_all]
        h2_r_all = [sb(f"h2_r{i}", [128, BW]) for i in range(2)]
        h2_r = [b[0:R, :] for b in h2_r_all]
        xT = [sb(f"xT{i}", [128, CH]) for i in range(3)]
        hid = [sb(f"hid{i}", [128, 2, CH]) for i in range(2)]
        rT = [sb(f"rT{i}", [128, CH]) for i in range(2)]
        x_up = sb("x_up", [128, 128])
        cmat = sb("cmat", [128, 128])
        sq = [sb(f"sq{i}", [R, BW]) for i in range(2)]
        y_r = sb("y_r", [R, BW])
        sq_b = sb("sq_b", [R, BW])
        ss = [sb(f"ss{i}", [R, TB]) for i in range(2)]
        sd = [sb(f"sd{i}", [R, TB]) for i in range(2)]
        rs = sb("rs", [R, TB])
        ss_b, sd_b, rs_b = sb("ss_b", [R, TB]), sb("sd_b", [R, TB]), sb("rs_b", [R, TB])

        p_idx = [sb(f"p_idx{i}", [R, TB], I32) for i in range(2)]
        p_row = [sb(f"p_row{i}", [R, BW]) for i in range(2)]
        g_idx = [sb(f"g_idx{i}", [R, TC], I32) for i in range(4)]
        g_row = [sb(f"g_row{i}", [R, TC * 128]) for i in range(4)]
        o_idx = [sb(f"o_idx{i}", [R, TC], I32) for i in range(2)]

        l_src = [sb(f"l_src{i}", [R, CW]) for i in range(4)]
        l_a = [sb(f"l_a{i}", [R, TC * 128]) for i in range(4)]
        l_b = [sb(f"l_b{i}", [R, CW]) for i in range(4)]
        l_k = [sb(f"l_k{i}", [D + 1, CH]) for i in range(4)]
        l_m = [wide[0:D + 1, i * CH:(i + 1) * CH] for i in range(4, 8)]
        l_z = [wide[0:D + 1, i * CH:(i + 1) * CH] for i in range(4)]
        l_in = [b[:, 0:CH] for b in x1_r_all + x2_r_all]
        l_up = [b[:, 0:CH] for b in x3_r_all + x4_r_all]
        l_ea = [b[:, 0:CH] for b in h0_r_all + h2_r_all]
        m_r = [sb(f"m_r{i}", [R, TC * 128]) for i in range(2)]
        agg = [sb(f"agg{i}", [128, CH]) for i in range(2)]
        zx = [sb(f"zx{i}", [D + 2, CH]) for i in range(2)]
        lxT = [sb(f"lxT{i}", [128, CH]) for i in range(4)]
        lhid = [sb(f"lhid{i}", [128, CH]) for i in range(2)]
        lhid2 = [sb(f"lhid2{i}", [128, CH]) for i in range(2)]
        u_r = [sb(f"u_r{i}", [R, TC * 128]) for i in range(2)]
        v_r = sb("v_r", [R, CW])
        w_rs = [sb(f"w_r{i}", [R, CW]) for i in range(2)]
        w_r = w_rs[0]
        n_r = [sb(f"n_r{i}", [R, CW]) for i in range(4)]
        lsq = sb("lsq", [R, CW])
        lmn, lss, lsd, lrs, lden = (sb(f"l_{x}", [R, TC]) for x in ("mn", "ss", "sd", "rs", "den"))
        zero1 = sb("zero1", [128, 1])

        bank = [ctx.enter_context(nc.psum_tensor(f"bank{i}", [128, 512], F32)) for i in range(4)]
        pair = [ctx.enter_context(nc.psum_tensor(f"pair{i}", [128, 2, 512], F32)) for i in range(2)]

        s_w = sem("weights_loaded")
        s_e = sem("edges_loaded")
        s_pad = sem("dst_padding_set")
        s_pool0 = sem("ident_steps")
        s_set = sem("sbuf_zeroed")
        s_prep = sem("dve_weight_steps")
        s_bt = sem("bias_transposed")
        s_c = sem("dve_scalar_steps")
        s_ct = sem("scalar_transposes")
        s_ca = sem("act_scalar_steps")
        s_rows = sem("scalar_rows_stored")
        s_init = sem("node_info_initialised")
        P = sems("pool", "copied idx0 idx1 xs0 xs1 xss0 xss1 sc0 sc1 inf0 inf1 xd0 xd1 xds0 xds1")
        Cn = sems("chain", "rowsT xT up hid dn res resT h0 h0b h2 h2b sq ssum std rstd"
                           " rows y sq2 ssum2 std2 rstd2 rows2 in0 in1 out0 out1 s0st0 s0st1 s1st0 s1st1")

        ctx.enter_context(nc.allow_non_contiguous_dma(reason="bias columns and the chunks' neighbours, once"))
        block = ctx.enter_context(nc.Block())

        W1 = [t["L0_gnn_W1"], t["L1_gnn_W1"], t["L3_gnn_uW1"][0:D, :]]
        W2 = [t["L0_gnn_W2"], t["L1_gnn_W2"], t["L3_gnn_uW2"]]
        B1 = [t["L0_gnn_b1"], t["L1_gnn_b1"], t["L3_gnn_ub1"]]
        BR = [t["L0_gnn_b2"], t["L1_gnn_b2"], t["L2_gnn_bias"], t["L3_gnn_ub2"]]

        def column(ap):
            return ap.rearrange("(p a) -> p a", a=1)

        def everywhere(ap, p=128):
            return ap.rearrange("(a f) -> a f", a=1).to_broadcast([p, ap.shape[0]])

        weight_loads = []
        for s in range(3):
            weight_loads += [(w_top[s][0:D, :], W1[s]), (w_bot[s][D:128, :], W1[s]), (w_dn[s][:, 0:D], W2[s]),
                             (b_up[:, s:s + 1], column(B1[s]))]
        weight_loads += [(b_row[:, i, :], everywhere(BR[i])) for i in range(4)]
        weight_loads += [(gat_raw[0:D, :], t["L2_gnn_W"]), (gat_raw[D:128, :], t["L2_gnn_W"]),
                         (gat_att[0:D, :], everywhere(t["L2_gnn_attn_l"], D)),
                         (gat_att[D:128, :], everywhere(t["L2_gnn_attn_r"], D)),
                         (w_msg[:, :], t["L3_gnn_mW1"][0:128, :]), (w_edge[0:DE, :], t["L3_gnn_mW1"][128:160, :]),
                         (w_msg2[:, :], t["L3_gnn_mW2"]), (w_upd[0:D, :], t["L3_gnn_uW1"][D:128, :]),
                         (w_upd[D:128, :], t["L3_gnn_uW1"][0:D, :]),
                         (b_msg[:, :], column(t["L3_gnn_mb1"])), (b_msg2[:, :], column(t["L3_gnn_mb2"]))]
        ALL_W = 16 * len(weight_loads)
        dst2 = t["dst"].rearrange("(c j) -> c j", j=CH)
        edge_loads = [(dst_c[:, 1:CH + 1], dst2), (dst_c[1:NC, 0:1], dst2[0:NC - 1, CH - 1:CH]),
                      (dst_c[0:NC - 1, CH + 1:CH + 2], dst2[1:NC, 0:1]),
                      (ew_c[:, :], t["edge_weight"].rearrange("(c j) -> c j", j=CH)),
                      (src_i[:, :], t["src_by_tile"]), (dst_i[:, :], t["dst_by_tile"]),
                      (ew_t[:, :], t["edge_weight_by_tile"])]
        ALL_E = 16 * len(edge_loads)
        N_ONES = 9 + 4 + 4 + 4 + 2 + 2 + 2
        N_SET = 13

        STAGE = [1, 0, 2]
        LAST = NB + NI
        MS = (LAST + 5) // 2
        UNITS = 6 * MS
        W0 = NB // 2

        def unit(m, u):
            q, pos = u // 3, u % 3
            real = (not isinstance(m, int)) or 0 <= 6 * m + u < UNITS
            return Unit(m * 6 + u, real, STAGE[pos], m * 2 + q, q % 2, u % 2, u % 3)

        def node_slots(slot, eng, pairs_loop, straight_after):
            slot(0, -1)
            for u in range(6):
                slot(0, u)
            for lo, hi in pairs_loop:
                if isinstance(hi, int) and hi - lo > 1:
                    with eng.Fori(lo, hi, 1) as m:
                        for u in range(6):
                            slot(m, u)
                else:
                    for u in range(6):
                        slot(lo, u)
            for m in straight_after:
                for u in range(6):
                    slot(m, u)
            for u in range(5):
                slot(MS, u)

        def half(buf):
            return buf[:, :].rearrange("p (k f) -> p k f", f=128)[:, :, 0:D]

        def n_view(ap):
            return ap.rearrange("p (j f) -> p j f", f=D)

        def spread(col, n):
            return col.unsqueeze(2).to_broadcast([R, n, D])

        def row_bias(i, n):
            return b_row[0:R, i, :].unsqueeze(1).to_broadcast([R, n, D])

        def chunk_slots(slot, eng):
            for k in range(8):
                slot(k, k % 4, k // 4, True, k > 0)
            with eng.Fori(2, NC // 4, 1) as j:
                for q in range(4):
                    slot(j * 4 + q, q, j, True, True)
            for k in range(4 * (NC // 4), NC):
                slot(k, k % 4, k // 4, True, True)
            slot(NC, NC % 4, NC // 4, False, True)

        def lagged_slots(slot, eng, deepest):
            def where(k, q, h):
                def at(lag):
                    if isinstance(k, int) and not 0 <= k - lag < NC:
                        return None
                    return k - lag, (q - lag) % 4, h + (q - lag) // 4, (q - lag) % 2
                return at

            for k in range(12):
                slot(where(k, k % 4, k // 4))
            with eng.Fori(3, NC // 4, 1) as j:
                for q in range(4):
                    slot(where(j * 4 + q, q, j))
            for k in range(4 * (NC // 4), NC + deepest):
                slot(where(k, k % 4, k // 4))

        def before(k, q, h):
            return k - 1, (q - 1) % 4, (h if q else h - 1), (q - 1) % 2

        shared, counted = {}, {}

        def level_sems(names, twice=()):
            made = {}
            for name in names.split():
                if name not in shared:
                    shared[name], counted[name] = sem(f"level_{name}"), 0
                made[name] = Shared(shared[name], counted[name])
                counted[name] += NC * (2 if name in twice else 1)
            return made

        def in_turn(name, n, per_chunk):
            made = []
            for r in range(n):
                key = f"{name}{r}"
                if key not in shared:
                    shared[key], counted[key] = sem(f"level_{key}"), 0
                made.append(Shared(shared[key], counted[key]))
                counted[key] += per_chunk * len(range(r, NC, n))
            return made

        LA = level_sems("msg msgT agg aggT xdT xcol xc up hid dn t1 t2 t3 t4 sq ssum std rstd rows")
        LB = level_sems("msg msgT agg aggT t1 t2 u uT ucol up hid dn rows")
        LC = level_sems("msg msgT agg aggT t1 t2 t3 t4 t5 sq ssum std rstd rows")
        LD = level_sems("lky1 lky2 lkyT col zx zc")
        LE = level_sems("msg agg aggT den den2 rden t1 t2 t3 sq ssum std rstd rows", twice=("msg",))
        LF = level_sems("msg msgT fill")
        LG = level_sems("srcT scol up hid dn msg agg up2 hid2 dn2 t1 t2 sq ssum std rstd rows")
        LD["c"], LD["ct"], LD["ca"] = sem("score_steps"), sem("score_transposes"), sem("score_exp")
        A_ld, A_st = in_turn("ld", 4, 48), in_turn("st", 4, 16)
        B_ld, B_ga, B_st = in_turn("ld", 4, 32), in_turn("ga", 4, 64), in_turn("st", 4, 16)
        C_ld, C_ga, C_st = in_turn("ld", 4, 48), in_turn("ga", 4, 64), in_turn("st", 4, 16)
        D_ld, D_ga, D_st = in_turn("ld", 4, 16), in_turn("ga", 4, 64), in_turn("zst", 2, 16)
        G_ld, G_st = in_turn("ld", 4, 64), in_turn("st", 4, 16)
        F_ld, F_st = in_turn("ld", 4, 32), in_turn("zst", 2, 16)
        M_ld, M_ga, M_sc = in_turn("ld", 4, 80), in_turn("ga", 4, 64), in_turn("sc", 2, 64)
        s_ones = sem("gat_ones_row")

        def all_stored(eng, st, k_total=NC, n=4):
            for r in range(n):
                at_least(eng, st[r], 16 * len(range(r, k_total, n)))

        @block.sync
        def _(sp):
            sp.wait_ge(s_pad, 1)
            for dst, src in edge_loads:
                sp.dma_start(dst, src).then_inc(s_e, 16)
            sp.wait_ge(s_set, N_SET)
            for dst, src in weight_loads:
                sp.dma_start(dst, src).then_inc(s_w, 16)
            sp.dma_start(info_d.rearrange("(p a) c -> p (a c)", p=R), info_fill).then_inc(s_init, 16)
            sp.wait_ge(s_c, C_ROWS)
            sp.dma_start(keep_d, keep_c[:, :]).then_inc(s_rows, 16)
            sp.dma_start(on_d, on_c[:, :]).then_inc(s_rows, 16)

            dense_in = t["x"].rearrange("(b p j) f -> b p (j f)", p=R, j=TB)
            dense_out = out.rearrange("(b p j) f -> b p (j f)", p=R, j=TB)
            xs_v = blocks(xs_d)
            in_sem, out_sem = [Cn["in0"], Cn["in1"]], [Cn["out0"], Cn["out1"]]
            s0_sem, s1_sem = [Cn["s0st0"], Cn["s0st1"]], [Cn["s1st0"], Cn["s1st1"]]

            def load(i, par, half, iso, first=False):
                if iso:
                    b, h0_read, xs_stored = i - NB, i - (NB + 1), (half - (NB // 2 - 1)) * 16
                    if not isinstance(i, int):
                        b = sp.snap(b)
                if iso:
                    at_least(sp, Cn["h0"], h0_read)
                if not first:
                    sp.wait_ge(Cn["rowsT"], i * 3 - 4)
                if iso:
                    sp.wait_ge([P["xss0"], P["xss1"]][par], xs_stored)
                    sp.dma_start(n_view(x_in[par][:, :]), xs_v[b]).then_inc(in_sem[par], 16)
                else:
                    sp.dma_start(x_in[par][:, :], dense_in[i]).then_inc(in_sem[par], 16)

            def store_dense(i, par):
                sp.wait_ge(Cn["rows"], i * 3 + 3)
                sp.dma_start(dense_out[i - 4], x4_r[par][:, :]).then_inc(out_sem[par], 16)

            def store_s0(i, par):
                b = i - NB
                sp.wait_ge(Cn["h0b"], b + 1)
                sp.dma_start(blocks(t0_d)[b], n_view(h0_r[par][:, :])).then_inc(s0_sem[par], 16)
                sp.wait_ge(Cn["rows"], i * 3 + 2)
                sp.dma_start(blocks(t1_d[E:2 * E, :])[b], n_view(x1_r[par][:, :])).then_inc(s0_sem[par], 16)

            def store_s1(i, par):
                b = i - NB - 2
                sp.wait_ge(Cn["h2b"], b + 1)
                sp.dma_start(blocks(t2_d[E:2 * E, :])[b], n_view(h2_r[par][:, :])).then_inc(s1_sem[par], 16)
                sp.wait_ge(Cn["rows"], i * 3 + 1)
                sp.dma_start(blocks(t3_d[E:2 * E, :])[b], n_view(x2_r[par][:, :])).then_inc(s1_sem[par], 16)
                sp.wait_ge(Cn["rows2"], i + 1)
                sp.dma_start(blocks(t4_d[E:2 * E, :])[b], n_view(x3_r[par][:, :])).then_inc(s1_sem[par], 16)

            def iteration(i):
                if i + 1 < LAST:
                    load(i + 1, (i + 1) % 2, (i + 1) // 2, i + 1 >= NB, first=i + 1 < 2)
                j = i - 1
                if NB <= j < LAST:
                    store_s0(j, j % 2)
                if NB + 2 <= j < LAST + 2:
                    store_s1(j, j % 2)
                if 4 <= j < NB + 4:
                    store_dense(j, j % 2)

            for i in range(-1, 6):
                iteration(i)
            with sp.Fori(3, NB // 2 - 1, 1) as m:
                for q in range(2):
                    load(m * 2 + (q + 1), (q + 1) % 2, None, False)
                    store_dense(m * 2 + (q - 1), (q - 1) % 2)
            for i in range(NB - 2, NB + 6):
                iteration(i)
            with sp.Fori(NB // 2 + 3, LAST // 2 - 1, 1) as m:
                for q in range(2):
                    load(m * 2 + (q + 1), (q + 1) % 2, m + (q + 1) // 2, True)
                    store_s0(m * 2 + (q - 1), (q - 1) % 2)
                    store_s1(m * 2 + (q - 1), (q - 1) % 2)
            for i in range(2 * (LAST // 2 - 1), LAST + 4):
                iteration(i)

            sp.wait_ge(s_ones, N_ONES)
            sp.wait_ge(s_rows, 32)
            for r in range(2):
                sp.wait_ge([P["xds0"], P["xds1"]][r], 16 * len(range(r, NI, 2)))
                sp.wait_ge(s0_sem[r], 32 * len(range(r, NI, 2)))

            def rows_of(table):
                return chunks(table[0:E, :])

            def level(loads, ld, used, st, done, where, behind=0):
                def ld_chunk(k, q, first):
                    pairs = loads(k, q)
                    if not first:
                        for s in used:
                            at_least(sp, s, k - 3)
                    for to, frm in pairs:
                        sp.dma_start(to, frm).then_inc(ld[q].sem, 16)

                def st_chunk(k, q):
                    to, frm = where(k, q)
                    at_least(sp, done, k + 1)
                    sp.dma_start(to, frm).then_inc(st[q % len(st)].sem, 16)

                for k in range(4):
                    ld_chunk(k, k, True)
                for k in range(8):
                    ld_chunk(k + 4, k % 4, False)
                    if k >= behind:
                        st_chunk(k - behind, (k - behind) % 4)
                with sp.Fori(2, NC // 4 - 1, 1) as j:
                    for q in range(4):
                        ld_chunk(j * 4 + (q + 4), q, False)
                        st_chunk(j * 4 + (q - behind), (q - behind) % 4)
                for k in range(4 * (NC // 4 - 1), NC + behind):
                    if k + 4 < NC:
                        ld_chunk(k + 4, k % 4, False)
                    st_chunk(k - behind, (k - behind) % 4)

            def bc(row_d, k, p):
                return row_d[k].rearrange("(a f) -> a f", a=1).to_broadcast([p, CH]) if isinstance(k, int) \
                    else row_d[k].rearrange("(a f) -> a f", a=1).to_broadcast([p, CH])

            def v4(ap):
                return ap.rearrange("p (k f) -> p k f", f=D)

            level(lambda k, q: [(v4(l_src[q][:, :]), chunks(t0_d)[k]), (half(l_a[q]), chunks(xd_d)[k]),
                                (l_k[q][0:D, :], bc(keep_d, k, D))],
                  A_ld, [LA["xdT"], LA["agg"]], A_st, LA["rows"], lambda k, q: (rows_of(t1_d)[k], v4(n_r[q][:, :])), behind=3)
            all_stored(sp, A_st)
            level(lambda k, q: [(half(l_a[q]), rows_of(t1_d)[k]), (l_k[q][0:D, :], bc(keep_d, k, D))],
                  B_ld, [LB["agg"], LB["t1"]], B_st, LB["rows"], lambda k, q: (rows_of(t2_d)[k], v4(n_r[q][:, :])), behind=3)
            all_stored(sp, B_st)
            level(lambda k, q: [(half(l_a[q]), rows_of(t2_d)[k]), (v4(l_b[q][:, :]), rows_of(t1_d)[k]),
                                (l_k[q][0:D, :], bc(keep_d, k, D))],
                  C_ld, [LC["rows"]], C_st, LC["rows"], lambda k, q: (rows_of(t3_d)[k], v4(n_r[q][:, :])))
            all_stored(sp, C_st)
            level(lambda k, q: [(half(l_a[q]), rows_of(t3_d)[k])],
                  D_ld, [LD["lky2"]], D_st, LD["zc"], lambda k, q: (z_d[k], zx[q % 2][:, :]))
            for r in range(2):
                at_least(sp, D_st[r], 16 * len(range(r, NC, 2)))
            sp.dma_start(s1_c[:, 0, :], z_d[:, D, :]).then_inc(s_rows, 16)
            sp.dma_start(s1_c[:, 1, :], z_d[:, D + 1, :]).then_inc(s_rows, 16)
            sp.wait_ge(LD["c"], D_ROWS)
            sp.dma_start(decay_d, s2_c[:, 0, :]).then_inc(s_rows, 16)
            sp.dma_start(ex_d, s2_c[:, 1, :]).then_inc(s_rows, 16)
            sp.wait_ge(s_rows, 96)
            sp.wait_ge(s_ones, N_ONES)
            level(lambda k, q: [(l_z[q][0:D, :], z_d[k, 0:D, :]), (l_m[q][:, :], bc(ex_d, k, D + 1)),
                                (l_k[q][:, :], bc(decay_d, k, D + 1)), (v4(l_b[q][:, :]), rows_of(t3_d)[k])],
                  G_ld, [LE["rows"]], G_st, LE["rows"], lambda k, q: (rows_of(t4_d)[k], v4(n_r[q][:, :])))
            all_stored(sp, G_st)
            def mirror(eng, k):
                return (NC - 1) - k if isinstance(k, int) else eng.snap(k * -1 + (NC - 1))

            level(lambda k, q: [(half(l_a[q]), rows_of(t4_d)[mirror(sp, k)]),
                                (l_k[q][0:D, :], bc(on_d, mirror(sp, k), D))],
                  F_ld, [LF["fill"]], F_st, LF["fill"],
                  lambda k, q: (x3f_d[mirror(sp, k)], agg[q % 2][0:D, :]))
            for r in range(2):
                at_least(sp, F_st[r], 16 * len(range(r, NC, 2)))

            def ld_m(k, q, first):
                if not first:
                    at_least(sp, LG["rows"], k - 3)
                for to, frm in [(l_in[q][D:128, :], x3f_d[k]), (l_up[q][D:128, :], x3f_d[k]),
                                (l_ea[q][0:DE, :], t["edge_attr_cols"].rearrange("f (c j) -> c f j", j=CH)[k]),
                                (l_k[q][0:D, :], bc(keep_d, k, D)), (v4(l_b[q][:, :]), rows_of(t4_d)[k])]:
                    sp.dma_start(to, frm).then_inc(M_ld[q].sem, 16)

            for k in range(4):
                ld_m(k, k, True)
            for k in range(4):
                ld_m(k + 4, k, False)
            with sp.Fori(1, NC // 4 - 1, 1) as j:
                for q in range(4):
                    ld_m(j * 4 + (q + 4), q, False)
            for k in range(4 * (NC // 4), NC):
                ld_m(k, k % 4, False)

        @block.gpsimd
        def _(pool):
            g = nc.gpsimd
            g.memset(ident[:, :], 0.0).then_inc(s_pool0, 1)
            pool.wait_ge(s_pool0, 1)
            g.affine_select(out=ident[:, :], in_=ident[:, :], compare_op=ALU.not_equal, fill=1.0, base=0,
                            pattern=[[-1, 128]], channel_multiplier=1).then_inc(s_pool0, 1)
            g.iota(slot_id[:, :], pattern=[[R, NT]], base=0, channel_multiplier=1,
                   allow_small_or_imprecise_dtypes=True).then_inc(s_pool0, 1)
            g.iota(gbase[:, :], pattern=[[R, NT]], base=E, channel_multiplier=1,
                   allow_small_or_imprecise_dtypes=True).then_inc(s_pool0, 1)
            pool.wait_ge(s_e, ALL_E)
            n_nodes, n_rows = pool.to_reg(N), pool.to_reg(2 * E)

            bound = pool.alloc_register("row_bound")

            def settle(rows):
                pool.reg_add(bound, rows, -1)

            def over_units(body, total):
                body(0, 0, 0)
                body(1, 1, 0)
                with pool.Fori(1, total // 2, 1) as j:
                    for q in range(2):
                        body(j * 2 + q, q, j)
                for b in range(2 * (total // 2), total):
                    body(b, b % 2, b // 2)

            copied = [0]

            def rows_by_index(idx, sem_got, sem_stored, to_d, base):
                def body(b, par, half):
                    at_least(pool, sem_stored[par], half * 16)
                    g.tensor_copy(p_idx[par][:, :], idx[:, bass.ds(b * TB, TB)]).then_inc(P["copied"], 1)
                    pool.wait_ge(P["copied"], b + (base + 1))
                    settle(n_nodes)
                    for j in range(TB):
                        g.indirect_dma_start(
                            out=p_row[par][:, j * D:(j + 1) * D], out_offset=None, in_=t["x"],
                            in_offset=bass.IndirectOffsetOnAxis(ap=p_idx[par][:, j:j + 1], axis=0),
                            bounds_check=bound, oob_is_err=False).then_inc(sem_got[par], 16)
                    pool.wait_ge(sem_got[par], (half + 1) * (16 * TB))
                    pool.dma_start(blocks(to_d)[b], n_view(p_row[par][:, :])).then_inc(sem_stored[par], 16)
                over_units(body, NI)

            rows_by_index(src_i, [P["xs0"], P["xs1"]], [P["xss0"], P["xss1"]], xs_d, 0)

            pool.wait_ge(s_init, 16)
            pool.wait_ge(s_c, C_INFO)
            sc = [P["sc0"], P["sc1"]]

            def scatter_info(b, par, half):
                at_least(pool, sc[par], half * (16 * TB))
                g.tensor_copy(p_idx[par][:, :], sidx[:, bass.ds(b * TB, TB)]).then_inc(P["copied"], 1)
                g.tensor_copy(p_row[par][:, 0:TB * 4], info_r[:, :, :].rearrange("p t c -> p (t c)")
                              [:, bass.ds(b * (TB * 4), TB * 4)]).then_inc(P["copied"], 1)
                pool.wait_ge(P["copied"], b * 2 + (NI + 2))
                settle(n_nodes)
                for j in range(TB):
                    g.indirect_dma_start(
                        out=info_d, out_offset=bass.IndirectOffsetOnAxis(ap=p_idx[par][:, j:j + 1], axis=0),
                        in_=p_row[par][:, 4 * j:4 * j + 4], in_offset=None,
                        bounds_check=bound, oob_is_err=False).then_inc(sc[par], 16)

            for r in range(2):
                pool.wait_ge([P["xss0"], P["xss1"]][r], 16 * len(range(r, NI, 2)))
            over_units(scatter_info, NI)
            for r in range(2):
                pool.wait_ge(sc[r], 16 * TB * len(range(r, NI, 2)))

            got = [P["inf0"], P["inf1"]]

            def gather_info(b, par, half):
                g.tensor_copy(p_idx[par][:, :], src_i[:, bass.ds(b * TB, TB)]).then_inc(P["copied"], 1)
                pool.wait_ge(P["copied"], b * 2 + (3 * NI + 1))
                settle(n_nodes)
                for j in range(TB):
                    g.indirect_dma_start(
                        out=p_row[par][:, 4 * j:4 * j + 4], out_offset=None, in_=info_d,
                        in_offset=bass.IndirectOffsetOnAxis(ap=p_idx[par][:, j:j + 1], axis=0),
                        bounds_check=bound, oob_is_err=False).then_inc(got[par], 16)
                pool.wait_ge(got[par], (half + 1) * (16 * TB))
                g.tensor_copy(info_r[:, :, :].rearrange("p t c -> p (t c)")[:, bass.ds(b * (TB * 4), TB * 4)],
                              p_row[par][:, 0:TB * 4]).then_inc(P["copied"], 1)

            over_units(gather_info, NI)
            pool.wait_ge(P["copied"], 5 * NI)
            rows_by_index(dst_i, [P["xd0"], P["xd1"]], [P["xds0"], P["xds1"]], xd_d, 5 * NI)

            def gather_level(table, ga, used, n_before):
                def body(k, q, h):
                    used(k)
                    g.tensor_copy(g_idx[q][:, :], gidx[:, bass.ds(k * TC, TC)]).then_inc(P["copied"], 1)
                    pool.wait_ge(P["copied"], k + (7 * NI - NI + n_before + 1))
                    settle(n_rows)
                    for j in range(TC):
                        g.indirect_dma_start(
                            out=g_row[q][:, j * 128:j * 128 + D], out_offset=None, in_=table,
                            in_offset=bass.IndirectOffsetOnAxis(ap=g_idx[q][:, j:j + 1], axis=0),
                            bounds_check=bound, oob_is_err=False).then_inc(ga[q].sem, 16)
                for k in range(4):
                    body(k, k, 0)
                with pool.Fori(1, NC // 4, 1) as j:
                    for q in range(4):
                        body(j * 4 + q, q, j)
                for k in range(4 * (NC // 4), NC):
                    body(k, k % 4, k // 4)

            for r in range(2):
                pool.wait_ge([Cn["s0st0"], Cn["s0st1"]][r], 32 * len(range(r, NI, 2)))
                pool.wait_ge([Cn["s1st0"], Cn["s1st1"]][r], 48 * len(range(r, NI, 2)))
            pool.wait_ge(s_c, C_ALL)
            pool.wait_ge(s_ones, N_ONES)
            all_stored(pool, A_st)
            gather_level(t1_d, B_ga, lambda k: at_least(pool, LB["msg"], k - 3), 0)
            all_stored(pool, B_st)
            gather_level(t2_d, C_ga, lambda k: at_least(pool, LC["msg"], k - 3), NC)
            all_stored(pool, C_st)
            gather_level(t3_d, D_ga, lambda k: at_least(pool, LD["lky1"], k - 3), 2 * NC)
            all_stored(pool, G_st)

            out_sem = [Cn["out0"], Cn["out1"]]
            for r in range(2):
                pool.wait_ge(out_sem[r], 16 * len(range(r, NB, 2)))

            def m_gather(k, q):
                at_least(pool, LG["srcT"], k - 3)
                g.tensor_copy(g_idx[q][:, :], gidx[:, bass.ds(k * TC, TC)]).then_inc(P["copied"], 1)
                for j in range(TC):
                    if j == 0:
                        pool.wait_ge(P["copied"], m_copies(k, True))
                        settle(n_rows)
                    g.indirect_dma_start(
                        out=g_row[q][:, j * 128:j * 128 + D], out_offset=None, in_=t4_d,
                        in_offset=bass.IndirectOffsetOnAxis(ap=g_idx[q][:, j:j + 1], axis=0),
                        bounds_check=bound, oob_is_err=False).then_inc(M_ga[q].sem, 16)

            M_LAG = 4
            BASE = 6 * NI + 3 * NC

            def m_copies(k, gather):
                if gather:
                    if isinstance(k, int):
                        return BASE + k + 1 + max(0, k - M_LAG)
                    return k * 2 + (BASE + 1 - M_LAG)
                if isinstance(k, int):
                    return BASE + (k + 1) + min(NC, k + 1 + M_LAG)
                return k * 2 + (BASE + 2 + M_LAG)

            def m_scatter(k, q, h):
                par = q % 2
                if isinstance(k, int):
                    at_least(pool, M_sc[par], 64 * (k // 2))
                else:
                    at_least(pool, M_sc[par], h * 128 + (q // 2) * 64)
                g.tensor_copy(o_idx[par][:, :], sidx[:, bass.ds(k * TC, TC)]).then_inc(P["copied"], 1)
                pool.wait_ge(P["copied"], m_copies(k, False))
                at_least(pool, LG["rows"], k + 1)
                settle(n_nodes)
                for j in range(TC):
                    g.indirect_dma_start(
                        out=out, out_offset=bass.IndirectOffsetOnAxis(ap=o_idx[par][:, j:j + 1], axis=0),
                        in_=n_r[q][:, j * D:(j + 1) * D], in_offset=None,
                        bounds_check=bound, oob_is_err=False).then_inc(M_sc[par].sem, 16)

            for k in range(8):
                m_gather(k, k % 4)
                if k >= M_LAG:
                    m_scatter(k - M_LAG, k % 4, 0)
            with pool.Fori(2, NC // 4, 1) as j:
                for q in range(4):
                    m_gather(j * 4 + q, q)
                    m_scatter(j * 4 + (q - M_LAG), q, j - 1)
            for k in range(4 * (NC // 4), NC + M_LAG):
                if k < NC:
                    m_gather(k, k % 4)
                m_scatter(k - M_LAG, k % 4, 0)
            for r in range(2):
                at_least(pool, M_sc[r], 64 * len(range(r, NC, 2)))

        @block.tensor
        def _(pe):
            T = nc.tensor
            pe.wait_ge(s_pool0, 2)

            def turn(dst, src, rows, cols):
                return T.transpose(dst, src, ident[0:rows, 0:rows])

            def summaries(n, wait_sem, v, done):
                pe.wait_ge(wait_sem, v)
                turn(bank[3][0:n, 0:NC], edge_c[:, 0:n], NC, n)
                turn(bank[3][0:n, 64:64 + NC], edge_c[:, 2:2 + n], NC, n).then_inc(done, 1)

            summaries(2, s_c, C_SUM, s_ct)
            pe.wait_ge(s_c, C_CARRY)
            turn(bank[3][0:NC, 128:130], carry_r[0:2, 0:NC], 2, NC).then_inc(s_ct, 1)
            pe.wait_ge(s_c, C_DINV)
            order = [s3_c[:, 0, :], s3_c[:, 1, :], last_c[:, :], s2_c[:, 0, :]]
            for a, what in enumerate(order):
                for k in range(TC):
                    mm = turn(bank[a % 4][0:R, k * NC:(k + 1) * NC], what[:, k * R:(k + 1) * R], NC, R)
                mm.then_inc(s_ct, 1)
            pe.wait_ge(s_c, C_INFO)
            pe.wait_ge(s_prep, PREP_TWO)
            for s in range(3):
                T.transpose(bank[s][:, 0:128], b_two[:, s, :], ident[:, :]).then_inc(s_bt, 1)

            pe.wait_ge(s_prep, PREP_ALL)
            rows_in = {0: x_in, 1: x1_r, 2: x3_r}

            def slot(m, u):
                a = unit(m, u + 1)
                if a.real:
                    if a.stage == 0 and not (isinstance(a.i, int) and a.i >= LAST):
                        pe.wait_ge([Cn["in0"], Cn["in1"]][a.par], (m + (u + 1) // 3 // 2) * 16 + 16
                                   if not isinstance(m, int) else 16 * (a.i // 2 + 1))
                    if a.stage == 1:
                        at_least(pe, Cn["rows"], a.n - 4 if not isinstance(a.n, int) or a.i >= 2 else 0)
                    if a.stage == 2:
                        at_least(pe, Cn["rows2"], a.i - 1)
                    at_least(pe, Cn["xT"], a.n)
                    for k in range(4):
                        mm = turn(bank[0][:, k * R:(k + 1) * R], rows_in[a.stage][a.par][:, 128 * k:128 * k + 128], R, 128)
                    mm.then_inc(Cn["rowsT"], 1)
                a = unit(m, u)
                if a.real:
                    pe.wait_ge(Cn["xT"], a.n + 1)
                    at_least(pe, Cn["hid"], a.n - 1)
                    T.matmul(pair[a.b2][:, 0, 0:CH], w_top[a.stage][:, :], xT[a.b3][:, :], start=True, stop=True)
                    T.matmul(pair[a.b2][:, 1, 0:CH], w_bot[a.stage][:, :], xT[a.b3][:, :], start=True, stop=True)\
                     .then_inc(Cn["up"], 1)
                a = unit(m, u - 2)
                if a.real:
                    pe.wait_ge(Cn["res"], a.n + 1)
                    at_least(pe, Cn["rows"], a.n - 1)
                    for k in range(4):
                        to, columns = bank[2 + a.b2][0:R, 128 * k:128 * k + 128], rT[a.b2][:, k * R:(k + 1) * R]
                        if a.stage == 0:
                            mm = T.matmul(to, columns, cmat[:, :], start=True, stop=True)
                        else:
                            mm = turn(to, columns, 128, R)
                    mm.then_inc(Cn["resT"], 1)
                a = unit(m, u - 1)
                if a.real:
                    pe.wait_ge(Cn["hid"], a.n + 1)
                    at_least(pe, Cn["res"], a.n)
                    T.matmul(bank[1][0:D, 0:CH], w_dn[a.stage][:, 0:D], hid[a.b2][:, 0, :], start=True, stop=True)
                    T.matmul(bank[1][D:128, 0:CH], w_dn[a.stage][:, 0:D], hid[a.b2][:, 1, :], start=True, stop=True)\
                     .then_inc(Cn["dn"], 1)

            node_slots(slot, pe, [(1, LAST // 2)], range(LAST // 2, MS))

            MT, XT, HT, OT, AT, UT = bank[0], bank[1], pair[0][:, 0, :], bank[2], bank[3], pair[0][:, 1, :]
            HT2 = pair[1][:, 0, :]
            XC = pair[1][:, 1, :]

            def tiles_to_cols(dst, src):
                for k in range(TC):
                    mm = turn(dst[:, k * R:(k + 1) * R], src[:, k * 128:(k + 1) * 128], R, 128)
                return mm

            def cols_to_tiles(dst, src):
                for k in range(TC):
                    mm = turn(dst[0:R, k * 128:(k + 1) * 128], src[:, k * R:(k + 1) * R], 128, R)
                return mm

            def down_rows(dst, h, w):
                for k in range(TC):
                    mm = T.matmul(dst[0:R, 128 * k:128 * k + 128], h[:, k * R:(k + 1) * R], w[:, :], start=True, stop=True)
                return mm

            pe.wait_ge(Cn["rows"], UNITS)
            pe.wait_ge(s_ones, N_ONES)

            def slot_a(at):
                if c := at(0):
                    k, q, h, p = c
                    at_least(pe, A_ld[q], h * 48 + 48)
                    at_least(pe, LA["xcol"], k)
                    tiles_to_cols(XT, l_a[q]).then_inc(LA["xdT"].sem, 1)
                if c := at(1):
                    k, q, h, p = c
                    at_least(pe, LA["msg"], k + 1)
                    at_least(pe, LA["agg"], k)
                    tiles_to_cols(MT, m_r[p]).then_inc(LA["msgT"].sem, 1)
                    at_least(pe, LA["xcol"], k + 1)
                    at_least(pe, LA["hid"], k)
                    T.matmul(HT[:, 0:CH], w_top[0][:, :], lxT[q][:, :], start=True, stop=True).then_inc(LA["up"].sem, 1)
                if c := at(2):
                    k, q, h, p = c
                    at_least(pe, LA["agg"], k + 1)
                    at_least(pe, LA["t2"], k)
                    for i in range(TC):
                        mm = T.matmul(AT[0:R, i * 128:(i + 1) * 128], agg[p][:, i * R:(i + 1) * R], cmat[:, :],
                                      start=True, stop=True)
                    mm.then_inc(LA["aggT"].sem, 1)
                    at_least(pe, LA["hid"], k + 1)
                    at_least(pe, LA["t1"], k)
                    down_rows(OT, lhid[p], w_dn[0]).then_inc(LA["dn"].sem, 1)
                    at_least(pe, LA["t4"], k)
                    down_rows(XC, lxT[q], x_up).then_inc(LA["xc"].sem, 1)
            lagged_slots(slot_a, pe, 5)
            at_least(pe, LA["rows"], NC)

            def slot_b(at):
                if c := at(3):
                    k, q, h, p = c
                    at_least(pe, LB["u"], k + 1)
                    at_least(pe, LB["ucol"], k)
                    tiles_to_cols(UT, u_r[p]).then_inc(LB["uT"].sem, 1)
                if c := at(1):
                    k, q, h, p = c
                    at_least(pe, LB["msg"], k + 1)
                    at_least(pe, LB["agg"], k)
                    tiles_to_cols(MT, m_r[p]).then_inc(LB["msgT"].sem, 1)
                if c := at(2):
                    k, q, h, p = c
                    at_least(pe, LB["agg"], k + 1)
                    at_least(pe, LB["t2"], k)
                    cols_to_tiles(AT, agg[p]).then_inc(LB["aggT"].sem, 1)
                if c := at(4):
                    k, q, h, p = c
                    at_least(pe, LB["hid"], k + 1)
                    at_least(pe, LB["rows"], k)
                    down_rows(OT, lhid[p], w_dn[1]).then_inc(LB["dn"].sem, 1)
                if c := at(3):
                    k, q, h, p = c
                    at_least(pe, LB["ucol"], k + 1)
                    at_least(pe, LB["hid"], k)
                    T.matmul(HT[:, 0:CH], w_top[1][:, :], lxT[p][:, :], start=True, stop=True).then_inc(LB["up"].sem, 1)
            lagged_slots(slot_b, pe, 5)
            at_least(pe, LB["rows"], NC)

            def slot_c(k, q, h, front, back):
                p = q % 2
                if front:
                    at_least(pe, LC["msg"], k + 1)
                    at_least(pe, LC["agg"], k)
                    tiles_to_cols(MT, m_r[p]).then_inc(LC["msgT"].sem, 1)
                    at_least(pe, LC["agg"], k + 1)
                    at_least(pe, LC["t2"], k)
                    cols_to_tiles(AT, agg[p]).then_inc(LC["aggT"].sem, 1)
            chunk_slots(slot_c, pe)
            at_least(pe, LC["rows"], NC)

            def slot_d(k, q, h, front, back):
                p = q % 2
                if front:
                    at_least(pe, LD["lky1"], k + 1)
                    at_least(pe, LD["lky2"], k + 1)
                    at_least(pe, LD["col"], k)
                    tiles_to_cols(MT, m_r[p]).then_inc(LD["lkyT"].sem, 1)
                if back:
                    kb, qb, hb, pb = before(k, q, h)
                    at_least(pe, LD["col"], kb + 1)
                    at_least(pe, LD["zc"], kb)
                    T.matmul(HT[0:128, 0:CH], gat_w[:, :], lxT[pb][:, :], start=True, stop=True).then_inc(LD["zx"].sem, 1)
            chunk_slots(slot_d, pe)
            summaries(1, LD["c"], D_SUM1, LD["ct"])
            pe.wait_ge(LD["c"], D_CARRY1)
            turn(bank[3][0:NC, 128:129], carry_r[0:1, 1:NC + 1], 1, NC).then_inc(LD["ct"], 1)
            summaries(1, LD["c"], D_SUM2, LD["ct"])
            pe.wait_ge(LD["c"], D_CARRY2)
            turn(bank[3][0:NC, 128:129], carry_r[0:1, 0:NC], 1, NC).then_inc(LD["ct"], 1)
            pe.wait_ge(LD["c"], D_ROWS)

            def slot_g(k, q, h, front, back):
                p = q % 2
                if front:
                    at_least(pe, LE["agg"], k + 1)
                    at_least(pe, LE["t1"], k)
                    cols_to_tiles(AT, agg[p]).then_inc(LE["aggT"].sem, 1)
            chunk_slots(slot_g, pe)
            at_least(pe, LE["rows"], NC)

            def slot_f(k, q, h, front, back):
                p = q % 2
                if front:
                    at_least(pe, LF["msg"], k + 1)
                    at_least(pe, LF["fill"], k)
                    tiles_to_cols(MT, m_r[p]).then_inc(LF["msgT"].sem, 1)
            chunk_slots(slot_f, pe)
            at_least(pe, LF["fill"], NC)

            def slot_m(k, q, h, front, back):
                p = q % 2
                if front:
                    at_least(pe, M_ga[q], h * 64 + 64)
                    at_least(pe, LG["scol"], k)
                    tiles_to_cols(MT, g_row[q]).then_inc(LG["srcT"].sem, 1)
                if back:
                    kb, qb, hb, pb = before(k, q, h)
                    at_least(pe, LG["agg"], kb + 1)
                    at_least(pe, LG["hid2"], kb)
                    T.matmul(HT2[:, 0:CH], w_upd[:, :], l_up[qb][:, :], start=True, stop=True).then_inc(LG["up2"].sem, 1)
                if front:
                    at_least(pe, M_ld[q], h * 80 + 80)
                    at_least(pe, LG["scol"], k + 1)
                    at_least(pe, LG["hid"], k)
                    T.matmul(HT[:, 0:CH], w_msg[:, :], l_in[q][:, :], start=True, stop=False)
                    T.matmul(HT[:, 0:CH], w_edge[:, :], l_ea[q][:, :], start=False, stop=True).then_inc(LG["up"].sem, 1)
                if back:
                    at_least(pe, LG["hid2"], kb + 1)
                    at_least(pe, LG["t1"], kb)
                    down_rows(OT, lhid2[pb], w_dn[2]).then_inc(LG["dn2"].sem, 1)
                if front:
                    at_least(pe, LG["hid"], k + 1)
                    at_least(pe, LG["msg"], k)
                    T.matmul(XT[0:D, 0:CH], w_msg2[:, :], lhid[p][:, :], start=True, stop=True).then_inc(LG["dn"].sem, 1)
            chunk_slots(slot_m, pe)

        @block.scalar
        def _(act):
            A = nc.scalar
            act.wait_ge(s_set, N_SET)
            act.wait_ge(s_c, C_DD)
            A.activation(s3_c[:, :, :], s2_c[:, :, :], ACT.Sqrt).then_inc(s_ca, 1)
            act.wait_ge(s_w, ALL_W)
            act.wait_ge(s_prep, PREP_ALL)

            def root(dst, src):
                return A.activation(dst, src, ACT.Sqrt, bias=eps[0:R, :], scale=1.0 / D)

            def slot(m, u):
                a = unit(m, u + 1)
                if a.real:
                    act.wait_ge(Cn["rowsT"], a.n + 1)
                    at_least(act, Cn["res"], a.n - 2)
                    A.activation(xT[a.b3][:, :], bank[0][:, 0:CH], ACT.Copy).then_inc(Cn["xT"], 1)
                a = unit(m, u - 5)
                if a.real and a.stage == 1:
                    act.wait_ge(Cn["ssum2"], a.i + 1)
                    at_least(act, Cn["rstd2"], a.i)
                    root(sd_b[:, :], ss_b[:, :]).then_inc(Cn["std2"], 1)
                a = unit(m, u - 3)
                if a.real:
                    at_least(act, Cn["rstd"], a.n - 1)
                    act.wait_ge(Cn["ssum"], a.n + 1)
                    root(sd[a.b2][:, :], ss[a.b2][:, :]).then_inc(Cn["std"], 1)
                a = unit(m, u)
                if a.real:
                    act.wait_ge(Cn["up"], a.n + 1)
                    at_least(act, Cn["dn"], a.n - 1)
                    A.activation(hid[a.b2][:, :, :], pair[a.b2][:, :, 0:CH], ACT.Relu,
                                 bias=b_up[:, a.stage:a.stage + 1]).then_inc(Cn["hid"], 1)
                a = unit(m, u - 2)
                if a.real:
                    at_least(act, Cn["ssum"], a.n - 1)
                    act.wait_ge(Cn["resT"], a.n + 1)
                    A.activation(sq[a.b2][:, :], bank[2 + a.b2][0:R, :], ACT.Square).then_inc(Cn["sq"], 1)
                a = unit(m, u - 3)
                if a.real and a.stage == 1:
                    act.wait_ge(Cn["y"], a.i + 1)
                    at_least(act, Cn["ssum2"], a.i)
                    A.activation(sq_b[:, :], y_r[:, :], ACT.Square).then_inc(Cn["sq2"], 1)

            node_slots(slot, act, [(1, MS - 1)], [MS - 1])

            MT, XT, HT, OT, AT, UT = bank[0], bank[1], pair[0][:, 0, :], bank[2], bank[3], pair[0][:, 1, :]
            HT2 = pair[1][:, 0, :]

            def norm(S, kb):
                at_least(act, S["t5"] if S is LC else S["t3"] if S is LE else S["t2"], kb + 1)
                at_least(act, S["ssum"], kb)
                A.activation(lsq[:, :], w_r[:, :], ACT.Square).then_inc(S["sq"].sem, 1)
                at_least(act, S["ssum"], kb + 1)
                at_least(act, S["rstd"], kb)
                root(lsd[:, :], lss[:, :]).then_inc(S["std"].sem, 1)

            def slot_a(at):
                if c := at(1):
                    k, q, h, p = c
                    at_least(act, LA["up"], k + 1)
                    at_least(act, LA["dn"], k - 1)
                    A.activation(lhid[p][:, :], HT[:, 0:CH], ACT.Relu, bias=b_up[:, 0:1]).then_inc(LA["hid"].sem, 1)
                if c := at(4):
                    k, q, h, p = c
                    at_least(act, LA["ssum"], k + 1)
                    at_least(act, LA["rstd"], k)
                    root(lsd[:, :], lss[:, :]).then_inc(LA["std"].sem, 1)
                if c := at(0):
                    k, q, h, p = c
                    at_least(act, LA["xdT"], k + 1)
                    at_least(act, LA["xc"], k - 3)
                    A.activation(lxT[q][0:D, :], XT[0:D, 0:CH], ACT.Copy).then_inc(LA["xcol"].sem, 1)
                if c := at(3):
                    k, q, h, p = c
                    at_least(act, LA["t4"], k + 1)
                    at_least(act, LA["ssum"], k)
                    A.activation(lsq[:, :], w_rs[p][:, :], ACT.Square).then_inc(LA["sq"].sem, 1)
            act.wait_ge(s_ones, N_ONES)
            lagged_slots(slot_a, act, 5)

            def slot_b(at):
                if c := at(3):
                    k, q, h, p = c
                    at_least(act, LB["uT"], k + 1)
                    at_least(act, LB["up"], k - 1)
                    A.activation(lxT[p][0:D, :], UT[0:D, 0:CH], ACT.Copy).then_inc(LB["ucol"].sem, 1)
                if c := at(4):
                    k, q, h, p = c
                    at_least(act, LB["dn"], k + 1)
                    at_least(act, B_st[q], h * 16)
                    A.activation(n_r[q][:, :].rearrange("p (k f) -> p k f", f=D),
                                 OT[0:R, :].rearrange("p (k f) -> p k f", f=128)[:, :, 0:D], ACT.Copy)\
                     .then_inc(LB["rows"].sem, 1)
                if c := at(3):
                    k, q, h, p = c
                    at_least(act, LB["up"], k + 1)
                    at_least(act, LB["dn"], k - 1)
                    A.activation(lhid[p][:, :], HT[:, 0:CH], ACT.Relu, bias=b_up[:, 1:2]).then_inc(LB["hid"].sem, 1)
            at_least(act, LA["rows"], NC)
            all_stored(act, A_st)
            lagged_slots(slot_b, act, 5)

            def slot_c(k, q, h, front, back):
                if back:
                    norm(LC, before(k, q, h)[0])
            chunk_slots(slot_c, act)

            def slot_d(k, q, h, front, back):
                p = q % 2
                if front:
                    at_least(act, LD["lkyT"], k + 1)
                    at_least(act, LD["zx"], k - 1)
                    A.activation(lxT[p][:, :], MT[:, 0:CH], ACT.Copy).then_inc(LD["col"].sem, 1)
                if back:
                    kb, qb, hb, pb = before(k, q, h)
                    at_least(act, LD["zx"], kb + 1)
                    if isinstance(kb, int):
                        at_least(act, D_st[pb], 16 * (kb // 2))
                    else:
                        at_least(act, D_st[pb], hb * 32 + (qb // 2) * 16)
                    A.activation(zx[pb][:, :], HT[0:D + 2, 0:CH], ACT.Copy).then_inc(LD["zc"].sem, 1)
            at_least(act, LC["rows"], NC)
            chunk_slots(slot_d, act)
            act.wait_ge(LD["c"], D_EXP)
            A.activation(s2_c[:, :, :], s3_c[:, :, :], ACT.Exp).then_inc(LD["ca"], 1)

            def slot_g(k, q, h, front, back):
                if back:
                    norm(LE, before(k, q, h)[0])
            chunk_slots(slot_g, act)

            def slot_m(k, q, h, front, back):
                p = q % 2
                if front:
                    at_least(act, LG["srcT"], k + 1)
                    at_least(act, LG["up"], k - 3)
                    A.activation(l_in[q][0:D, :], MT[0:D, 0:CH], ACT.Copy).then_inc(LG["scol"].sem, 1)
                if back:
                    kb, qb, hb, pb = before(k, q, h)
                    at_least(act, LG["up2"], kb + 1)
                    at_least(act, LG["dn2"], kb - 1)
                    A.activation(lhid2[pb][:, :], HT2[:, 0:CH], ACT.Relu, bias=b_up[:, 2:3]).then_inc(LG["hid2"].sem, 1)
                if front:
                    at_least(act, LG["up"], k + 1)
                    at_least(act, LG["dn"], k - 1)
                    A.activation(lhid[p][:, :], HT[:, 0:CH], ACT.Relu, bias=b_msg[:, :]).then_inc(LG["hid"].sem, 1)
                    at_least(act, LG["dn"], k + 1)
                    at_least(act, LG["agg"], k - 3)
                    A.activation(l_m[q][0:D, :], XT[0:D, 0:CH], ACT.Identity, bias=b_msg2[:, :]).then_inc(LG["msg"].sem, 1)
                if back:
                    norm(LG, kb)
            at_least(act, LE["rows"], NC)
            at_least(act, LF["fill"], NC)
            chunk_slots(slot_m, act)

        @block.vector
        def _(dve):
            V = nc.vector
            c = [0, 0]

            def step(ins):
                c[0] += 1
                ins.then_inc(s_c, 1)
                dve.wait_ge(s_c, c[0])

            def prep(ins):
                c[1] += 1
                ins.then_inc(s_prep, 1)
                dve.wait_ge(s_prep, c[1])

            V.memset(dst_c[:, :], -1).then_inc(s_pad, 1)
            zeroed = [w_top[s] for s in range(3)] + [w_bot[s] for s in range(3)] + [w_dn[s] for s in range(3)] \
                + [gat_w, w_edge]
            for w in zeroed:
                V.memset(w[:, :], 0.0).then_inc(s_set, 1)
            V.memset(eps[:, :], EPS).then_inc(s_set, 1)
            V.memset(info_fill, 1.0).then_inc(s_ones, 1)
            dve.wait_ge(s_ones, 1)
            V.memset(info_fill.rearrange("p (a c) -> p a c", c=4)[:, :, 0:1], -1.0).then_inc(s_set, 1)

            dve.wait_ge(s_e, ALL_E)
            V.memset(one_c[:, :], 1.0).then_inc(s_c, 1)
            c[0] += 1
            step(V.tensor_copy(dstf_c[:, :], dst_c[:, :]))
            V.tensor_tensor(keep_c[:, :], dstf_c[:, 0:CH], dstf_c[:, 1:CH + 1], ALU.is_equal).then_inc(s_c, 1)
            V.tensor_tensor(on_c[:, :], dstf_c[:, 1:CH + 1], dstf_c[:, 2:CH + 2], ALU.is_equal).then_inc(s_c, 1)
            c[0] += 2
            dve.wait_ge(s_c, c[0])
            assert c[0] == C_ROWS
            step(V.tensor_scalar(last_c[:, :], on_c[:, :], -1.0, 1.0, ALU.mult, ALU.add))
            V.tensor_tensor_scan(s1_c[:, 0, :], keep_c[:, :], one_c[:, :], 0.0, ALU.mult, ALU.add).then_inc(s_c, 1)
            V.tensor_tensor_scan(s1_c[:, 1, :], keep_c[:, :], ew_c[:, :], 0.0, ALU.mult, ALU.add).then_inc(s_c, 1)
            V.tensor_reduce(edge_c[:, 0:1], keep_c[:, :], AX_X, ALU.min).then_inc(s_c, 1)
            V.tensor_reduce(edge_c[:, 1:2], keep_c[:, :], AX_X, ALU.min).then_inc(s_c, 1)
            c[0] += 4
            dve.wait_ge(s_c, c[0])
            step(V.tensor_copy(edge_c[:, 2:4], s1_c[:, :, CH - 1]))
            assert c[0] == C_SUM
            dve.wait_ge(s_ct, 1)
            step(V.tensor_copy(top[:, :, 0:NC], bank[3][0:2, 0:128].rearrange("p (a b) -> p a b", a=2)[:, :, 0:NC]))
            step(V.memset(carry_r[:, :], 0.0))
            step(V.tensor_tensor_scan(carry_r[0:2, 1:NC + 1], top[:, 0, 0:NC], top[:, 1, 0:NC], 0.0, ALU.mult, ALU.add))
            assert c[0] == C_CARRY
            dve.wait_ge(s_ct, 2)
            step(V.tensor_copy(carry_c[:, :], bank[3][0:NC, 128:130]))
            V.tensor_tensor_scan(s1_c[:, 0, :], keep_c[:, :], one_c[:, :], carry_c[:, 0:1], ALU.mult, ALU.add).then_inc(s_c, 1)
            V.tensor_tensor_scan(s1_c[:, 1, :], keep_c[:, :], ew_c[:, :], carry_c[:, 1:2], ALU.mult, ALU.add).then_inc(s_c, 1)
            c[0] += 2
            dve.wait_ge(s_c, c[0])
            step(V.tensor_scalar(s1_c[:, :, :], s1_c[:, :, :], 1.0, None, ALU.add))
            step(V.tensor_scalar(s2_c[:, :, :], s1_c[:, :, :], 1e-30, None, ALU.max))
            assert c[0] == C_DD
            dve.wait_ge(s_ca, 1)
            step(V.reciprocal(s3_c[:, :, :], s3_c[:, :, :]))
            step(V.tensor_scalar(s1_c[:, :, :], s1_c[:, :, :], 0.0, None, ALU.is_gt))
            step(V.tensor_tensor(s3_c[:, :, :], s3_c[:, :, :], s1_c[:, :, :], ALU.mult))
            step(V.tensor_scalar(s2_c[:, 0, :], on_c[:, :], FAR, None, ALU.mult))
            step(V.tensor_tensor(s2_c[:, 0, :], s2_c[:, 0, :], dstf_c[:, 1:CH + 1], ALU.add))
            assert c[0] == C_DINV

            def tiled(a):
                return bank[a][0:R, 0:NT].rearrange("p (k c) -> p c k", k=TC)

            def in_tiles(ap):
                return ap.rearrange("p (c k) -> p c k", k=TC)

            dve.wait_ge(s_ct, 6)
            dve.wait_ge(s_pool0, 4)
            V.tensor_copy(in_tiles(d0_t[:, :]), tiled(0)).then_inc(s_c, 1)
            V.tensor_copy(in_tiles(d1_t[:, :]), tiled(1)).then_inc(s_c, 1)
            V.tensor_copy(in_tiles(last_t[:, :]), tiled(2)).then_inc(s_c, 1)
            V.tensor_copy(in_tiles(sidx[:, :]), tiled(3)).then_inc(s_c, 1)
            V.tensor_copy(info_r[:, :, 0], slot_id[:, :]).then_inc(s_c, 1)
            V.memset(info_r[:, :, 3], 0.0).then_inc(s_c, 1)
            c[0] += 6
            dve.wait_ge(s_c, c[0])
            V.tensor_copy(info_r[:, :, 1], d0_t[:, :]).then_inc(s_c, 1)
            V.tensor_copy(info_r[:, :, 2], d1_t[:, :]).then_inc(s_c, 1)
            c[0] += 2
            assert c[0] == C_INFO

            dve.wait_ge(s_w, ALL_W)

            def centre(view, n, width, m):
                prep(V.tensor_reduce(m, view, AX_X, ALU.add))
                prep(V.tensor_scalar(m, m, -1.0 / width, None, ALU.mult))
                prep(V.tensor_tensor(view, view, m.unsqueeze(2).to_broadcast([128, n, width]), ALU.add))

            centre(b_row[:, :, :], 4, D, mean6[:, 0:4])
            for s in range(3):
                centre(w_dn[s][:, 0:D].unsqueeze(1), 1, D, mean6[:, 4 + s:5 + s])
            prep(V.memset(cmat[:, :], 0.0))
            for half_of in (slice(0, D), slice(D, 128)):
                prep(V.memset(cmat[half_of, half_of], -1.0 / D))
            dve.wait_ge(s_pool0, 2)
            prep(V.tensor_tensor(cmat[:, :], cmat[:, :], ident[:, :], ALU.add))
            prep(V.memset(x_up[:, :], 0.0))
            prep(V.tensor_copy(x_up[0:D, 0:D], cmat[0:D, 0:D]))
            prep(V.tensor_copy(x_up[D:D + 1, 0:D], b_row[D:D + 1, 0, :]))
            prep(V.tensor_tensor(gat_tmp[:, :], gat_raw[:, :], gat_att[:, :], ALU.mult))
            prep(V.tensor_reduce(gat_w[0:D, D:D + 1], gat_tmp[0:D, :], AX_X, ALU.add))
            prep(V.tensor_reduce(gat_w[D:128, D + 1:D + 2], gat_tmp[D:128, :], AX_X, ALU.add))
            centre(gat_raw[:, :].unsqueeze(1), 1, D, mean6[:, 7:8])
            prep(V.tensor_copy(gat_w[0:D, 0:D], gat_raw[0:D, :]))
            for s, i in enumerate((0, 1, 3)):
                prep(V.tensor_copy(b_two[:, s, 0:D], b_row[:, i, :]))
                prep(V.tensor_copy(b_two[:, s, D:128], b_row[:, i, :]))
            assert c[1] == PREP_TWO
            dve.wait_ge(s_bt, 3)
            for s in range(3):
                prep(V.tensor_copy(b_dn[:, s:s + 1], bank[s][:, 0:1]))
            for i in (0, 1):
                V.memset(x1_r[i][:, :], 0.0).then_inc(s_prep, 1)
                V.memset(x3_r[i][:, :], 0.0).then_inc(s_prep, 1)
                c[1] += 2
            assert c[1] == PREP_ALL

            iso_sem0, iso_sem1 = [Cn["s0st0"], Cn["s0st1"]], [Cn["s1st0"], Cn["s1st1"]]

            def pR(a):
                return bank[2 + a.b2][0:R, :]

            def slot_of(mode):
                def slot(m, u):
                    known = mode is None

                    def iso0(i):
                        return NB <= i < LAST if known else mode == "iso"

                    def iso1(i):
                        return NB + 2 <= i < LAST + 2 if known else mode == "iso"

                    def half_after(i, q, first):
                        return (i - 2 - first) // 2 + 1 if known else m + (q - (first + 2 - first % 2) // 2 + 1 - 0)

                    a = unit(m, u - 3)
                    if a.real:
                        dve.wait_ge(Cn["sq"], a.n + 1)
                        at_least(dve, Cn["std"], a.n - 1)
                        V.tensor_reduce(ss[a.b2][:, :], n_view(sq[a.b2][:, :]), AX_X, ALU.add).then_inc(Cn["ssum"], 1)
                    at_m = m + (u - 3) // 3 // 2
                    if a.real and a.stage == 0 and iso0(a.i):
                        if not known or a.i - 2 >= NB:
                            v = 32 * ((a.i - 2 - NB) // 2 + 1) if known else (at_m - NB // 2) * 32
                            dve.wait_ge(iso_sem0[a.par], v)
                        V.tensor_tensor(h0_r[a.par][:, :], pR(a), x_in[a.par][:, :], ALU.subtract).then_inc(Cn["h0"], 1)
                        dve.wait_ge(Cn["h0"], a.i - NB + 1)
                        V.tensor_tensor(n_view(h0_r[a.par][:, :]), n_view(h0_r[a.par][:, :]), row_bias(0, TB),
                                        ALU.subtract).then_inc(Cn["h0b"], 1)
                    at_m = m + (u - 3) // 3 // 2
                    if a.real and a.stage == 1 and iso1(a.i):
                        if not known or a.i - 2 >= NB + 2:
                            v = 48 * ((a.i - 2 - NB - 2) // 2 + 1) if known else (at_m - NB // 2 - 1) * 48
                            dve.wait_ge(iso_sem1[a.par], v)
                        V.tensor_tensor(h2_r[a.par][:, :], pR(a), x1_r[a.par][:, :], ALU.subtract).then_inc(Cn["h2"], 1)
                        dve.wait_ge(Cn["h2"], a.i - NB - 1)
                        V.tensor_tensor(n_view(h2_r[a.par][:, :]), n_view(h2_r[a.par][:, :]), row_bias(1, TB),
                                        ALU.subtract).then_inc(Cn["h2b"], 1)
                    a = unit(m, u - 4)
                    if a.real and a.stage == 1:
                        dve.wait_ge(Cn["sq2"], a.i + 1)
                        at_least(dve, Cn["std2"], a.i)
                        V.tensor_reduce(ss_b[:, :], n_view(sq_b[:, :]), AX_X, ALU.add).then_inc(Cn["ssum2"], 1)
                    a = unit(m, u - 5)
                    if a.real and a.stage == 1:
                        dve.wait_ge(Cn["std2"], a.i + 1)
                        V.reciprocal(rs_b[:, :], sd_b[:, :]).then_inc(Cn["rstd2"], 1)
                        dve.wait_ge(Cn["rstd2"], a.i + 1)
                        if not known or a.i >= 2:
                            dve.wait_ge(Cn["rowsT"], a.n + 3)
                        at_m = m + (u - 5) // 3 // 2
                        if (known and NB + 2 <= a.i - 2 < LAST + 2) or mode == "iso":
                            v = 48 * ((a.i - 2 - NB - 2) // 2 + 1) if known else (at_m - NB // 2 - 1) * 48
                            dve.wait_ge(iso_sem1[a.par], v)
                        V.tensor_tensor(n_view(x3_r[a.par][:, :]), n_view(y_r[:, :]), spread(rs_b[:, :], TB), ALU.mult)\
                         .then_inc(Cn["rows2"], 1)
                    a = unit(m, u - 3)
                    if a.real:
                        qq = (u - 3) // 3 // 2
                        at_m = m + qq
                        dve.wait_ge(Cn["std"], a.n + 1)
                        V.reciprocal(rs[:, :], sd[a.b2][:, :]).then_inc(Cn["rstd"], 1)
                        dve.wait_ge(Cn["rstd"], a.n + 1)
                        dst = {0: x1_r, 1: x2_r, 2: x4_r}[a.stage][a.par]
                        if a.stage == 0:
                            if not known or a.i >= 2:
                                dve.wait_ge(Cn["rowsT"], a.n)
                            if (known and NB <= a.i - 2 < LAST) or mode == "iso":
                                v = 32 * ((a.i - 2 - NB) // 2 + 1) if known else (at_m - NB // 2) * 32
                                dve.wait_ge(iso_sem0[a.par], v)
                        if a.stage == 1:
                            if (known and NB + 2 <= a.i - 2 < LAST + 2) or mode == "iso":
                                v = 48 * ((a.i - 2 - NB - 2) // 2 + 1) if known else (at_m - NB // 2 - 1) * 48
                                dve.wait_ge(iso_sem1[a.par], v)
                        if a.stage == 2:
                            if (known and 4 <= a.i - 2 < NB + 4) or mode == "dense":
                                v = 16 * ((a.i - 6) // 2 + 1) if known else (at_m - 2) * 16
                                dve.wait_ge([Cn["out0"], Cn["out1"]][a.par], v)
                        V.tensor_tensor(n_view(dst[:, :]), n_view(pR(a)), spread(rs[:, :], TB), ALU.mult)\
                         .then_inc(Cn["rows"], 1)
                        if a.stage == 1:
                            dve.wait_ge(Cn["rows"], a.n + 1)
                            at_least(dve, Cn["rows2"], a.i)
                            V.tensor_tensor(n_view(y_r[:, :]), n_view(x2_r[a.par][:, :]), row_bias(2, TB), ALU.add)\
                             .then_inc(Cn["y"], 1)
                    a = unit(m, u - 1)
                    if a.real:
                        dve.wait_ge(Cn["dn"], a.n + 1)
                        at_least(dve, Cn["resT"], a.n - 1)
                        V.scalar_tensor_tensor(rT[a.b2][:, :], bank[1][:, 0:CH], b_dn[:, a.stage:a.stage + 1],
                                               xT[a.b3][:, :], ALU.add, ALU.add).then_inc(Cn["res"], 1)
                return slot

            def run(mode, lo, hi):
                s = slot_of(mode)
                with dve.Fori(lo, hi, 1) as m:
                    for u in range(6):
                        s(m, u)

            known = slot_of(None)
            known(0, -1)
            for m in range(0, 4):
                for u in range(6):
                    known(m, u)
            run("dense", 4, NB // 2)
            for m in range(NB // 2, NB // 2 + 4):
                for u in range(6):
                    known(m, u)
            run("iso", NB // 2 + 4, LAST // 2)
            for m in range(LAST // 2, MS):
                for u in range(6):
                    known(m, u)
            for u in range(5):
                known(MS, u)

            dve.wait_ge(P["copied"], 5 * NI)
            step(V.tensor_scalar(gfl[:, :], info_r[:, :, 0], 0.0, None, ALU.is_ge))
            step(V.tensor_tensor(w0_t[:, :], info_r[:, :, 0], gbase[:, :], ALU.subtract))
            step(V.tensor_tensor(w0_t[:, :], w0_t[:, :], gfl[:, :], ALU.mult))
            step(V.tensor_tensor(gidx[:, :], w0_t[:, :], gbase[:, :], ALU.add))
            step(V.tensor_copy(w0_t[:, :], info_r[:, :, 1]))
            step(V.tensor_tensor(w1_t[:, :], info_r[:, :, 2], ew_t[:, :], ALU.mult))
            assert c[0] == C_ALL
            for i in range(4):
                V.memset(lxT[i][:, :], 0.0).then_inc(s_ones, 1)
                dve.wait_ge(s_ones, 2 + i * 2)
                V.memset(lxT[i][D:D + 1, :], 1.0).then_inc(s_ones, 1)
            for r in range(2):
                dve.wait_ge(iso_sem0[r], 32 * len(range(r, NI, 2)))
                dve.wait_ge(iso_sem1[r], 48 * len(range(r, NI, 2)))
            for buf in l_ea + l_a + g_row + m_r + u_r + agg:
                V.memset(buf[:, :], 0.0).then_inc(s_ones, 1)

            dve.wait_ge(s_ones, N_ONES)

            def v4(ap):
                return ap.rearrange("p (k f) -> p k f", f=D)

            def tile_scalar(tt, k):
                return tt[:, bass.ds(k * TC, TC)].unsqueeze(2).to_broadcast([R, TC, D])

            def finish(S, kb, qb, hb, val, st):
                at_least(dve, S["sq"], kb + 1)
                V.tensor_reduce(lss[:, :], v4(lsq[:, :]), AX_X, ALU.add).then_inc(S["ssum"].sem, 1)
                at_least(dve, S["std"], kb + 1)
                V.reciprocal(lrs[:, :], lsd[:, :]).then_inc(S["rstd"].sem, 1)
                at_least(dve, S["rstd"], kb + 1)
                if st is not None:
                    at_least(dve, st[qb], hb * 16)
                V.tensor_tensor(v4(n_r[qb][:, :]), v4(val), spread(lrs[:, :], TC), ALU.mult).then_inc(S["rows"].sem, 1)

            def scan(S, k, q, data, width, name_done, first, msg_sem):
                at_least(dve, msg_sem, k + 1)
                init = 0.0 if first else agg[(q - 1) % 2][0:width, CH - 1:CH]
                V.tensor_tensor_scan(agg[q % 2][0:width, :], l_k[q][0:width, :], data, init,
                                     ALU.mult, ALU.add).then_inc(name_done.sem, 1)

            MT, XT, OT, AT = bank[0], bank[1], bank[2], bank[3]
            OTv = OT[0:R, :].rearrange("p (k f) -> p k f", f=128)[:, :, 0:D]
            ATv = AT[0:R, :].rearrange("p (k f) -> p k f", f=128)[:, :, 0:D]

            XCv = pair[1][0:R, 1, :].rearrange("p (k f) -> p k f", f=128)[:, :, 0:D]

            def slot_a(at):
                if c := at(1):
                    k, q, h, p = c
                    at_least(dve, LA["aggT"], k - 1)
                    scan(LA, k, q, MT[0:D, 0:CH], D, LA["agg"], isinstance(k, int) and k == 0, LA["msgT"])
                if c := at(3):
                    k, q, h, p = c
                    at_least(dve, LA["t4"], k)
                    at_least(dve, LA["dn"], k + 1)
                    V.tensor_tensor(v4(v_r[:, :]), OTv, tile_scalar(d0_t, k), ALU.mult).then_inc(LA["t1"].sem, 1)
                if c := at(4):
                    k, q, h, p = c
                    at_least(dve, LA["sq"], k + 1)
                    V.tensor_reduce(lss[:, :], v4(lsq[:, :]), AX_X, ALU.add).then_inc(LA["ssum"].sem, 1)
                if c := at(3):
                    k, q, h, p = c
                    at_least(dve, LA["t1"], k + 1)
                    at_least(dve, LA["aggT"], k + 1)
                    V.tensor_tensor(v4(v_r[:, :]), v4(v_r[:, :]), ATv, ALU.add).then_inc(LA["t2"].sem, 1)
                if c := at(0):
                    k, q, h, p = c
                    at_least(dve, A_ld[q], h * 48 + 48)
                    at_least(dve, LA["msgT"], k - 1)
                    V.tensor_tensor(half(m_r[p]), v4(l_src[q][:, :]), tile_scalar(w0_t, k), ALU.mult)\
                     .then_inc(LA["msg"].sem, 1)
                if c := at(3):
                    k, q, h, p = c
                    at_least(dve, LA["t2"], k + 1)
                    V.tensor_tensor(v4(v_r[:, :]), v4(v_r[:, :]), tile_scalar(d0_t, k), ALU.mult).then_inc(LA["t3"].sem, 1)
                if c := at(4):
                    k, q, h, p = c
                    at_least(dve, LA["std"], k + 1)
                    V.reciprocal(lrs[:, :], lsd[:, :]).then_inc(LA["rstd"].sem, 1)
                if c := at(3):
                    k, q, h, p = c
                    at_least(dve, LA["t3"], k + 1)
                    at_least(dve, LA["xc"], k + 1)
                    at_least(dve, LA["rows"], k - 1)
                    V.tensor_tensor(v4(w_rs[p][:, :]), v4(v_r[:, :]), XCv, ALU.add).then_inc(LA["t4"].sem, 1)
                if c := at(4):
                    k, q, h, p = c
                    at_least(dve, LA["rstd"], k + 1)
                    at_least(dve, A_st[q], h * 16)
                    V.tensor_tensor(v4(n_r[q][:, :]), v4(w_rs[p][:, :]), spread(lrs[:, :], TC), ALU.mult)\
                     .then_inc(LA["rows"].sem, 1)
            lagged_slots(slot_a, dve, 5)

            def slot_b(at):
                if c := at(1):
                    k, q, h, p = c
                    at_least(dve, B_ld[q], h * 32 + 32)
                    at_least(dve, LB["aggT"], k - 1)
                    scan(LB, k, q, MT[0:D, 0:CH], D, LB["agg"], isinstance(k, int) and k == 0, LB["msgT"])
                if c := at(2):
                    k, q, h, p = c
                    at_least(dve, LB["u"], k)
                    V.tensor_tensor(v4(v_r[:, :]), half(l_a[q]), tile_scalar(d1_t, k), ALU.mult).then_inc(LB["t1"].sem, 1)
                    at_least(dve, LB["t1"], k + 1)
                    at_least(dve, LB["aggT"], k + 1)
                    V.tensor_tensor(v4(v_r[:, :]), v4(v_r[:, :]), ATv, ALU.add).then_inc(LB["t2"].sem, 1)
                if c := at(0):
                    k, q, h, p = c
                    at_least(dve, B_ga[q], h * 64 + 64)
                    at_least(dve, LB["msgT"], k - 1)
                    V.tensor_tensor(half(m_r[p]), half(g_row[q]), tile_scalar(w1_t, k), ALU.mult)\
                     .then_inc(LB["msg"].sem, 1)
                if c := at(2):
                    k, q, h, p = c
                    at_least(dve, LB["t2"], k + 1)
                    at_least(dve, LB["uT"], k - 1)
                    V.tensor_tensor(half(u_r[p]), v4(v_r[:, :]), tile_scalar(d1_t, k), ALU.mult).then_inc(LB["u"].sem, 1)
            at_least(dve, LA["rows"], NC)
            lagged_slots(slot_b, dve, 5)
            at_least(dve, LB["rows"], NC)
            all_stored(dve, B_st)

            def slot_c(k, q, h, front, back):
                p = q % 2
                if front:
                    at_least(dve, C_ga[q], h * 64 + 64)
                    at_least(dve, LC["msgT"], k - 1)
                    V.tensor_tensor(half(m_r[p]), half(g_row[q]), tile_scalar(w1_t, k), ALU.mult)\
                     .then_inc(LC["msg"].sem, 1)
                    at_least(dve, C_ld[q], h * 48 + 48)
                if back:
                    kb, qb, hb, pb = before(k, q, h)
                    V.tensor_tensor(v4(v_r[:, :]), half(l_a[qb]), tile_scalar(d1_t, kb), ALU.mult).then_inc(LC["t1"].sem, 1)
                    at_least(dve, LC["t1"], kb + 1)
                    at_least(dve, LC["aggT"], kb + 1)
                    at_least(dve, LC["rows"], kb)
                    V.tensor_tensor(v4(w_r[:, :]), v4(v_r[:, :]), ATv, ALU.add).then_inc(LC["t2"].sem, 1)
                    at_least(dve, LC["t2"], kb + 1)
                    V.tensor_tensor(v4(v_r[:, :]), v4(w_r[:, :]), tile_scalar(d1_t, kb), ALU.mult).then_inc(LC["t3"].sem, 1)
                    at_least(dve, LC["t3"], kb + 1)
                    V.tensor_tensor(w_r[:, :], v_r[:, :], l_b[qb][:, :], ALU.add).then_inc(LC["t4"].sem, 1)
                    at_least(dve, LC["t4"], kb + 1)
                    V.tensor_tensor(v4(w_r[:, :]), v4(w_r[:, :]), row_bias(1, TC), ALU.add).then_inc(LC["t5"].sem, 1)
                if front:
                    at_least(dve, LC["aggT"], k - 1)
                    scan(LC, k, q, MT[0:D, 0:CH], D, LC["agg"], isinstance(k, int) and k == 0, LC["msgT"])
                if back:
                    finish(LC, kb, qb, hb, w_r[:, :], C_st)
            chunk_slots(slot_c, dve)
            at_least(dve, LC["rows"], NC)

            def slot_d(k, q, h, front, back):
                p = q % 2
                if front:
                    mv = m_r[p][:, :].rearrange("p (k f) -> p k f", f=128)
                    at_least(dve, D_ga[q], h * 64 + 64)
                    at_least(dve, LD["lkyT"], k - 1)
                    V.scalar_tensor_tensor(mv[:, :, 0:D], half(g_row[q]), 0.2, half(g_row[q]),
                                           ALU.mult, ALU.max).then_inc(LD["lky1"].sem, 1)
                    at_least(dve, D_ld[q], h * 16 + 16)
                    V.scalar_tensor_tensor(mv[:, :, D:128], half(l_a[q]), 0.2, half(l_a[q]),
                                           ALU.mult, ALU.max).then_inc(LD["lky2"].sem, 1)
            chunk_slots(slot_d, dve)

            dc = [0]

            def dstep(ins):
                dc[0] += 1
                ins.then_inc(LD["c"], 1)
                dve.wait_ge(LD["c"], dc[0])

            dve.wait_ge(s_rows, 64)
            el, er, s3a, s3b = s1_c[:, 0, :], s1_c[:, 1, :], s3_c[:, 0, :], s3_c[:, 1, :]
            dstep(V.tensor_tensor(er, er, last_c[:, :], ALU.mult))
            dstep(V.tensor_tensor_scan(s3a[:, ::-1], on_c[:, ::-1], er[:, ::-1], 0.0, ALU.mult, ALU.add))
            dstep(V.tensor_reduce(edge_c[:, 0:1], on_c[:, :], AX_X, ALU.min))
            dstep(V.tensor_copy(edge_c[:, 2:3], s3a[:, 0:1]))
            assert dc[0] == D_SUM1
            dve.wait_ge(LD["ct"], 1)
            dstep(V.tensor_copy(top[0:1, :, 0:NC], bank[3][0:1, 0:128].rearrange("p (a b) -> p a b", a=2)[:, :, 0:NC]))
            dstep(V.memset(carry_r[:, :], 0.0))
            dstep(V.tensor_tensor_scan(carry_r[0:1, 0:NC][:, ::-1], top[0:1, 0, 0:NC][:, ::-1],
                                       top[0:1, 1, 0:NC][:, ::-1], 0.0, ALU.mult, ALU.add))
            assert dc[0] == D_CARRY1
            dve.wait_ge(LD["ct"], 2)
            dstep(V.tensor_copy(carry_c[:, 0:1], bank[3][0:NC, 128:129]))
            dstep(V.tensor_tensor_scan(s3a[:, ::-1], on_c[:, ::-1], er[:, ::-1], carry_c[:, 0:1], ALU.mult, ALU.add))
            dstep(V.tensor_tensor(s3b, el, s3a, ALU.add))
            dstep(V.scalar_tensor_tensor(el, s3b, 0.2, s3b, ALU.mult, ALU.max))
            dstep(V.tensor_scalar(er, keep_c[:, :], -1.0, BIG, ALU.add, ALU.mult))
            dstep(V.tensor_tensor_scan(s3a, er, el, -BIG, ALU.add, ALU.max))
            dstep(V.tensor_reduce(edge_c[:, 0:1], er, AX_X, ALU.min))
            dstep(V.tensor_copy(edge_c[:, 2:3], s3a[:, CH - 1:CH]))
            assert dc[0] == D_SUM2
            dve.wait_ge(LD["ct"], 3)
            dstep(V.tensor_copy(top[0:1, :, 0:NC], bank[3][0:1, 0:128].rearrange("p (a b) -> p a b", a=2)[:, :, 0:NC]))
            dstep(V.memset(carry_r[:, :], -BIG))
            dstep(V.tensor_tensor_scan(carry_r[0:1, 1:NC + 1], top[0:1, 0, 0:NC], top[0:1, 1, 0:NC], -BIG, ALU.add, ALU.max))
            assert dc[0] == D_CARRY2
            dve.wait_ge(LD["ct"], 4)
            dstep(V.tensor_copy(carry_c[:, 0:1], bank[3][0:NC, 128:129]))
            mx = dstf_c[:, 0:CH + 1]
            dstep(V.tensor_copy(mx[:, 0:1], carry_c[:, 0:1]))
            dstep(V.tensor_tensor_scan(mx[:, 1:CH + 1], er, el, carry_c[:, 0:1], ALU.add, ALU.max))
            dstep(V.tensor_tensor(s3a, mx[:, 0:CH], mx[:, 1:CH + 1], ALU.subtract))
            dstep(V.tensor_scalar(s3a, s3a, 0.0, None, ALU.min))
            dstep(V.tensor_tensor(s3b, el, mx[:, 1:CH + 1], ALU.subtract))
            assert dc[0] == D_EXP
            dve.wait_ge(LD["ca"], 1)
            dstep(V.tensor_tensor(s2_c[:, 0, :], s2_c[:, 0, :], keep_c[:, :], ALU.mult))
            assert dc[0] == D_ROWS

            AT65 = AT[0:R, :].rearrange("p (k f) -> p k f", f=128)

            def slot_g(k, q, h, front, back):
                if front:
                    at_least(dve, G_ld[q], h * 64 + 64)
                    V.tensor_tensor(l_z[q][0:D, :], l_z[q][0:D, :], l_m[q][0:D, :], ALU.mult).then_inc(LE["msg"].sem, 1)
                    V.tensor_copy(l_z[q][D:D + 1, :], l_m[q][D:D + 1, :]).then_inc(LE["msg"].sem, 1)
                    at_least(dve, LE["aggT"], k - 1)
                    at_least(dve, LE["msg"], k * 2 + 2)
                    init = 0.0 if isinstance(k, int) and k == 0 else agg[(q - 1) % 2][0:D + 1, CH - 1:CH]
                    at_least(dve, LE["agg"], k)
                    V.tensor_tensor_scan(agg[q % 2][0:D + 1, :], l_k[q][:, :], l_z[q][:, :], init,
                                         ALU.mult, ALU.add).then_inc(LE["agg"].sem, 1)
                if back:
                    kb, qb, hb, pb = before(k, q, h)
                    at_least(dve, LE["aggT"], kb + 1)
                    V.tensor_scalar(lden[:, :], AT65[:, :, D], 0.0, None, ALU.is_equal).then_inc(LE["den"].sem, 1)
                    at_least(dve, LE["den"], kb + 1)
                    V.tensor_tensor(lmn[:, :], AT65[:, :, D], lden[:, :], ALU.add).then_inc(LE["den2"].sem, 1)
                    at_least(dve, LE["den2"], kb + 1)
                    V.reciprocal(lden[:, :], lmn[:, :]).then_inc(LE["rden"].sem, 1)
                    at_least(dve, LE["rden"], kb + 1)
                    V.tensor_tensor(v4(v_r[:, :]), AT65[:, :, 0:D], spread(lden[:, :], TC), ALU.mult).then_inc(LE["t1"].sem, 1)
                    at_least(dve, LE["t1"], kb + 1)
                    at_least(dve, LE["rows"], kb)
                    V.tensor_tensor(w_r[:, :], v_r[:, :], l_b[qb][:, :], ALU.add).then_inc(LE["t2"].sem, 1)
                    at_least(dve, LE["t2"], kb + 1)
                    V.tensor_tensor(v4(w_r[:, :]), v4(w_r[:, :]), row_bias(2, TC), ALU.add).then_inc(LE["t3"].sem, 1)
                    finish(LE, kb, qb, hb, w_r[:, :], G_st)
            chunk_slots(slot_g, dve)
            at_least(dve, LE["rows"], NC)

            def slot_f(k, q, h, front, back):
                p = q % 2
                if front:
                    live = tile_scalar(last_t, (NC - 1) - k if isinstance(k, int) else dve.snap(k * -1 + (NC - 1)))
                    at_least(dve, F_ld[q], h * 32 + 32)
                    at_least(dve, LF["msgT"], k - 1)
                    V.tensor_tensor(half(m_r[p]), half(l_a[q]), live, ALU.mult)\
                     .then_inc(LF["msg"].sem, 1)
                    at_least(dve, LF["msgT"], k + 1)
                    if isinstance(k, int):
                        at_least(dve, F_st[p], 16 * (k // 2))
                    else:
                        at_least(dve, F_st[p], h * 32 + (q // 2) * 16)
                    first = isinstance(k, int) and k == 0
                    at_least(dve, LF["fill"], k)
                    V.tensor_tensor_scan(agg[p][0:D, ::-1], l_k[q][0:D, ::-1], MT[0:D, 0:CH][:, ::-1],
                                         0.0 if first else agg[1 - p][0:D, 0:1], ALU.mult, ALU.add).then_inc(LF["fill"].sem, 1)
            chunk_slots(slot_f, dve)
            for r in range(2):
                at_least(dve, F_st[r], 16 * len(range(r, NC, 2)))

            def slot_m(k, q, h, front, back):
                p = q % 2
                if back:
                    kb, qb, hb, pb = before(k, q, h)
                    at_least(dve, LG["dn2"], kb + 1)
                    V.tensor_tensor(v4(v_r[:, :]), OTv, v4(l_b[qb][:, :]), ALU.add).then_inc(LG["t1"].sem, 1)
                    at_least(dve, LG["t1"], kb + 1)
                    at_least(dve, LG["rows"], kb)
                    V.tensor_tensor(v4(w_r[:, :]), v4(v_r[:, :]), row_bias(3, TC), ALU.add).then_inc(LG["t2"].sem, 1)
                if front:
                    at_least(dve, LG["msg"], k + 1)
                    at_least(dve, LG["agg"], k)
                    init = 0.0 if isinstance(k, int) and k == 0 else l_up[(q - 1) % 4][0:D, CH - 1:CH]
                    V.tensor_tensor_scan(l_up[q][0:D, :], l_k[q][0:D, :], l_m[q][0:D, :], init,
                                         ALU.mult, ALU.add).then_inc(LG["agg"].sem, 1)
                if back:
                    if isinstance(kb, int):
                        at_least(dve, M_sc[pb], 64 * ((kb - 4) // 2 + 1))
                    else:
                        at_least(dve, M_sc[pb], hb * 128 + ((qb // 2) * 64 - 64))
                    finish(LG, kb, qb, hb, w_r[:, :], None)
            chunk_slots(slot_m, dve)


C_ROWS = 4
C_SUM = 10
C_CARRY = 13
C_DD = 18
C_DINV = 23
C_INFO = 31
C_ALL = 37
PREP_TWO = 32
PREP_ALL = 39
D_SUM1, D_CARRY1, D_SUM2, D_CARRY2, D_EXP, D_ROWS = 4, 7, 15, 18, 24, 25

_INS = ["x", "dst", "edge_weight",
        "L0_gnn_W1", "L0_gnn_b1", "L0_gnn_W2", "L0_gnn_b2", "L1_gnn_W1", "L1_gnn_b1", "L1_gnn_W2", "L1_gnn_b2",
        "L2_gnn_W", "L2_gnn_attn_l", "L2_gnn_attn_r", "L2_gnn_bias", "L3_gnn_mW1", "L3_gnn_mb1", "L3_gnn_mW2",
        "L3_gnn_mb2", "L3_gnn_uW1", "L3_gnn_ub1", "L3_gnn_uW2", "L3_gnn_ub2"]


def kernel(**inputs):
    import numpy as _np
    import concourse.bacc as _bacc
    from concourse import mybir as _mybir
    from concourse.bass_utils import run_bass_kernel_spmd as _run

    given = {n: _np.asarray(inputs[n]) for n in _INS}
    for n, name in (("src", "src_by_tile"), ("dst", "dst_by_tile"), ("edge_weight", "edge_weight_by_tile")):
        given[name] = _np.asarray(inputs[n]).reshape(NT, R).T
    given["edge_attr_cols"] = _np.asarray(inputs["edge_attr_32"]).T
    nc = _bacc.Bacc("TRN2", target_bir_lowering=False, num_devices=1)
    arrays, t = {}, {}
    for name, a in given.items():
        a = _np.ascontiguousarray(a)
        arrays[f"in_{name}"] = a
        t[name] = nc.dram_tensor(f"in_{name}", a.shape, _mybir.dt.from_np(a.dtype), kind="ExternalInput").ap()
    out = nc.dram_tensor("out_rows", (N, D), F32, kind="ExternalOutput").ap()
    build(nc, t, out)
    r = _run(nc, [arrays], core_ids=[0])
    return r.results[0]["out_rows"]
```

```python
from contextlib import ExitStack

import concourse.bass as bass
from concourse import mybir

F32 = mybir.dt.float32
I32 = mybir.dt.int32
ALU = mybir.AluOpType
ACT = mybir.ActivationFunctionType
AX_X = mybir.AxisListType.X

N = 100000
E = 25000
D = 64
DE = 32
H = 128
R = 125
TB = 8
BLK = R * TB
BW = TB * D
TC = 4
CH = R * TC
CW = TC * D
NT = E // R
NC = E // CH
NB = N // BLK
NI = E // BLK
EPS = 1e-5
BIG = 3.0e38
FAR = 1.0e6


class Shared:

    def __init__(self, sem, base):
        self.sem, self.base = sem, base


class Run:

    def __init__(self, lo, hi, cols, down, rows, up, ups):
        self.lo, self.hi, self.cols, self.down, self.rows, self.up, self.ups = lo, hi, cols, down, rows, up, ups


class Unit:

    def __init__(self, n, real, pos, stage, i, par, b2, b3):
        self.n, self.real, self.pos, self.stage = n, real, pos, stage
        self.i, self.par, self.b2, self.b3 = i, par, b2, b3


def at_least(eng, sem, value):
    if isinstance(value, int) and value <= 0:
        return
    if isinstance(sem, Shared):
        sem, value = sem.sem, value + sem.base
    eng.wait_ge(sem, value)


def build(nc, t, out):
    ctx = ExitStack()
    with ctx:
        def sb(name, shape, dt=F32):
            return ctx.enter_context(nc.sbuf_tensor(name, shape, dt))

        def sem(name):
            return ctx.enter_context(nc.semaphore(name))

        def sems(prefix, names):
            return {n: sem(f"{prefix}_{n}") for n in names.split()}

        def dram(name, shape, dt=F32):
            return nc.dram_tensor(name, shape, dt, kind="Internal").ap()

        xs_d = dram("xs_rows", (E, D))
        xd_d = dram("xd_rows", (E, D))
        t0_d = dram("t0_h0", (E, D))
        t1_d = dram("t1_x1", (2 * E, D))
        t2_d = dram("t2_h2", (2 * E, D))
        base_d = dram("l1_base", (E, D))
        t3_d = dram("t3_x2", (2 * E, D))
        t4_d = dram("t4_x3", (2 * E, D))
        info_d = dram("node_info", (N, 4))
        keep_d = dram("keep_row", (NC, CH))
        on_d = dram("on_row", (NC, CH))
        z_d = dram("z_cols", (NC, D + 2, CH))
        decay_d = dram("decay_row", (NC, CH))
        ex_d = dram("ex_row", (NC, CH))


        def chunks(ap):
            return ap.rearrange("(c k p) f -> c p k f", k=TC, p=R)

        def blocks(ap):
            return ap.rearrange("(b j p) f -> b p j f", j=TB, p=R)

        ident = sb("ident", [128, 128])
        w_top = [sb(f"w_top{s}", [128, H]) for s in range(3)]
        w_bot = [sb(f"w_bot{s}", [128, H]) for s in range(3)]
        w_dn = [sb(f"w_dn{s}", [H, 128]) for s in range(3)]
        b_up = sb("b_up", [H, 3])
        b_dn = sb("b_dn", [128, 3])
        b_row = sb("b_row", [128, 4, D])
        b_two = sb("b_two", [128, 3, 128])
        gat_w = sb("gat_w", [128, 128])
        gat_raw = sb("gat_raw", [128, D])
        gat_att = sb("gat_att", [128, D])
        gat_tmp = sb("gat_tmp", [128, D])
        w_msg = sb("w_msg", [128, H])
        w_edge = sb("w_edge", [128, H])
        w_msg2 = sb("w_msg2", [H, D])
        w_upd = sb("w_upd", [128, H])
        b_msg = sb("b_msg", [H, 1])
        b_msg2 = sb("b_msg2", [D, 1])
        mean6 = sb("mean6", [128, 8])
        eps = sb("eps", [128, 1])
        wide = sb("wide", [128, 8 * CH])
        info_fill = wide[0:R, 0:N // R * 4]

        src_i = sb("src_i", [R, NT], I32)
        dst_i = sb("dst_i", [R, NT], I32)
        ew_t = sb("ew_t", [R, NT])
        d0_t = sb("d0_t", [R, NT])
        d1_t = sb("d1_t", [R, NT])
        last_t = sb("last_t", [R, NT])
        w0_t = sb("w0_t", [R, NT])
        d1q_t = sb("d1q_t", [R, NT])
        w1_t = sb("w1_t", [R, NT])
        gidx = sb("gidx", [R, NT], I32)
        gfl = sb("gfl", [R, NT])
        gbase = sb("gbase", [R, NT])
        slot_id = sb("slot_id", [R, NT])
        info_r = sb("info_r", [R, NT, 4])
        sidx = sb("sidx", [R, NT], I32)
        fidx = sb("fidx", [R, NT], I32)

        dst_c = sb("dst_c", [NC, CH + 2], I32)
        dstf_c = sb("dstf_c", [NC, CH + 2])
        ew_c = sb("ew_c", [NC, CH])
        one_c = sb("one_c", [NC, CH])
        keep_c = sb("keep_c", [NC, CH])
        last_c = sb("last_c", [NC, CH])
        on_c = sb("on_c", [NC, CH])
        s1_c = sb("s1_c", [NC, 2, CH])
        s2_c = sb("s2_c", [NC, 2, CH])
        s3_c = sb("s3_c", [NC, 2, CH])
        edge_c = sb("edge_c", [NC, 4])
        top = sb("top", [2, 2, NC + 1])
        carry_r = sb("carry_r", [2, NC + 1])
        carry_c = sb("carry_c", [NC, 2])

        x_in_all = [sb(f"x_in{i}", [128, BW]) for i in range(2)]
        x_in = [b[0:R, :] for b in x_in_all]
        x_in_c = [b[:, 0:CH] for b in x_in_all]
        x1_r_all = [sb(f"x1_r{i}", [128, BW]) for i in range(2)]
        x1_r = [b[0:R, :] for b in x1_r_all]
        x2_r_all = [sb(f"x2_r{i}", [128, BW]) for i in range(2)]
        x2_r = [b[0:R, :] for b in x2_r_all]
        x3_r_all = [sb(f"x3_r{i}", [128, BW]) for i in range(2)]
        x3_r = [b[0:R, :] for b in x3_r_all]
        x4_r_all = [sb(f"x4_r{i}", [128, BW]) for i in range(2)]
        x4_r = [b[0:R, :] for b in x4_r_all]
        h0_r_all = [sb(f"h0_r{i}", [128, BW]) for i in range(2)]
        h0_r = [b[0:R, :] for b in h0_r_all]
        h2_r_all = [sb(f"h2_r{i}", [128, BW]) for i in range(2)]
        h2_r = [b[0:R, :] for b in h2_r_all]
        xT = [sb(f"xT{i}", [128, CH]) for i in range(3)]
        hid = [sb(f"hid{i}", [128, 2, CH]) for i in range(2)]
        rT = [sb(f"rT{i}", [128, CH]) for i in range(2)]
        x_up = sb("x_up", [128, 128])
        x_dn = sb("x_dn", [128, 128])
        g_out = sb("g_out", [128, 128])
        cmat = sb("cmat", [128, 128])
        sq = [sb(f"sq{i}", [R, BW]) for i in range(2)]
        y_r = sb("y_r", [R, BW])
        sq_b = sb("sq_b", [R, BW])
        ss = [sb(f"ss{i}", [R, TB]) for i in range(2)]
        sd = [sb(f"sd{i}", [R, TB]) for i in range(2)]
        rs = sb("rs", [R, TB])
        ss_b, sd_b, rs_b = sb("ss_b", [R, TB]), sb("sd_b", [R, TB]), sb("rs_b", [R, TB])

        p_idx = [sb(f"p_idx{i}", [R, TB], I32) for i in range(2)]
        p_row = [sb(f"p_row{i}", [R, TB * 4]) for i in range(2)]
        g_idx = [sb(f"g_idx{i}", [R, 4 * TC], I32) for i in range(2)]
        g_row = [sb(f"g_row{i}", [R, TC * 128]) for i in range(4)]
        o_idx = [sb(f"o_idx{i}", [R, 4 * TC], I32) for i in range(2)]

        l_src = [sb(f"l_src{i}", [R, CW]) for i in range(4)]
        l_a = [sb(f"l_a{i}", [R, TC * 128]) for i in range(4)]
        l_b = [sb(f"l_b{i}", [R, CW]) for i in range(4)]
        l_k = [sb(f"l_k{i}", [128, CH]) for i in range(4)]
        l_m = [wide[0:D + 1, i * CH:(i + 1) * CH] for i in range(4, 8)]
        l_z = [wide[0:D + 1, i * CH:(i + 1) * CH] for i in range(4)]
        l_in = [b[:, 0:CH] for b in x1_r_all + x2_r_all]
        l_up = [b[:, 0:CH] for b in x3_r_all + x4_r_all]
        l_ea = [b[:, 0:CH] for b in h0_r_all + h2_r_all]
        m_r = [sb(f"m_r{i}", [R, TC * 128]) for i in range(2)]
        agg = [sb(f"agg{i}", [128, CH]) for i in range(2)]
        zx = [sb(f"zx{i}", [D + 2, CH]) for i in range(2)]
        lxT = [sb(f"lxT{i}", [128, CH]) for i in range(4)]
        lhid = [sb(f"lhid{i}", [128, CH]) for i in range(2)]
        lhid2 = [sb(f"lhid2{i}", [128, CH]) for i in range(2)]
        u_r = [sb(f"u_r{i}", [R, TC * 128]) for i in range(2)]
        v_r = sb("v_r", [R, CW])
        w_rs = [sb(f"w_r{i}", [R, CW]) for i in range(2)]
        n_r = [sb(f"n_r{i}", [R, CW]) for i in range(4)]
        lsq = sb("lsq", [R, CW])
        lrden, lss, lsd, lrs, lden = (sb(f"l_{x}", [R, TC]) for x in ("rden", "ss", "sd", "rs", "den"))

        s_w = sem("weights_loaded")
        s_e = sem("edges_loaded")
        s_pad = sem("dst_padding_set")
        s_pool0 = sem("ident_steps")
        s_set = sem("sbuf_zeroed")
        s_prep = sem("dve_weight_steps")
        s_bt = sem("bias_transposed")
        s_c = sem("dve_scalar_steps")
        s_ct = sem("scalar_transposes")
        s_ca = sem("act_scalar_steps")
        s_rows = sem("scalar_rows_stored")
        s_init = sem("node_info_initialised")
        P = sems("pool", "copied idx0 idx1 xs0 xs1 xss0 xss1 sc0 sc1 inf0 inf1 xd0 xd1 xds0 xds1")
        Cn = sems("chain", "rowsT xT up hid dn res resT h0 h0b h2 h2b sq ssum std rstd"
                           " rows y sq2 ssum2 std2 rstd2 rows2 in0 in1 out0 out1 s0st0 s0st1 s1st0 s1st1")

        ctx.enter_context(nc.allow_non_contiguous_dma(reason="bias columns and the chunks' neighbours, once"))
        block = ctx.enter_context(nc.Block())

        W1 = [t["L0_gnn_W1"], t["L1_gnn_W1"], t["L3_gnn_uW1"][0:D, :]]
        W2 = [t["L0_gnn_W2"], t["L1_gnn_W2"], t["L3_gnn_uW2"]]
        B1 = [t["L0_gnn_b1"], t["L1_gnn_b1"], t["L3_gnn_ub1"]]
        BR = [t["L0_gnn_b2"], t["L1_gnn_b2"], t["L2_gnn_bias"], t["L3_gnn_ub2"]]

        def column(ap):
            return ap.rearrange("(p a) -> p a", a=1)

        def everywhere(ap, p=128):
            return ap.rearrange("(a f) -> a f", a=1).to_broadcast([p, ap.shape[0]])

        weight_loads = []
        for s in range(3):
            weight_loads += [(w_top[s][0:D, :], W1[s]), (w_bot[s][D:128, :], W1[s]), (w_dn[s][:, 0:D], W2[s]),
                             (b_up[:, s:s + 1], column(B1[s]))]
        weight_loads += [(b_row[:, i, :], everywhere(BR[i])) for i in range(4)]
        weight_loads += [(gat_raw[0:D, :], t["L2_gnn_W"]), (gat_raw[D:128, :], t["L2_gnn_W"]),
                         (gat_att[0:D, :], everywhere(t["L2_gnn_attn_l"], D)),
                         (gat_att[D:128, :], everywhere(t["L2_gnn_attn_r"], D)),
                         (w_msg[:, :], t["L3_gnn_mW1"][0:128, :]), (w_edge[0:DE, :], t["L3_gnn_mW1"][128:160, :]),
                         (w_msg2[:, :], t["L3_gnn_mW2"]), (w_upd[0:D, :], t["L3_gnn_uW1"][D:128, :]),
                         (w_upd[D:128, :], t["L3_gnn_uW1"][0:D, :]),
                         (b_msg[:, :], column(t["L3_gnn_mb1"])), (b_msg2[:, :], column(t["L3_gnn_mb2"]))]
        ALL_W = 16 * len(weight_loads)
        dst2 = t["dst"].rearrange("(c j) -> c j", j=CH)
        edge_loads = [(dst_c[:, 1:CH + 1], dst2), (dst_c[1:NC, 0:1], dst2[0:NC - 1, CH - 1:CH]),
                      (dst_c[0:NC - 1, CH + 1:CH + 2], dst2[1:NC, 0:1]),
                      (ew_c[:, :], t["edge_weight"].rearrange("(c j) -> c j", j=CH)),
                      (src_i[:, :], t["src_by_tile"]), (dst_i[:, :], t["dst_by_tile"]),
                      (ew_t[:, :], t["edge_weight_by_tile"])]
        ALL_E = 16 * len(edge_loads)
        EARLY_ONES = 1 + 8 + 4 + 2 + 2 + 2
        N_ONES = EARLY_ONES + 4 + 4
        N_SET = 13

        STAGE = [1, 0, 2]
        LAST = NB + NI
        MS = (LAST + 5) // 2
        BESIDE_ONE = 8

        bank = [ctx.enter_context(nc.psum_tensor(f"bank{i}", [128, 512], F32)) for i in range(4)]
        pair = [ctx.enter_context(nc.psum_tensor(f"pair{i}", [128, 2, 512], F32)) for i in range(2)]

        MAIN = Run(0, MS - 3 * BESIDE_ONE, bank[0], bank[1], [bank[2], bank[3]], pair, 2)
        BESIDE = [bank[1], bank[2], [pair[1][:, 0, :], pair[1][:, 1, :]], [pair[0], pair[0]], 1]
        WITH_C, WITH_D, WITH_G = [Run(MS - n * BESIDE_ONE, MS - (n - 1) * BESIDE_ONE, *BESIDE) for n in (3, 2, 1)]

        def unit(run, m, u):
            q, pos = u // 3, u % 3
            real = (not isinstance(m, int)) or 6 * run.lo <= 6 * m + u < 6 * run.hi
            return Unit(m * 6 + u, real, pos, STAGE[pos], m * 2 + q, q % 2, u % 2, u % 3)

        def is_dense(mode, i):
            return i >= NI if mode is None else mode == "dense"

        def turned(mode, i, pos):
            return i * 2 + (NI + [1, 1, 2][pos]) if is_dense(mode, i) else i * 3 + (pos + 1)

        def columns_of(mode, a):
            return x_in_c[a.par] if a.stage == 0 and is_dense(mode, a.i) else xT[a.b3]

        def main_slots(make, eng, midway=None):
            known = make(None)

            def straight(lo, hi):
                for m in range(lo, hi):
                    for u in range(6):
                        known(m, u)

            def looped(mode, lo, hi):
                slot = make(mode)
                with eng.Fori(lo, hi, 1) as m:
                    for u in range(6):
                        slot(m, u)

            known(0, -1)
            straight(0, 4)
            looped("iso", 4, NI // 2)
            straight(NI // 2, NI // 2 + 5)
            if midway is not None:
                midway()
            looped("dense", NI // 2 + 5, MAIN.hi - 1)
            straight(MAIN.hi - 1, MAIN.hi)
            for u in range(5):
                known(MAIN.hi, u)

        def beside(make):
            by_number, in_loop = make(None), make("dense")
            return lambda m, u: (by_number if isinstance(m, int) else in_loop)(m, u)

        def half(buf):
            return buf[:, :].rearrange("p (k f) -> p k f", f=128)[:, :, 0:D]

        def n_view(ap):
            return ap.rearrange("p (j f) -> p j f", f=D)

        def spread(col, n):
            return col.unsqueeze(2).to_broadcast([R, n, D])

        def row_bias(i, n):
            return b_row[0:R, i, :].unsqueeze(1).to_broadcast([R, n, D])

        def where(k, q, h):
            def at(lag):
                if isinstance(k, int) and not 0 <= k - lag < NC:
                    return None
                return k - lag, (q - lag) % 4, h + (q - lag) // 4, (q - lag) % 2
            return at

        def lagged_slots(slot, eng, deepest):
            for k in range(12):
                slot(where(k, k % 4, k // 4))
            with eng.Fori(3, NC // 4, 1) as j:
                for q in range(4):
                    slot(where(j * 4 + q, q, j))
            for k in range(4 * (NC // 4), NC + deepest):
                slot(where(k, k % 4, k // 4))

        def shared_slots(slot, chain, run, eng, deepest, after=None, before=None):
            def both(k, q, h, m, u):
                if before is not None and m is not None:
                    before(m, u)
                slot(where(k, q, h))
                if m is not None:
                    chain(m, u)
                if after is not None:
                    after(where(k, q, h))

            def straight(k):
                m, u = (k - 1) // 6, (k - 1) % 6
                both(k, k % 4, k // 4, None if k > 53 else run.lo + m, -1 if k == 0 else u)

            both(0, 0, 0, run.lo, -1)
            for k in range(1, 12):
                straight(k)
            with eng.Fori(1, 4, 1) as j:
                for r in range(12):
                    both(j * 12 + r, r % 4, j * 3 + r // 4, j * 2 + (run.lo + (r - 1) // 6), (r - 1) % 6)
            for k in range(48, max(NC + deepest, 54)):
                straight(k)

        def mirror(eng, k):
            return (NC - 1) - k if isinstance(k, int) else eng.snap(k * -1 + (NC - 1))

        shared, counted = {}, {}

        def level_sems(names):
            made = {}
            for name in names.split():
                if name not in shared:
                    shared[name], counted[name] = sem(f"level_{name}"), 0
                made[name] = Shared(shared[name], counted[name])
                counted[name] += NC
            return made

        def in_turn(name, n, per_chunk):
            made = []
            for r in range(n):
                key = f"{name}{r}"
                if key not in shared:
                    shared[key], counted[key] = sem(f"level_{key}"), 0
                made.append(Shared(shared[key], counted[key]))
                counted[key] += per_chunk * len(range(r, NC, n))
            return made

        LA = level_sems("msg msgT agg aggT xdT xcol xc up hid dn t1 t2 t3 t4 sq ssum std rstd rows")
        LB = level_sems("msg msgT agg aggT t1 t2 u xb b1 base uT ucol up hid dn rows")
        LC = level_sems("msg msgT agg aggT t1 t2 sq ssum std rstd rows")
        LD = level_sems("lky1 lky2 lkyT col zx zc")
        LE = level_sems("msg agg aggT den rden t1 t2 sq ssum std rstd rows")
        LG = level_sems("live srcT scol fill fillc up hid dn msg agg up2 hid2 dn2 t1 sq ssum std rstd rows")
        LD["c"], LD["ct"], LD["ca"] = sem("score_steps"), sem("score_transposes"), sem("score_exp")
        A_ld, A_st = in_turn("ld", 4, 48), in_turn("st", 4, 16)
        B_ld, B_ga, B_st = in_turn("ld", 4, 32), in_turn("ga", 4, 64), in_turn("st", 4, 16)
        B_bst = in_turn("bst", 4, 16)
        C_ld, C_ga, C_st = in_turn("ld", 4, 32), in_turn("ga", 4, 64), in_turn("st", 4, 16)
        D_ld, D_ga, D_st = in_turn("ld", 4, 16), in_turn("ga", 4, 64), in_turn("zst", 2, 16)
        G_ld, G_st = in_turn("ld", 4, 64), in_turn("st", 4, 16)
        M_ld, M_ga, M_sc = in_turn("ld", 4, 48), in_turn("ga", 4, 64), in_turn("sc", 2, 64)
        s_ones = sem("constant_rows_set")

        def all_stored(eng, st, k_total=NC, n=4):
            for r in range(n):
                at_least(eng, st[r], 16 * len(range(r, k_total, n)))

        @block.sync
        def _(sp):
            sp.wait_ge(s_pad, 1)
            for dst, src in edge_loads:
                sp.dma_start(dst, src).then_inc(s_e, 16)
            sp.wait_ge(s_set, N_SET - 1)
            for dst, src in weight_loads:
                sp.dma_start(dst, src).then_inc(s_w, 16)
            sp.wait_ge(s_set, N_SET)
            sp.dma_start(info_d.rearrange("(p a) c -> p (a c)", p=R), info_fill).then_inc(s_init, 16)
            sp.wait_ge(s_c, C_ROWS)
            sp.dma_start(keep_d, keep_c[:, :]).then_inc(s_rows, 16)
            sp.dma_start(on_d, on_c[:, :]).then_inc(s_rows, 16)

            dense_out = out.rearrange("(b p j) f -> b p (j f)", p=R, j=TB)
            xs_v = blocks(xs_d)
            in_sem, out_sem = [Cn["in0"], Cn["in1"]], [Cn["out0"], Cn["out1"]]
            s0_sem, s1_sem = [Cn["s0st0"], Cn["s0st1"]], [Cn["s1st0"], Cn["s1st1"]]

            def load(i, par, half, iso):
                known = isinstance(i, int)
                if iso or (known and i - 2 < NI):
                    at_least(sp, Cn["h0"], i - 1)
                if iso or (known and i - 2 < NI):
                    at_least(sp, Cn["rowsT"], i * 3 - 4)
                else:
                    sp.wait_ge(Cn["res"], i * 3 - 4)
                if iso:
                    sp.wait_ge([P["xss0"], P["xss1"]][par], half * 16 + 16)
                    sp.dma_start(n_view(x_in[par][:, :]), xs_v[i]).then_inc(in_sem[par], 16)
                else:
                    block_no = min(i, LAST - 1) - NI if known else i - NI
                    sp.dma_start(x_in_c[par], t["x_cols"][block_no]).then_inc(in_sem[par], 16)

            def store_dense(i, par):
                sp.wait_ge(Cn["rows"], i * 3 + 3)
                sp.dma_start(dense_out[i - (NI + 4)], x4_r[par][:, :]).then_inc(out_sem[par], 16)

            def store_s0(i, par):
                sp.wait_ge(Cn["h0b"], i + 1)
                sp.dma_start(blocks(t0_d)[i], n_view(h0_r[par][:, :])).then_inc(s0_sem[par], 16)
                sp.wait_ge(Cn["rows"], i * 3 + 2)
                sp.dma_start(blocks(t1_d[E:2 * E, :])[i], n_view(x1_r[par][:, :])).then_inc(s0_sem[par], 16)

            def store_s1(i, par):
                b = i - 2
                sp.wait_ge(Cn["h2b"], i - 1)
                sp.dma_start(blocks(t2_d[E:2 * E, :])[b], n_view(h2_r[par][:, :])).then_inc(s1_sem[par], 16)
                sp.wait_ge(Cn["rows"], i * 3 + 1)
                sp.dma_start(blocks(t3_d[E:2 * E, :])[b], n_view(x2_r[par][:, :])).then_inc(s1_sem[par], 16)
                sp.wait_ge(Cn["rows2"], i + 1)
                sp.dma_start(blocks(t4_d[E:2 * E, :])[b], n_view(x3_r[par][:, :])).then_inc(s1_sem[par], 16)

            def iteration(i):
                load(i + 1, (i + 1) % 2, (i + 1) // 2, i + 1 < NI)
                j = i - 1
                if 0 <= j < NI:
                    store_s0(j, j % 2)
                if 2 <= j < NI + 2:
                    store_s1(j, j % 2)
                if NI + 4 <= j:
                    store_dense(j, j % 2)

            for i in range(-1, 4):
                iteration(i)
            with sp.Fori(2, NI // 2 - 1, 1) as m:
                for q in range(2):
                    load(m * 2 + (q + 1), (q + 1) % 2, m + (q + 1) // 2, True)
                    store_s0(m * 2 + (q - 1), (q - 1) % 2)
                    store_s1(m * 2 + (q - 1), (q - 1) % 2)
            for i in range(2 * (NI // 2 - 1), NI + 7):
                iteration(i)
            with sp.Fori((NI + 7) // 2, MAIN.hi, 1) as m:
                for q in range(2):
                    load(m * 2 + (q + 1), (q + 1) % 2, None, False)
                    store_dense(m * 2 + (q - 1), (q - 1) % 2)
            load(2 * MAIN.hi + 1, 1, None, False)

            sp.wait_ge(s_ones, EARLY_ONES)
            sp.wait_ge(s_rows, 32)
            for r in range(2):
                sp.wait_ge(s0_sem[r], 32 * len(range(r, NI, 2)))

            def rows_of(table):
                return chunks(table[0:E, :])

            def level(loads, ld, used, st, done, where, behind=0, run=None, late=0, also=None, need=None):
                def ld_chunk(k, q, first):
                    pairs = loads(k, q)
                    if not first:
                        for s in used:
                            at_least(sp, s, k - 3)
                    if need is not None:
                        need(k, q)
                    for to, frm in pairs:
                        sp.dma_start(to, frm).then_inc(ld[q].sem, 16)

                def st_chunk(k, q):
                    to, frm = where(k, q)
                    at_least(sp, done, k + 1)
                    sp.dma_start(to, frm).then_inc(st[q % len(st)].sem, 16)
                    if also is not None:
                        st2, done2, where2 = also
                        to, frm = where2(k, q)
                        at_least(sp, done2, k + 1)
                        sp.dma_start(to, frm).then_inc(st2[q].sem, 16)

                for k in range(4):
                    ld_chunk(k, k, True)

                def straight(k):
                    if k + 4 < NC:
                        ld_chunk(k + 4, k % 4, False)
                    if k >= behind:
                        st_chunk(k - behind, (k - behind) % 4)
                    if run is not None and k % 3 == 0:
                        i = 2 * run.lo + k // 3 - late
                        if 2 * run.lo <= i < 2 * run.hi:
                            if i + 2 < 2 * MS:
                                load(i + 2, i % 2, None, False)
                            store_dense(i - 1, (i - 1) % 2)

                body = 4 if run is None else 12
                first = 2 if run is None else 1
                loops = NC // 4 - 1 if run is None else 2 if run is WITH_G else 3
                for k in range(first * body):
                    straight(k)
                with sp.Fori(first, loops, 1) as j:
                    for r in range(body):
                        ld_chunk(j * body + (r + 4), r % 4, False)
                        st_chunk(j * body + (r - behind), (r - behind) % 4)
                        if run is not None and r % 3 == 0:
                            i = j * 4 + (2 * run.lo + r // 3 - late)
                            load(i + 2, (r // 3 - late) % 2, None, False)
                            store_dense(i - 1, (r // 3 - late - 1) % 2)
                for k in range(loops * body, NC + behind):
                    straight(k)

            def bc(row_d, k, p):
                return row_d[k].rearrange("(a f) -> a f", a=1).to_broadcast([p, CH])

            def v4(ap):
                return ap.rearrange("p (k f) -> p k f", f=D)

            def x_dst_there(k, q):
                sp.wait_ge([P["xds0"], P["xds1"]][q // 2], k * 4 + (16 - 4 * q))

            level(lambda k, q: [(v4(l_src[q][:, :]), chunks(t0_d)[k]), (half(l_a[q]), chunks(xd_d)[k]),
                                (l_k[q][0:D, :], bc(keep_d, k, D))],
                  A_ld, [LA["xdT"], LA["agg"]], A_st, LA["rows"], lambda k, q: (rows_of(t1_d)[k], v4(n_r[q][:, :])), behind=3,
                  need=x_dst_there)
            all_stored(sp, A_st)
            level(lambda k, q: [(half(l_a[q]), rows_of(t1_d)[k]), (l_k[q][0:D, :], bc(keep_d, k, D))],
                  B_ld, [LB["xb"]], B_st, LB["rows"], lambda k, q: (rows_of(t2_d)[k], v4(n_r[q][:, :])), behind=3,
                  also=(B_bst, LB["base"], lambda k, q: (chunks(base_d)[k], v4(l_src[q][:, :]))))
            all_stored(sp, B_st)
            all_stored(sp, B_bst)
            level(lambda k, q: [(v4(l_b[q][:, :]), chunks(base_d)[k]),
                                (l_k[q][0:D, :], bc(keep_d, k, D))],
                  C_ld, [LC["t2"]], C_st, LC["rows"], lambda k, q: (rows_of(t3_d)[k], v4(n_r[q][:, :])),
                  behind=1, run=WITH_C)
            all_stored(sp, C_st)
            level(lambda k, q: [(half(l_a[q]), rows_of(t3_d)[k])],
                  D_ld, [LD["lky2"]], D_st, LD["zc"], lambda k, q: (z_d[k], zx[q % 2][:, :]), behind=2, run=WITH_D, late=1)
            for r in range(2):
                at_least(sp, D_st[r], 16 * len(range(r, NC, 2)))
            sp.dma_start(s1_c[:, 0, :], z_d[:, D, :]).then_inc(s_rows, 16)
            sp.dma_start(s1_c[:, 1, :], z_d[:, D + 1, :]).then_inc(s_rows, 16)
            sp.wait_ge(LD["c"], D_ROWS)
            sp.dma_start(decay_d, s2_c[:, 0, :]).then_inc(s_rows, 16)
            sp.dma_start(ex_d, s2_c[:, 1, :]).then_inc(s_rows, 16)
            sp.wait_ge(s_rows, 96)
            sp.wait_ge(s_ones, N_ONES)
            level(lambda k, q: [(l_z[q][0:D, :], z_d[k, 0:D, :]), (l_m[q][:, :], bc(ex_d, k, D + 1)),
                                (l_k[q][0:D + 1, :], bc(decay_d, k, D + 1)), (v4(l_b[q][:, :]), rows_of(t3_d)[k])],
                  G_ld, [LE["agg"], LE["t2"]], G_st, LE["rows"], lambda k, q: (rows_of(t4_d)[k], v4(n_r[q][:, :])), behind=1,
                  run=WITH_G, late=1)
            all_stored(sp, G_st)

            def ld_m(k, q, first):
                c = mirror(sp, k)
                if not first:
                    at_least(sp, LG["agg"], k - 3)
                for to, frm in [(half(l_a[q]), rows_of(t4_d)[c]), (l_k[q][:, :], bc(on_d, c, 128)),
                                (l_ea[q][0:DE, :], t["edge_attr_cols"].rearrange("f (c j) -> c f j", j=CH)[c])]:
                    sp.dma_start(to, frm).then_inc(M_ld[q].sem, 16)

            for k in range(4):
                ld_m(k, k, True)
            for k in range(4):
                ld_m(k + 4, k, False)
            with sp.Fori(1, NC // 4 - 1, 1) as j:
                for q in range(4):
                    ld_m(j * 4 + (q + 4), q, False)
            for k in range(4 * (NC // 4), NC):
                ld_m(k, k % 4, False)

        @block.gpsimd
        def _(pool):
            g = nc.gpsimd
            g.memset(ident[:, :], 0.0).then_inc(s_pool0, 1)
            pool.wait_ge(s_pool0, 1)
            g.affine_select(out=ident[:, :], in_=ident[:, :], compare_op=ALU.not_equal, fill=1.0, base=0,
                            pattern=[[-1, 128]], channel_multiplier=1).then_inc(s_pool0, 1)
            g.iota(slot_id[:, :], pattern=[[R, NT]], base=0, channel_multiplier=1,
                   allow_small_or_imprecise_dtypes=True).then_inc(s_pool0, 1)
            g.iota(gbase[:, :], pattern=[[R, NT]], base=E, channel_multiplier=1,
                   allow_small_or_imprecise_dtypes=True).then_inc(s_pool0, 1)
            pool.wait_ge(s_e, ALL_E)
            n_nodes, n_rows = pool.to_reg(N), pool.to_reg(2 * E)

            bound = pool.alloc_register("row_bound")

            def settle(rows):
                pool.reg_add(bound, rows, -1)

            def over_units(body, total):
                body(0, 0, 0)
                body(1, 1, 0)
                with pool.Fori(1, total // 2, 1) as j:
                    for q in range(2):
                        body(j * 2 + q, q, j)
                for b in range(2 * (total // 2), total):
                    body(b, b % 2, b // 2)

            def rows_by_index(idx, sem_got, sem_stored, to_d, base):
                def store(b, r, half):
                    par = r % 2
                    pool.wait_ge(sem_got[par], (half + 1) * (16 * TB))
                    at_least(pool, sem_stored[par], half * 16)
                    pool.dma_start(blocks(to_d)[b], n_view(g_row[r][:, :])).then_inc(sem_stored[par], 16)

                def body(b, r, half):
                    par = r % 2
                    g.tensor_copy(p_idx[par][:, :], idx[:, bass.ds(b * TB, TB)]).then_inc(P["copied"], 1)
                    pool.wait_ge(P["copied"], b + (base + 1))
                    settle(n_nodes)
                    for j in range(TB):
                        g.indirect_dma_start(
                            out=g_row[r][:, j * D:(j + 1) * D], out_offset=None, in_=t["x"],
                            in_offset=bass.IndirectOffsetOnAxis(ap=p_idx[par][:, j:j + 1], axis=0),
                            bounds_check=bound, oob_is_err=False).then_inc(sem_got[par], 16)
                    if not (isinstance(b, int) and b == 0):
                        store(b - 1, (r - 1) % 4, half - (1 - par))

                for b in range(4):
                    body(b, b, b // 2)
                with pool.Fori(1, NI // 4, 1) as j:
                    for r in range(4):
                        body(j * 4 + r, r, j * 2 + r // 2)
                for b in range(4 * (NI // 4), NI):
                    body(b, b % 4, b // 2)
                store(NI - 1, (NI - 1) % 4, (NI - 1) // 2)

            rows_by_index(src_i, [P["xs0"], P["xs1"]], [P["xss0"], P["xss1"]], xs_d, 0)

            pool.wait_ge(s_init, 16)
            pool.wait_ge(s_c, C_INFO)
            sc = [P["sc0"], P["sc1"]]

            def scatter_info(b, par, half):
                at_least(pool, sc[par], half * (16 * TB))
                g.tensor_copy(p_idx[par][:, :], sidx[:, bass.ds(b * TB, TB)]).then_inc(P["copied"], 1)
                g.tensor_copy(p_row[par][:, 0:TB * 4], info_r[:, :, :].rearrange("p t c -> p (t c)")
                              [:, bass.ds(b * (TB * 4), TB * 4)]).then_inc(P["copied"], 1)
                pool.wait_ge(P["copied"], b * 2 + (NI + 2))
                settle(n_nodes)
                for j in range(TB):
                    g.indirect_dma_start(
                        out=info_d, out_offset=bass.IndirectOffsetOnAxis(ap=p_idx[par][:, j:j + 1], axis=0),
                        in_=p_row[par][:, 4 * j:4 * j + 4], in_offset=None,
                        bounds_check=bound, oob_is_err=False).then_inc(sc[par], 16)

            over_units(scatter_info, NI)
            for r in range(2):
                pool.wait_ge(sc[r], 16 * TB * len(range(r, NI, 2)))

            got = [P["inf0"], P["inf1"]]

            def take_info(b, par, half):
                pool.wait_ge(got[par], (half + 1) * (16 * TB))
                g.tensor_copy(info_r[:, :, :].rearrange("p t c -> p (t c)")[:, bass.ds(b * (TB * 4), TB * 4)],
                              p_row[par][:, 0:TB * 4]).then_inc(P["copied"], 1)

            def gather_info(b, par, half):
                g.tensor_copy(p_idx[par][:, :], src_i[:, bass.ds(b * TB, TB)]).then_inc(P["copied"], 1)
                pool.wait_ge(P["copied"], 3 * NI + 1 if isinstance(b, int) and b == 0 else b * 2 + 3 * NI)
                settle(n_nodes)
                for j in range(TB):
                    g.indirect_dma_start(
                        out=p_row[par][:, 4 * j:4 * j + 4], out_offset=None, in_=info_d,
                        in_offset=bass.IndirectOffsetOnAxis(ap=p_idx[par][:, j:j + 1], axis=0),
                        bounds_check=bound, oob_is_err=False).then_inc(got[par], 16)
                if not (isinstance(b, int) and b == 0):
                    take_info(b - 1, 1 - par, half - (1 - par))

            over_units(gather_info, NI)
            take_info(NI - 1, (NI - 1) % 2, (NI - 1) // 2)
            pool.wait_ge(P["copied"], 5 * NI)
            for r in range(2):
                pool.wait_ge([P["xss0"], P["xss1"]][r], 16 * len(range(r, NI, 2)))
            rows_by_index(dst_i, [P["xd0"], P["xd1"]], [P["xds0"], P["xds1"]], xd_d, 5 * NI)

            GROUPS = (NC + 3) // 4

            def pool_slots(body, peeled, total):
                for k in range(peeled):
                    body(k, k % 8, k // 8)
                with pool.Fori(peeled // 8, NC // 8, 1) as j:
                    for r in range(8):
                        body(j * 8 + r, r, j)
                for k in range(8 * (NC // 8), total):
                    body(k, k % 8, k // 8)

            def gather_level(table, ga, used, n_before):
                def body(k, r, j):
                    q, group = r % 4, g_idx[r // 4]
                    used(k)
                    if q == 0:
                        n = min(4 * TC, NT - k * TC) if isinstance(k, int) else 4 * TC
                        g.tensor_copy(group[:, 0:n], gidx[:, bass.ds(k * TC, n)]).then_inc(P["copied"], 1)
                        pool.wait_ge(P["copied"], j * 2 + (r // 4 + 1 + 6 * NI + n_before * GROUPS))
                    settle(n_rows)
                    for i in range(TC):
                        g.indirect_dma_start(
                            out=g_row[q][:, i * 128:i * 128 + D], out_offset=None, in_=table,
                            in_offset=bass.IndirectOffsetOnAxis(ap=group[:, q * TC + i:q * TC + i + 1], axis=0),
                            bounds_check=bound, oob_is_err=False).then_inc(ga[q].sem, 16)
                pool_slots(body, 8, NC)

            for r in range(2):
                pool.wait_ge([Cn["s0st0"], Cn["s0st1"]][r], 32 * len(range(r, NI, 2)))
                pool.wait_ge([Cn["s1st0"], Cn["s1st1"]][r], 48 * len(range(r, NI, 2)))
            pool.wait_ge(s_c, C_ALL)
            all_stored(pool, A_st)
            gather_level(t1_d, B_ga, lambda k: at_least(pool, LB["msg"], k - 3), 0)
            all_stored(pool, B_st)
            gather_level(t2_d, C_ga, lambda k: at_least(pool, LC["msg"], k - 3), 1)
            all_stored(pool, C_st)
            gather_level(t3_d, D_ga, lambda k: at_least(pool, LD["lky1"], k - 3), 2)

            def slot_g(at):
                k, q, h, p = at(0)
                at_least(pool, G_ld[q], h * 64 + 64)
                g.tensor_tensor(l_m[q][:, :], l_z[q][:, :], l_m[q][:, :], ALU.mult).then_inc(LE["msg"].sem, 1)
            lagged_slots(slot_g, pool, 0)
            all_stored(pool, G_st)

            out_sem = [Cn["out0"], Cn["out1"]]
            for r in range(2):
                pool.wait_ge(out_sem[r], 16 * len(range(r, NB, 2)))

            M_LAG = 4
            BASE = 6 * NI + 3 * GROUPS

            def group_of(index, group, k):
                if isinstance(k, int):
                    n = min(4, NC - k)
                    cols = slice((NC - n - k) * TC, (NC - k) * TC)
                    return g.tensor_copy(group[:, 0:n * TC], index[:, cols])
                return g.tensor_copy(group[:, :], index[:, bass.ds(pool.snap(k * -TC + (NC - 4) * TC), 4 * TC)])

            def column(group, k, q, i):
                n = min(4, NC - (k - q)) if isinstance(k, int) else 4
                c = (n - 1 - q) * TC + i
                return group[:, c:c + 1]

            def m_body(k, r, j):
                q = r % 4
                known = isinstance(k, int)
                if not known or k < NC:
                    at_least(pool, LG["srcT"], k - 3)
                    if q == 0:
                        group_of(gidx, g_idx[r // 4], k).then_inc(P["copied"], 1)
                        pool.wait_ge(P["copied"], BASE + 1 if known and k == 0 else j * 4 + (2 * (r // 4) + BASE))
                    settle(n_rows)
                    for i in range(TC):
                        g.indirect_dma_start(
                            out=g_row[q][:, i * 128:i * 128 + D], out_offset=None, in_=t4_d,
                            in_offset=bass.IndirectOffsetOnAxis(ap=column(g_idx[r // 4], k, q, i), axis=0),
                            bounds_check=bound, oob_is_err=False).then_inc(M_ga[q].sem, 16)
                if known and k < M_LAG:
                    return
                kk, par, group = k - M_LAG, r % 2, o_idx[1 - r // 4]
                at_least(pool, M_sc[par], j * 256 + 64 * ((r - M_LAG) // 2))
                if q == 0:
                    group_of(fidx, group, kk).then_inc(P["copied"], 1)
                    copies = j * 4 + (2 * (r // 4) + 1 + BASE)
                    pool.wait_ge(P["copied"], copies - 1 if known and k >= NC else copies)
                at_least(pool, LG["rows"], kk + 1)
                settle(n_nodes)
                for i in range(TC):
                    g.indirect_dma_start(
                        out=out, out_offset=bass.IndirectOffsetOnAxis(ap=column(group, kk, q, i), axis=0),
                        in_=n_r[q][:, i * D:(i + 1) * D], in_offset=None,
                        bounds_check=bound, oob_is_err=False).then_inc(M_sc[par].sem, 16)

            pool_slots(m_body, 16, NC + M_LAG)
            for r in range(2):
                at_least(pool, M_sc[r], 64 * len(range(r, NC, 2)))

        @block.tensor
        def _(pe):
            T = nc.tensor
            pe.wait_ge(s_pool0, 2)

            def turn(dst, src, rows, cols):
                return T.transpose(dst, src, ident[0:rows, 0:rows])

            def summaries(n, wait_sem, v, done):
                pe.wait_ge(wait_sem, v)
                turn(bank[3][0:n, 0:NC], edge_c[:, 0:n], NC, n)
                turn(bank[3][0:n, 64:64 + NC], edge_c[:, 2:2 + n], NC, n).then_inc(done, 1)

            summaries(2, s_c, C_SUM, s_ct)
            pe.wait_ge(s_c, C_CARRY)
            turn(bank[3][0:NC, 128:130], carry_r[0:2, 0:NC], 2, NC).then_inc(s_ct, 1)
            pe.wait_ge(s_c, C_DINV)
            order = [s3_c[:, 0, :], s3_c[:, 1, :], last_c[:, :], s2_c[:, 0, :], s1_c[:, 0, :]]
            tile_order = bank + [pair[0][:, 0, :]]
            for a, what in enumerate(order):
                for k in range(TC):
                    mm = turn(tile_order[a][0:R, k * NC:(k + 1) * NC], what[:, k * R:(k + 1) * R], NC, R)
                mm.then_inc(s_ct, 1)
            pe.wait_ge(s_c, C_INFO)
            pe.wait_ge(s_prep, PREP_TWO)
            for s in range(3):
                T.transpose(bank[s][:, 0:128], b_two[:, s, :], ident[:, :]).then_inc(s_bt, 1)

            pe.wait_ge(s_prep, PREP_ALL)
            rows_in = {0: x_in, 1: x1_r, 2: x3_r}

            def chain(run, mode):
                def slot(m, u):
                    a = unit(run, m, u + 1)
                    if a.real and not (a.stage == 0 and is_dense(mode, a.i)):
                        if a.stage == 0:
                            pe.wait_ge([Cn["in0"], Cn["in1"]][a.par], (m + (u + 1) // 3 // 2) * 16 + 16)
                        if a.stage == 1:
                            at_least(pe, Cn["rows"], a.n - 4 if not isinstance(a.n, int) or a.i >= 2 else 0)
                        if a.stage == 2:
                            at_least(pe, Cn["rows2"], a.i - 1)
                        at_least(pe, Cn["xT"], turned(mode, a.i, a.pos) - 1)
                        for k in range(4):
                            mm = turn(run.cols[:, k * R:(k + 1) * R], rows_in[a.stage][a.par][:, 128 * k:128 * k + 128], R, 128)
                        mm.then_inc(Cn["rowsT"], 1)
                    a = unit(run, m, u)
                    if a.real:
                        if a.stage == 0 and is_dense(mode, a.i):
                            pe.wait_ge([Cn["in0"], Cn["in1"]][a.par], (m + u // 3 // 2) * 16 + 16)
                        else:
                            pe.wait_ge(Cn["xT"], turned(mode, a.i, a.pos))
                        columns = columns_of(mode, a)
                        at_least(pe, Cn["hid"], a.n + 1 - run.ups)
                        T.matmul(run.up[a.b2][:, 0, 0:CH], w_top[a.stage][:, :], columns[:, :], start=True, stop=True)
                        T.matmul(run.up[a.b2][:, 1, 0:CH], w_bot[a.stage][:, :], columns[:, :], start=True, stop=True)\
                         .then_inc(Cn["up"], 1)
                    a = unit(run, m, u - 2)
                    if a.real:
                        pe.wait_ge(Cn["res"], a.n + 1)
                        at_least(pe, Cn["rows"], a.n - 1)
                        for k in range(4):
                            to, from_ = run.rows[a.b2][0:R, 128 * k:128 * k + 128], rT[a.b2][:, k * R:(k + 1) * R]
                            if a.stage == 0:
                                mm = T.matmul(to, from_, cmat[:, :], start=True, stop=True)
                            else:
                                mm = turn(to, from_, 128, R)
                        mm.then_inc(Cn["resT"], 1)
                    a = unit(run, m, u - 1)
                    if a.real:
                        pe.wait_ge(Cn["hid"], a.n + 1)
                        at_least(pe, Cn["res"], a.n)
                        T.matmul(run.down[0:D, 0:CH], w_dn[a.stage][:, 0:D], hid[a.b2][:, 0, :], start=True, stop=True)
                        T.matmul(run.down[D:128, 0:CH], w_dn[a.stage][:, 0:D], hid[a.b2][:, 1, :], start=True, stop=True)\
                         .then_inc(Cn["dn"], 1)
                return slot

            main_slots(lambda mode: chain(MAIN, mode), pe)

            MT, XT, HT, OT, AT, UT = bank[0], bank[1], pair[0][:, 0, :], bank[2], bank[3], pair[0][:, 1, :]
            HT2 = pair[1][:, 0, :]
            XC = pair[1][:, 1, :]

            def tiles_to_cols(dst, src):
                for k in range(TC):
                    mm = turn(dst[:, k * R:(k + 1) * R], src[:, k * 128:(k + 1) * 128], R, 128)
                return mm

            def cols_to_tiles(dst, src):
                for k in range(TC):
                    mm = turn(dst[0:R, k * 128:(k + 1) * 128], src[:, k * R:(k + 1) * R], 128, R)
                return mm

            def down_rows(dst, h, w):
                for k in range(TC):
                    mm = T.matmul(dst[0:R, 128 * k:128 * k + 128], h[:, k * R:(k + 1) * R], w[:, :], start=True, stop=True)
                return mm

            pe.wait_ge(Cn["rows"], 6 * MAIN.hi)
            pe.wait_ge(s_ones, EARLY_ONES)

            def slot_a(at):
                if c := at(0):
                    k, q, h, p = c
                    at_least(pe, A_ld[q], h * 48 + 48)
                    at_least(pe, LA["xcol"], k)
                    tiles_to_cols(XT, l_a[q]).then_inc(LA["xdT"].sem, 1)
                if c := at(1):
                    k, q, h, p = c
                    at_least(pe, LA["msg"], k + 1)
                    at_least(pe, LA["agg"], k)
                    tiles_to_cols(MT, m_r[p]).then_inc(LA["msgT"].sem, 1)
                    at_least(pe, LA["xcol"], k + 1)
                    at_least(pe, LA["hid"], k)
                    T.matmul(HT[:, 0:CH], w_top[0][:, :], lxT[q][:, :], start=True, stop=True).then_inc(LA["up"].sem, 1)
                if c := at(2):
                    k, q, h, p = c
                    at_least(pe, LA["agg"], k + 1)
                    at_least(pe, LA["t2"], k)
                    for i in range(TC):
                        mm = T.matmul(AT[0:R, i * 128:(i + 1) * 128], agg[p][:, i * R:(i + 1) * R], cmat[:, :],
                                      start=True, stop=True)
                    mm.then_inc(LA["aggT"].sem, 1)
                    at_least(pe, LA["hid"], k + 1)
                    at_least(pe, LA["t1"], k)
                    down_rows(OT, lhid[p], w_dn[0]).then_inc(LA["dn"].sem, 1)
                    at_least(pe, LA["t4"], k)
                    down_rows(XC, lxT[q], x_up).then_inc(LA["xc"].sem, 1)
            lagged_slots(slot_a, pe, 5)
            at_least(pe, LA["rows"], NC)

            def slot_b(at):
                if c := at(3):
                    k, q, h, p = c
                    at_least(pe, LB["u"], k + 1)
                    at_least(pe, LB["ucol"], k)
                    tiles_to_cols(UT, u_r[p]).then_inc(LB["uT"].sem, 1)
                if c := at(1):
                    k, q, h, p = c
                    at_least(pe, LB["msg"], k + 1)
                    at_least(pe, LB["agg"], k)
                    tiles_to_cols(MT, m_r[p]).then_inc(LB["msgT"].sem, 1)
                if c := at(2):
                    k, q, h, p = c
                    at_least(pe, LB["agg"], k + 1)
                    at_least(pe, LB["t2"], k)
                    cols_to_tiles(AT, agg[p]).then_inc(LB["aggT"].sem, 1)
                if c := at(4):
                    k, q, h, p = c
                    at_least(pe, LB["hid"], k + 1)
                    at_least(pe, LB["rows"], k)
                    down_rows(OT, lhid[p], w_dn[1]).then_inc(LB["dn"].sem, 1)
                if c := at(3):
                    k, q, h, p = c
                    at_least(pe, LB["ucol"], k + 1)
                    at_least(pe, LB["hid"], k)
                    T.matmul(HT[:, 0:CH], w_top[1][:, :], lxT[p][:, :], start=True, stop=True).then_inc(LB["up"].sem, 1)
            lagged_slots(slot_b, pe, 5)
            at_least(pe, LB["rows"], NC)

            def slot_c(at):
                if c := at(1):
                    k, q, h, p = c
                    at_least(pe, LC["msg"], k + 1)
                    at_least(pe, LC["agg"], k)
                    tiles_to_cols(MT, m_r[p]).then_inc(LC["msgT"].sem, 1)

            def after_c(at):
                if c := at(2):
                    k, q, h, p = c
                    at_least(pe, LC["agg"], k + 1)
                    at_least(pe, LC["t1"], k)
                    cols_to_tiles(AT, agg[p]).then_inc(LC["aggT"].sem, 1)
            shared_slots(slot_c, beside(lambda mode: chain(WITH_C, mode)), WITH_C, pe, 4, after_c)
            at_least(pe, LC["rows"], NC)

            def slot_d(at):
                if c := at(1):
                    k, q, h, p = c
                    at_least(pe, LD["lky2"], k + 1)
                    at_least(pe, LD["col"], k)
                    tiles_to_cols(MT, m_r[p]).then_inc(LD["lkyT"].sem, 1)
                if c := at(2):
                    k, q, h, p = c
                    at_least(pe, LD["col"], k + 1)
                    at_least(pe, LD["zc"], k)
                    T.matmul(AT[0:128, 0:CH], gat_w[:, :], lxT[p][:, :], start=True, stop=True).then_inc(LD["zx"].sem, 1)
            shared_slots(slot_d, beside(lambda mode: chain(WITH_D, mode)), WITH_D, pe, 4)
            pe.wait_ge(Cn["rows"], 6 * WITH_D.hi)
            summaries(1, LD["c"], D_SUM1, LD["ct"])
            pe.wait_ge(LD["c"], D_CARRY1)
            turn(bank[3][0:NC, 128:129], carry_r[0:1, 1:NC + 1], 1, NC).then_inc(LD["ct"], 1)
            summaries(1, LD["c"], D_SUM2, LD["ct"])
            pe.wait_ge(LD["c"], D_CARRY2)
            turn(bank[3][0:NC, 128:129], carry_r[0:1, 0:NC], 1, NC).then_inc(LD["ct"], 1)
            pe.wait_ge(LD["c"], D_ROWS)

            def after_g(at):
                if c := at(1):
                    k, q, h, p = c
                    at_least(pe, LE["agg"], k + 1)
                    at_least(pe, LE["t1"], k)
                    down_rows(AT, agg[p], g_out).then_inc(LE["aggT"].sem, 1)
            shared_slots(lambda at: None, beside(lambda mode: chain(WITH_G, mode)), WITH_G, pe, 3, after_g)
            pe.wait_ge(Cn["rows"], 6 * MS)
            at_least(pe, LE["rows"], NC)

            def slot_m(at):
                if c := at(1):
                    k, q, h, p = c
                    at_least(pe, LG["fill"], k + 1)
                    at_least(pe, LG["hid"], k)
                    T.matmul(HT[:, 0:CH], w_msg[:, :], l_in[q][:, :], start=True, stop=False)
                    T.matmul(HT[:, 0:CH], w_edge[:, :], l_ea[q][:, :], start=False, stop=True).then_inc(LG["up"].sem, 1)
                if c := at(2):
                    k, q, h, p = c
                    at_least(pe, LG["agg"], k + 1)
                    at_least(pe, LG["fillc"], k + 1)
                    at_least(pe, LG["hid2"], k)
                    T.matmul(HT2[:, 0:CH], w_upd[:, :], l_up[q][:, :], start=True, stop=True).then_inc(LG["up2"].sem, 1)
                if c := at(1):
                    k, q, h, p = c
                    at_least(pe, LG["hid"], k + 1)
                    at_least(pe, LG["msg"], k)
                    T.matmul(XT[0:D, 0:CH], w_msg2[:, :], lhid[p][:, :], start=True, stop=True).then_inc(LG["dn"].sem, 1)
                if c := at(2):
                    k, q, h, p = c
                    at_least(pe, LG["hid2"], k + 1)
                    at_least(pe, LG["t1"], k)
                    for i in range(TC):
                        to, tile = OT[0:R, 128 * i:128 * i + 128], slice(i * R, (i + 1) * R)
                        T.matmul(to, lhid2[p][:, tile], w_dn[2][:, :], start=True, stop=False)
                        mm = T.matmul(to, l_in[q][:, tile], x_dn[:, :], start=False, stop=True)
                    mm.then_inc(LG["dn2"].sem, 1)
                if c := at(0):
                    k, q, h, p = c
                    at_least(pe, M_ga[q], h * 64 + 64)
                    at_least(pe, LG["live"], k + 1)
                    at_least(pe, LG["fill"], k)
                    tiles_to_cols(MT, g_row[q]).then_inc(LG["srcT"].sem, 1)
            pe.wait_ge(s_ones, N_ONES)
            lagged_slots(slot_m, pe, 2)

        @block.scalar
        def _(act):
            A = nc.scalar
            act.wait_ge(s_c, C_DD)
            A.activation(s3_c[:, :, :], s2_c[:, :, :], ACT.Sqrt).then_inc(s_ca, 1)
            act.wait_ge(s_w, ALL_W)
            act.wait_ge(s_prep, PREP_ALL)

            def root(dst, src):
                return A.activation(dst, src, ACT.Sqrt, bias=eps[0:R, :], scale=1.0 / D)

            def chain(run, mode):
                def slot(m, u):
                    a = unit(run, m, u + 1)
                    if a.real and not (a.stage == 0 and is_dense(mode, a.i)):
                        act.wait_ge(Cn["rowsT"], turned(mode, a.i, a.pos))
                        at_least(act, Cn["res"], a.n - 2)
                        A.activation(xT[a.b3][:, :], run.cols[:, 0:CH], ACT.Copy).then_inc(Cn["xT"], 1)
                    a = unit(run, m, u - 5)
                    if a.real and a.stage == 1:
                        act.wait_ge(Cn["ssum2"], a.i + 1)
                        at_least(act, Cn["rstd2"], a.i)
                        root(sd_b[:, :], ss_b[:, :]).then_inc(Cn["std2"], 1)
                    a = unit(run, m, u - 3)
                    if a.real:
                        at_least(act, Cn["rstd"], a.n - 1)
                        act.wait_ge(Cn["ssum"], a.n + 1)
                        root(sd[a.b2][:, :], ss[a.b2][:, :]).then_inc(Cn["std"], 1)
                    a = unit(run, m, u)
                    if a.real:
                        act.wait_ge(Cn["up"], a.n + 1)
                        at_least(act, Cn["dn"], a.n - 1)
                        A.activation(hid[a.b2][:, :, :], run.up[a.b2][:, :, 0:CH], ACT.Relu,
                                     bias=b_up[:, a.stage:a.stage + 1]).then_inc(Cn["hid"], 1)
                    a = unit(run, m, u - 2)
                    if a.real:
                        at_least(act, Cn["ssum"], a.n - 1)
                        act.wait_ge(Cn["resT"], a.n + 1)
                        A.activation(sq[a.b2][:, :], run.rows[a.b2][0:R, :], ACT.Square).then_inc(Cn["sq"], 1)
                    a = unit(run, m, u - 3)
                    if a.real and a.stage == 1:
                        act.wait_ge(Cn["y"], a.i + 1)
                        at_least(act, Cn["ssum2"], a.i)
                        A.activation(sq_b[:, :], y_r[:, :], ACT.Square).then_inc(Cn["sq2"], 1)
                return slot

            main_slots(lambda mode: chain(MAIN, mode), act)

            MT, XT, HT, OT, AT, UT = bank[0], bank[1], pair[0][:, 0, :], bank[2], bank[3], pair[0][:, 1, :]
            HT2 = pair[1][:, 0, :]

            def slot_a(at):
                if c := at(1):
                    k, q, h, p = c
                    at_least(act, LA["up"], k + 1)
                    at_least(act, LA["dn"], k - 1)
                    A.activation(lhid[p][:, :], HT[:, 0:CH], ACT.Relu, bias=b_up[:, 0:1]).then_inc(LA["hid"].sem, 1)
                if c := at(4):
                    k, q, h, p = c
                    at_least(act, LA["ssum"], k + 1)
                    at_least(act, LA["rstd"], k)
                    root(lsd[:, :], lss[:, :]).then_inc(LA["std"].sem, 1)
                if c := at(0):
                    k, q, h, p = c
                    at_least(act, LA["xdT"], k + 1)
                    at_least(act, LA["xc"], k - 3)
                    A.activation(lxT[q][0:D, :], XT[0:D, 0:CH], ACT.Copy).then_inc(LA["xcol"].sem, 1)
                if c := at(3):
                    k, q, h, p = c
                    at_least(act, LA["t4"], k + 1)
                    at_least(act, LA["ssum"], k)
                    A.activation(lsq[:, :], w_rs[p][:, :], ACT.Square).then_inc(LA["sq"].sem, 1)
            act.wait_ge(s_ones, EARLY_ONES)
            lagged_slots(slot_a, act, 5)

            def slot_b(at):
                if c := at(3):
                    k, q, h, p = c
                    at_least(act, LB["uT"], k + 1)
                    at_least(act, LB["up"], k - 1)
                    A.activation(lxT[p][0:D, :], UT[0:D, 0:CH], ACT.Copy).then_inc(LB["ucol"].sem, 1)
                if c := at(4):
                    k, q, h, p = c
                    at_least(act, LB["dn"], k + 1)
                    at_least(act, B_st[q], h * 16)
                    at_least(act, LB["b1"], k - 3)
                    A.activation(n_r[q][:, :].rearrange("p (k f) -> p k f", f=D),
                                 OT[0:R, :].rearrange("p (k f) -> p k f", f=128)[:, :, 0:D], ACT.Copy)\
                     .then_inc(LB["rows"].sem, 1)
                if c := at(3):
                    k, q, h, p = c
                    at_least(act, LB["up"], k + 1)
                    at_least(act, LB["dn"], k - 1)
                    A.activation(lhid[p][:, :], HT[:, 0:CH], ACT.Relu, bias=b_up[:, 1:2]).then_inc(LB["hid"].sem, 1)
            at_least(act, LA["rows"], NC)
            all_stored(act, A_st)
            lagged_slots(slot_b, act, 5)

            def slot_c(at):
                if c := at(4):
                    k, q, h, p = c
                    at_least(act, LC["ssum"], k + 1)
                    at_least(act, LC["rstd"], k)
                    root(lsd[:, :], lss[:, :]).then_inc(LC["std"].sem, 1)

            def after_c(at):
                if c := at(3):
                    k, q, h, p = c
                    at_least(act, LC["t2"], k + 1)
                    at_least(act, LC["ssum"], k)
                    A.activation(lsq[:, :], w_rs[p][:, :], ACT.Square).then_inc(LC["sq"].sem, 1)
            shared_slots(slot_c, beside(lambda mode: chain(WITH_C, mode)), WITH_C, act, 4, after_c)

            def slot_d(at):
                if c := at(1):
                    k, q, h, p = c
                    at_least(act, LD["lkyT"], k + 1)
                    at_least(act, LD["zx"], k - 1)
                    A.activation(lxT[p][:, :], MT[:, 0:CH], ACT.Copy).then_inc(LD["col"].sem, 1)
                if c := at(2):
                    k, q, h, p = c
                    at_least(act, LD["zx"], k + 1)
                    if isinstance(k, int):
                        at_least(act, D_st[p], 16 * (k // 2))
                    else:
                        at_least(act, D_st[p], h * 32 + (q // 2) * 16)
                    A.activation(zx[p][:, :], AT[0:D + 2, 0:CH], ACT.Copy).then_inc(LD["zc"].sem, 1)
            at_least(act, LC["rows"], NC)
            shared_slots(slot_d, beside(lambda mode: chain(WITH_D, mode)), WITH_D, act, 4)
            act.wait_ge(LD["c"], D_EXP)
            A.activation(s2_c[:, :, :], s3_c[:, :, :], ACT.Exp).then_inc(LD["ca"], 1)

            def slot_g(at):
                if c := at(3):
                    k, q, h, p = c
                    at_least(act, LE["ssum"], k + 1)
                    at_least(act, LE["rstd"], k)
                    root(lsd[:, :], lss[:, :]).then_inc(LE["std"].sem, 1)

            def after_g(at):
                if c := at(2):
                    k, q, h, p = c
                    at_least(act, LE["t2"], k + 1)
                    at_least(act, LE["ssum"], k)
                    A.activation(lsq[:, :], w_rs[p][:, :], ACT.Square).then_inc(LE["sq"].sem, 1)
            shared_slots(slot_g, beside(lambda mode: chain(WITH_G, mode)), WITH_G, act, 3, after_g)

            def slot_m(at):
                if c := at(1):
                    k, q, h, p = c
                    at_least(act, LG["fill"], k + 1)
                    at_least(act, LG["up2"], k - 3)
                    A.activation(l_up[q][D:128, :], l_in[q][D:128, :], ACT.Copy).then_inc(LG["fillc"].sem, 1)
                    at_least(act, LG["up"], k + 1)
                    at_least(act, LG["dn"], k - 1)
                    A.activation(lhid[p][:, :], HT[:, 0:CH], ACT.Relu, bias=b_msg[:, :]).then_inc(LG["hid"].sem, 1)
                if c := at(2):
                    k, q, h, p = c
                    at_least(act, LG["up2"], k + 1)
                    at_least(act, LG["dn2"], k - 1)
                    A.activation(lhid2[p][:, :], HT2[:, 0:CH], ACT.Relu, bias=b_up[:, 2:3]).then_inc(LG["hid2"].sem, 1)
                if c := at(1):
                    k, q, h, p = c
                    at_least(act, LG["dn"], k + 1)
                    at_least(act, LG["agg"], k - 3)
                    A.activation(l_m[q][0:D, :], XT[0:D, 0:CH], ACT.Identity, bias=b_msg2[:, :]).then_inc(LG["msg"].sem, 1)
                if c := at(2):
                    k, q, h, p = c
                    at_least(act, LG["t1"], k + 1)
                    at_least(act, LG["ssum"], k)
                    A.activation(lsq[:, :], w_rs[p][:, :], ACT.Square).then_inc(LG["sq"].sem, 1)
                if c := at(0):
                    k, q, h, p = c
                    at_least(act, LG["srcT"], k + 1)
                    at_least(act, LG["dn2"], k - 3)
                    A.activation(l_in[q][0:D, :], MT[0:D, 0:CH], ACT.Copy).then_inc(LG["scol"].sem, 1)
                if c := at(2):
                    k, q, h, p = c
                    at_least(act, LG["ssum"], k + 1)
                    at_least(act, LG["rstd"], k)
                    root(lsd[:, :], lss[:, :]).then_inc(LG["std"].sem, 1)
            at_least(act, LE["rows"], NC)
            lagged_slots(slot_m, act, 2)

        @block.vector
        def _(dve):
            V = nc.vector
            c = [0, 0]

            def step(ins):
                c[0] += 1
                ins.then_inc(s_c, 1)
                dve.wait_ge(s_c, c[0])

            def prep(ins):
                c[1] += 1
                ins.then_inc(s_prep, 1)
                dve.wait_ge(s_prep, c[1])

            V.memset(dst_c[:, :], -1).then_inc(s_pad, 1)
            zeroed = [w_top[s] for s in range(3)] + [w_bot[s] for s in range(3)] + [w_dn[s] for s in range(3)] \
                + [gat_w, w_edge]
            for w in zeroed:
                V.memset(w[:, :], 0.0).then_inc(s_set, 1)
            V.memset(eps[:, :], EPS).then_inc(s_set, 1)

            dve.wait_ge(s_e, ALL_E)
            V.memset(one_c[:, :], 1.0).then_inc(s_c, 1)
            c[0] += 1
            step(V.tensor_copy(dstf_c[:, :], dst_c[:, :]))
            V.tensor_tensor(keep_c[:, :], dstf_c[:, 0:CH], dstf_c[:, 1:CH + 1], ALU.is_equal).then_inc(s_c, 1)
            V.tensor_tensor(on_c[:, :], dstf_c[:, 1:CH + 1], dstf_c[:, 2:CH + 2], ALU.is_equal).then_inc(s_c, 1)
            c[0] += 2
            dve.wait_ge(s_c, c[0])
            assert c[0] == C_ROWS
            step(V.tensor_scalar(last_c[:, :], on_c[:, :], -1.0, 1.0, ALU.mult, ALU.add))
            V.tensor_tensor_scan(s1_c[:, 0, :], keep_c[:, :], one_c[:, :], 0.0, ALU.mult, ALU.add).then_inc(s_c, 1)
            V.tensor_tensor_scan(s1_c[:, 1, :], keep_c[:, :], ew_c[:, :], 0.0, ALU.mult, ALU.add).then_inc(s_c, 1)
            V.tensor_reduce(edge_c[:, 0:1], keep_c[:, :], AX_X, ALU.min).then_inc(s_c, 1)
            V.tensor_reduce(edge_c[:, 1:2], keep_c[:, :], AX_X, ALU.min).then_inc(s_c, 1)
            c[0] += 4
            dve.wait_ge(s_c, c[0])
            step(V.tensor_copy(edge_c[:, 2:4], s1_c[:, :, CH - 1]))
            assert c[0] == C_SUM
            dve.wait_ge(s_ct, 1)
            step(V.tensor_copy(top[:, :, 0:NC], bank[3][0:2, 0:128].rearrange("p (a b) -> p a b", a=2)[:, :, 0:NC]))
            step(V.memset(carry_r[:, :], 0.0))
            step(V.tensor_tensor_scan(carry_r[0:2, 1:NC + 1], top[:, 0, 0:NC], top[:, 1, 0:NC], 0.0, ALU.mult, ALU.add))
            assert c[0] == C_CARRY
            dve.wait_ge(s_ct, 2)
            step(V.tensor_copy(carry_c[:, :], bank[3][0:NC, 128:130]))
            V.tensor_tensor_scan(s1_c[:, 0, :], keep_c[:, :], one_c[:, :], carry_c[:, 0:1], ALU.mult, ALU.add).then_inc(s_c, 1)
            V.tensor_tensor_scan(s1_c[:, 1, :], keep_c[:, :], ew_c[:, :], carry_c[:, 1:2], ALU.mult, ALU.add).then_inc(s_c, 1)
            c[0] += 2
            dve.wait_ge(s_c, c[0])
            step(V.tensor_scalar(s1_c[:, :, :], s1_c[:, :, :], 1.0, None, ALU.add))
            step(V.tensor_scalar(s2_c[:, :, :], s1_c[:, :, :], 1e-30, None, ALU.max))
            assert c[0] == C_DD
            V.memset(info_fill, 1.0).then_inc(s_ones, 1)
            dve.wait_ge(s_ones, 1)
            V.memset(info_fill.rearrange("p (a c) -> p a c", c=4)[:, :, 0:1], -1.0).then_inc(s_set, 1)
            dve.wait_ge(s_ca, 1)
            step(V.reciprocal(s3_c[:, :, :], s3_c[:, :, :]))
            step(V.tensor_scalar(s1_c[:, :, :], s1_c[:, :, :], 0.0, None, ALU.is_gt))
            step(V.tensor_tensor(s3_c[:, :, :], s3_c[:, :, :], s1_c[:, :, :], ALU.mult))
            step(V.tensor_scalar(s2_c[:, 0, :], on_c[:, :], FAR, None, ALU.mult))
            step(V.tensor_tensor(s2_c[:, 0, :], s2_c[:, 0, :], dstf_c[:, 1:CH + 1], ALU.add))
            step(V.tensor_scalar(s1_c[:, 0, :], keep_c[:, :], FAR, None, ALU.mult))
            step(V.tensor_tensor(s1_c[:, 0, :], s1_c[:, 0, :], dstf_c[:, 1:CH + 1], ALU.add))
            assert c[0] == C_DINV

            def tiled(a):
                return (bank + [pair[0][:, 0, :]])[a][0:R, 0:NT].rearrange("p (k c) -> p c k", k=TC)

            def in_tiles(ap):
                return ap.rearrange("p (c k) -> p c k", k=TC)

            dve.wait_ge(s_ct, 7)
            dve.wait_ge(s_pool0, 4)
            V.tensor_copy(in_tiles(d0_t[:, :]), tiled(0)).then_inc(s_c, 1)
            V.tensor_copy(in_tiles(d1_t[:, :]), tiled(1)).then_inc(s_c, 1)
            V.tensor_copy(in_tiles(last_t[:, :]), tiled(2)).then_inc(s_c, 1)
            V.tensor_copy(in_tiles(sidx[:, :]), tiled(3)).then_inc(s_c, 1)
            V.tensor_copy(in_tiles(fidx[:, :]), tiled(4)).then_inc(s_c, 1)
            V.tensor_copy(info_r[:, :, 0], slot_id[:, :]).then_inc(s_c, 1)
            V.memset(info_r[:, :, 3], 0.0).then_inc(s_c, 1)
            c[0] += 7
            dve.wait_ge(s_c, c[0])
            V.tensor_copy(info_r[:, :, 1], d0_t[:, :]).then_inc(s_c, 1)
            V.tensor_copy(info_r[:, :, 2], d1_t[:, :]).then_inc(s_c, 1)
            c[0] += 2
            assert c[0] == C_INFO

            dve.wait_ge(s_w, ALL_W)

            def centre(view, n, width, m):
                prep(V.tensor_reduce(m, view, AX_X, ALU.add))
                prep(V.tensor_scalar(m, m, -1.0 / width, None, ALU.mult))
                prep(V.tensor_tensor(view, view, m.unsqueeze(2).to_broadcast([128, n, width]), ALU.add))

            centre(b_row[:, :, :], 4, D, mean6[:, 0:4])
            for s in range(3):
                centre(w_dn[s][:, 0:D].unsqueeze(1), 1, D, mean6[:, 4 + s:5 + s])
            prep(V.memset(cmat[:, :], 0.0))
            for half_of in (slice(0, D), slice(D, 128)):
                prep(V.memset(cmat[half_of, half_of], -1.0 / D))
            dve.wait_ge(s_pool0, 2)
            prep(V.tensor_tensor(cmat[:, :], cmat[:, :], ident[:, :], ALU.add))
            prep(V.memset(g_out[:, :], 0.0))
            prep(V.tensor_copy(g_out[0:D + 1, 0:D + 1], ident[0:D + 1, 0:D + 1]))
            prep(V.tensor_copy(g_out[D:D + 1, 0:D], b_row[D:D + 1, 2, :]))
            prep(V.memset(x_dn[:, :], 0.0))
            prep(V.tensor_copy(x_dn[D:128, 0:D], ident[D:128, D:128]))
            prep(V.memset(x_up[:, :], 0.0))
            prep(V.tensor_copy(x_up[0:D, 0:D], cmat[0:D, 0:D]))
            prep(V.tensor_copy(x_up[D:D + 1, 0:D], b_row[D:D + 1, 0, :]))
            prep(V.tensor_tensor(gat_tmp[:, :], gat_raw[:, :], gat_att[:, :], ALU.mult))
            prep(V.tensor_reduce(gat_w[0:D, D:D + 1], gat_tmp[0:D, :], AX_X, ALU.add))
            prep(V.tensor_reduce(gat_w[D:128, D + 1:D + 2], gat_tmp[D:128, :], AX_X, ALU.add))
            centre(gat_raw[:, :].unsqueeze(1), 1, D, mean6[:, 7:8])
            prep(V.tensor_copy(gat_w[0:D, 0:D], gat_raw[0:D, :]))
            for s, i in enumerate((0, 1, 3)):
                prep(V.tensor_copy(b_two[:, s, 0:D], b_row[:, i, :]))
                prep(V.tensor_copy(b_two[:, s, D:128], b_row[:, i, :]))
            assert c[1] == PREP_TWO
            dve.wait_ge(s_bt, 3)
            for s in range(3):
                prep(V.tensor_copy(b_dn[:, s:s + 1], bank[s][:, 0:1]))
            for i in (0, 1):
                V.memset(x1_r[i][:, :], 0.0).then_inc(s_prep, 1)
                V.memset(x3_r[i][:, :], 0.0).then_inc(s_prep, 1)
                c[1] += 2
            assert c[1] == PREP_ALL

            iso_sem0, iso_sem1 = [Cn["s0st0"], Cn["s0st1"]], [Cn["s1st0"], Cn["s1st1"]]

            def chain(run, mode):
                known = mode is None

                def stored(first, i):
                    return (i - 2 - first) // 2 + 1

                def first(m, u):
                    def iso0(i):
                        return i < NI if known else mode == "iso"

                    def iso1(i):
                        return 2 <= i < NI + 2 if known else mode == "iso"

                    a = unit(run, m, u - 3)
                    if a.real:
                        dve.wait_ge(Cn["sq"], a.n + 1)
                        at_least(dve, Cn["std"], a.n - 1)
                        V.tensor_reduce(ss[a.b2][:, :], n_view(sq[a.b2][:, :]), AX_X, ALU.add).then_inc(Cn["ssum"], 1)
                    at_m = m + (u - 3) // 3 // 2
                    if a.real and a.stage == 0 and iso0(a.i):
                        if not known or a.i - 2 >= 0:
                            v = 32 * stored(0, a.i) if known else at_m * 32
                            dve.wait_ge(iso_sem0[a.par], v)
                        V.tensor_tensor(h0_r[a.par][:, :], run.rows[a.b2][0:R, :], x_in[a.par][:, :], ALU.subtract).then_inc(Cn["h0"], 1)
                        dve.wait_ge(Cn["h0"], a.i + 1)
                        V.tensor_tensor(n_view(h0_r[a.par][:, :]), n_view(h0_r[a.par][:, :]), row_bias(0, TB),
                                        ALU.subtract).then_inc(Cn["h0b"], 1)
                    at_m = m + (u - 3) // 3 // 2
                    if a.real and a.stage == 1 and iso1(a.i):
                        if not known or a.i - 2 >= 2:
                            v = 48 * stored(2, a.i) if known else at_m * 48 - 48
                            dve.wait_ge(iso_sem1[a.par], v)
                        V.tensor_tensor(h2_r[a.par][:, :], run.rows[a.b2][0:R, :], x1_r[a.par][:, :], ALU.subtract).then_inc(Cn["h2"], 1)
                        dve.wait_ge(Cn["h2"], a.i - 1)
                        V.tensor_tensor(n_view(h2_r[a.par][:, :]), n_view(h2_r[a.par][:, :]), row_bias(1, TB),
                                        ALU.subtract).then_inc(Cn["h2b"], 1)
                def rest(m, u):
                    a = unit(run, m, u - 4)
                    if a.real and a.stage == 1:
                        dve.wait_ge(Cn["sq2"], a.i + 1)
                        at_least(dve, Cn["std2"], a.i)
                        V.tensor_reduce(ss_b[:, :], n_view(sq_b[:, :]), AX_X, ALU.add).then_inc(Cn["ssum2"], 1)
                    a = unit(run, m, u - 5)
                    if a.real and a.stage == 1:
                        dve.wait_ge(Cn["std2"], a.i + 1)
                        V.reciprocal(rs_b[:, :], sd_b[:, :]).then_inc(Cn["rstd2"], 1)
                    a = unit(run, m, u - 3)
                    if a.real:
                        dve.wait_ge(Cn["std"], a.n + 1)
                        V.reciprocal(rs[:, :], sd[a.b2][:, :]).then_inc(Cn["rstd"], 1)
                    a = unit(run, m, u - 5)
                    if a.real and a.stage == 1:
                        dve.wait_ge(Cn["rstd2"], a.i + 1)
                        if not known or a.i >= 2:
                            dve.wait_ge(Cn["rowsT"], turned(mode, a.i, 2))
                        at_m = m + (u - 5) // 3 // 2
                        if (known and 2 <= a.i - 2 < NI + 2) or mode == "iso":
                            v = 48 * stored(2, a.i) if known else at_m * 48 - 48
                            dve.wait_ge(iso_sem1[a.par], v)
                        V.tensor_tensor(n_view(x3_r[a.par][:, :]), n_view(y_r[:, :]), spread(rs_b[:, :], TB), ALU.mult)\
                         .then_inc(Cn["rows2"], 1)
                    a = unit(run, m, u - 3)
                    if a.real:
                        qq = (u - 3) // 3 // 2
                        at_m = m + qq
                        dve.wait_ge(Cn["rstd"], a.n + 1)
                        dst = {0: x1_r, 1: x2_r, 2: x4_r}[a.stage][a.par]
                        if a.stage == 0:
                            if not known or a.i >= 2:
                                dve.wait_ge(Cn["rowsT"], turned(mode, a.i, 0))
                            if (known and 0 <= a.i - 2 < NI) or mode == "iso":
                                v = 32 * stored(0, a.i) if known else at_m * 32
                                dve.wait_ge(iso_sem0[a.par], v)
                        if a.stage == 1:
                            if (known and 2 <= a.i - 2 < NI + 2) or mode == "iso":
                                v = 48 * stored(2, a.i) if known else at_m * 48 - 48
                                dve.wait_ge(iso_sem1[a.par], v)
                        if a.stage == 2:
                            if (known and NI + 4 <= a.i - 2) or mode == "dense":
                                v = 16 * stored(NI + 4, a.i) if known else at_m * 16 - 16 * ((NI + 5) // 2 - a.par)
                                dve.wait_ge([Cn["out0"], Cn["out1"]][a.par], v)
                        V.tensor_tensor(n_view(dst[:, :]), n_view(run.rows[a.b2][0:R, :]), spread(rs[:, :], TB), ALU.mult)\
                         .then_inc(Cn["rows"], 1)
                    a = unit(run, m, u - 3)
                    if a.real:
                        if a.stage == 1:
                            dve.wait_ge(Cn["rows"], a.n + 1)
                            at_least(dve, Cn["rows2"], a.i)
                            V.tensor_tensor(n_view(y_r[:, :]), n_view(x2_r[a.par][:, :]), row_bias(2, TB), ALU.add)\
                             .then_inc(Cn["y"], 1)
                    a = unit(run, m, u - 1)
                    if a.real:
                        dve.wait_ge(Cn["dn"], a.n + 1)
                        at_least(dve, Cn["resT"], a.n - 1)
                        V.scalar_tensor_tensor(rT[a.b2][:, :], run.down[:, 0:CH], b_dn[:, a.stage:a.stage + 1],
                                               columns_of(mode, a)[:, :], ALU.add, ALU.add).then_inc(Cn["res"], 1)
                def slot(m, u):
                    first(m, u)
                    rest(m, u)

                return slot, first, rest

            def set_for_levels():
                for i in range(4):
                    V.memset(lxT[i][:, :], 0.0).then_inc(s_ones, 1)
                    dve.wait_ge(s_ones, 2 + i * 2)
                    V.memset(lxT[i][D:D + 1, :], 1.0).then_inc(s_ones, 1)
                for buf in l_a + m_r + u_r + agg:
                    V.memset(buf[:, :], 0.0).then_inc(s_ones, 1)

            main_slots(lambda mode: chain(MAIN, mode)[0], dve, set_for_levels)

            dve.wait_ge(P["copied"], 5 * NI)
            step(V.tensor_scalar(gfl[:, :], info_r[:, :, 0], 0.0, None, ALU.is_ge))
            step(V.tensor_tensor(w0_t[:, :], info_r[:, :, 0], gbase[:, :], ALU.subtract))
            step(V.tensor_tensor(w0_t[:, :], w0_t[:, :], gfl[:, :], ALU.mult))
            step(V.tensor_tensor(gidx[:, :], w0_t[:, :], gbase[:, :], ALU.add))
            step(V.tensor_copy(w0_t[:, :], info_r[:, :, 1]))
            step(V.tensor_tensor(w1_t[:, :], info_r[:, :, 2], ew_t[:, :], ALU.mult))
            step(V.tensor_tensor(d1q_t[:, :], d1_t[:, :], d1_t[:, :], ALU.mult))
            assert c[0] == C_ALL
            dve.wait_ge(s_ones, EARLY_ONES)

            def v4(ap):
                return ap.rearrange("p (k f) -> p k f", f=D)

            def tile_scalar(tt, k):
                return tt[:, bass.ds(k * TC, TC)].unsqueeze(2).to_broadcast([R, TC, D])

            def scan(S, k, q, data, width, name_done, first, msg_sem):
                at_least(dve, msg_sem, k + 1)
                init = 0.0 if first else agg[(q - 1) % 2][0:width, CH - 1:CH]
                V.tensor_tensor_scan(agg[q % 2][0:width, :], l_k[q][0:width, :], data, init,
                                     ALU.mult, ALU.add).then_inc(name_done.sem, 1)

            MT, XT, OT, AT = bank[0], bank[1], bank[2], bank[3]
            OTv = OT[0:R, :].rearrange("p (k f) -> p k f", f=128)[:, :, 0:D]
            ATv = AT[0:R, :].rearrange("p (k f) -> p k f", f=128)[:, :, 0:D]

            XCv = pair[1][0:R, 1, :].rearrange("p (k f) -> p k f", f=128)[:, :, 0:D]

            def slot_a(at):
                if c := at(3):
                    k, q, h, p = c
                    at_least(dve, LA["t4"], k)
                    at_least(dve, LA["dn"], k + 1)
                    V.tensor_tensor(v4(v_r[:, :]), OTv, tile_scalar(d0_t, k), ALU.mult).then_inc(LA["t1"].sem, 1)
                if c := at(4):
                    k, q, h, p = c
                    at_least(dve, LA["sq"], k + 1)
                    V.tensor_reduce(lss[:, :], v4(lsq[:, :]), AX_X, ALU.add).then_inc(LA["ssum"].sem, 1)
                if c := at(3):
                    k, q, h, p = c
                    at_least(dve, LA["t1"], k + 1)
                    at_least(dve, LA["aggT"], k + 1)
                    V.tensor_tensor(v4(v_r[:, :]), v4(v_r[:, :]), ATv, ALU.add).then_inc(LA["t2"].sem, 1)
                if c := at(0):
                    k, q, h, p = c
                    at_least(dve, A_ld[q], h * 48 + 48)
                    at_least(dve, LA["msgT"], k - 1)
                    V.tensor_tensor(half(m_r[p]), v4(l_src[q][:, :]), tile_scalar(w0_t, k), ALU.mult)\
                     .then_inc(LA["msg"].sem, 1)
                if c := at(3):
                    k, q, h, p = c
                    at_least(dve, LA["t2"], k + 1)
                    V.tensor_tensor(v4(v_r[:, :]), v4(v_r[:, :]), tile_scalar(d0_t, k), ALU.mult).then_inc(LA["t3"].sem, 1)
                if c := at(4):
                    k, q, h, p = c
                    at_least(dve, LA["std"], k + 1)
                    V.reciprocal(lrs[:, :], lsd[:, :]).then_inc(LA["rstd"].sem, 1)
                if c := at(3):
                    k, q, h, p = c
                    at_least(dve, LA["t3"], k + 1)
                    at_least(dve, LA["xc"], k + 1)
                    at_least(dve, LA["rows"], k - 1)
                    V.tensor_tensor(v4(w_rs[p][:, :]), v4(v_r[:, :]), XCv, ALU.add).then_inc(LA["t4"].sem, 1)
                if c := at(1):
                    k, q, h, p = c
                    at_least(dve, LA["aggT"], k - 1)
                    scan(LA, k, q, MT[0:D, 0:CH], D, LA["agg"], isinstance(k, int) and k == 0, LA["msgT"])
                if c := at(4):
                    k, q, h, p = c
                    at_least(dve, LA["rstd"], k + 1)
                    at_least(dve, A_st[q], h * 16)
                    V.tensor_tensor(v4(n_r[q][:, :]), v4(w_rs[p][:, :]), spread(lrs[:, :], TC), ALU.mult)\
                     .then_inc(LA["rows"].sem, 1)
            lagged_slots(slot_a, dve, 5)

            def slot_b(at):
                if c := at(1):
                    k, q, h, p = c
                    at_least(dve, B_ld[q], h * 32 + 32)
                    at_least(dve, LB["aggT"], k - 1)
                    scan(LB, k, q, MT[0:D, 0:CH], D, LB["agg"], isinstance(k, int) and k == 0, LB["msgT"])
                if c := at(5):
                    k, q, h, p = c
                    at_least(dve, LB["rows"], k + 1)
                    at_least(dve, LB["base"], k)
                    V.tensor_tensor(v4(w_rs[0][:, :]), v4(n_r[q][:, :]), tile_scalar(d1q_t, k), ALU.mult).then_inc(LB["b1"].sem, 1)
                if c := at(2):
                    k, q, h, p = c
                    at_least(dve, LB["u"], k)
                    V.tensor_tensor(v4(v_r[:, :]), half(l_a[q]), tile_scalar(d1_t, k), ALU.mult).then_inc(LB["t1"].sem, 1)
                if c := at(5):
                    k, q, h, p = c
                    at_least(dve, LB["b1"], k + 1)
                    at_least(dve, LB["xb"], k + 1)
                    at_least(dve, B_bst[q], h * 16)
                    V.tensor_tensor(l_src[q][:, :], w_rs[0][:, :], l_b[q][:, :], ALU.add).then_inc(LB["base"].sem, 1)
                if c := at(2):
                    k, q, h, p = c
                    at_least(dve, LB["t1"], k + 1)
                    at_least(dve, LB["aggT"], k + 1)
                    V.tensor_tensor(v4(v_r[:, :]), v4(v_r[:, :]), ATv, ALU.add).then_inc(LB["t2"].sem, 1)
                    at_least(dve, LB["base"], k - 3)
                    V.tensor_tensor(v4(l_b[q][:, :]), half(l_a[q]), row_bias(1, TC), ALU.add).then_inc(LB["xb"].sem, 1)
                if c := at(0):
                    k, q, h, p = c
                    at_least(dve, B_ga[q], h * 64 + 64)
                    at_least(dve, LB["msgT"], k - 1)
                    V.tensor_tensor(half(m_r[p]), half(g_row[q]), tile_scalar(w1_t, k), ALU.mult)\
                     .then_inc(LB["msg"].sem, 1)
                if c := at(2):
                    k, q, h, p = c
                    at_least(dve, LB["t2"], k + 1)
                    at_least(dve, LB["uT"], k - 1)
                    V.tensor_tensor(half(u_r[p]), v4(v_r[:, :]), tile_scalar(d1_t, k), ALU.mult).then_inc(LB["u"].sem, 1)
            at_least(dve, LA["rows"], NC)
            lagged_slots(slot_b, dve, 5)
            at_least(dve, LB["rows"], NC)
            all_stored(dve, B_st)

            def slot_c(at):
                if c := at(3):
                    k, q, h, p = c
                    at_least(dve, LC["t2"], k)
                    at_least(dve, LC["aggT"], k + 1)
                    V.tensor_tensor(v4(v_r[:, :]), ATv, tile_scalar(d1_t, k), ALU.mult).then_inc(LC["t1"].sem, 1)
                if c := at(4):
                    k, q, h, p = c
                    at_least(dve, LC["sq"], k + 1)
                    V.tensor_reduce(lss[:, :], v4(lsq[:, :]), AX_X, ALU.add).then_inc(LC["ssum"].sem, 1)
                if c := at(3):
                    k, q, h, p = c
                    at_least(dve, LC["t1"], k + 1)
                    at_least(dve, C_ld[q], h * 32 + 32)
                    at_least(dve, LC["rows"], k - 1)
                    V.tensor_tensor(w_rs[p][:, :], v_r[:, :], l_b[q][:, :], ALU.add).then_inc(LC["t2"].sem, 1)
                if c := at(0):
                    k, q, h, p = c
                    at_least(dve, C_ga[q], h * 64 + 64)
                    at_least(dve, LC["msgT"], k - 1)
                    V.tensor_tensor(half(m_r[p]), half(g_row[q]), tile_scalar(w1_t, k), ALU.mult)\
                     .then_inc(LC["msg"].sem, 1)
                if c := at(4):
                    k, q, h, p = c
                    at_least(dve, LC["std"], k + 1)
                    V.reciprocal(lrs[:, :], lsd[:, :]).then_inc(LC["rstd"].sem, 1)
                if c := at(1):
                    k, q, h, p = c
                    at_least(dve, C_ld[q], h * 32 + 32)
                    at_least(dve, LC["aggT"], k - 1)
                    scan(LC, k, q, MT[0:D, 0:CH], D, LC["agg"], isinstance(k, int) and k == 0, LC["msgT"])
                if c := at(4):
                    k, q, h, p = c
                    at_least(dve, LC["rstd"], k + 1)
                    at_least(dve, C_st[q], h * 16)
                    V.tensor_tensor(v4(n_r[q][:, :]), v4(w_rs[p][:, :]), spread(lrs[:, :], TC), ALU.mult)\
                     .then_inc(LC["rows"].sem, 1)
            first, rest = [beside(lambda mode, part=part: chain(WITH_C, mode)[part]) for part in (1, 2)]
            shared_slots(slot_c, rest, WITH_C, dve, 4, before=first)
            at_least(dve, LC["rows"], NC)

            def slot_d(at):
                if c := at(0):
                    k, q, h, p = c
                    mv = m_r[p][:, :].rearrange("p (k f) -> p k f", f=128)
                    at_least(dve, D_ga[q], h * 64 + 64)
                    at_least(dve, LD["lkyT"], k - 1)
                    V.scalar_tensor_tensor(mv[:, :, 0:D], half(g_row[q]), 0.2, half(g_row[q]),
                                           ALU.mult, ALU.max).then_inc(LD["lky1"].sem, 1)
                    at_least(dve, D_ld[q], h * 16 + 16)
                    V.scalar_tensor_tensor(mv[:, :, D:128], half(l_a[q]), 0.2, half(l_a[q]),
                                           ALU.mult, ALU.max).then_inc(LD["lky2"].sem, 1)
            first, rest = [beside(lambda mode, part=part: chain(WITH_D, mode)[part]) for part in (1, 2)]
            shared_slots(slot_d, rest, WITH_D, dve, 4, before=first)

            dc = [0]

            def dstep(ins):
                dc[0] += 1
                ins.then_inc(LD["c"], 1)
                dve.wait_ge(LD["c"], dc[0])

            for buf in l_z:
                V.memset(buf[D:D + 1, :], 1.0).then_inc(s_ones, 1)
            for r in range(2):
                dve.wait_ge(iso_sem0[r], 32 * len(range(r, NI, 2)))
                dve.wait_ge(iso_sem1[r], 48 * len(range(r, NI, 2)))
            for buf in l_ea:
                V.memset(buf[:, :], 0.0).then_inc(s_ones, 1)
            dve.wait_ge(s_ones, N_ONES)
            dve.wait_ge(s_rows, 64)
            el, er, s3a, s3b = s1_c[:, 0, :], s1_c[:, 1, :], s3_c[:, 0, :], s3_c[:, 1, :]
            dstep(V.tensor_tensor(er, er, last_c[:, :], ALU.mult))
            dstep(V.tensor_tensor_scan(s3a[:, ::-1], on_c[:, ::-1], er[:, ::-1], 0.0, ALU.mult, ALU.add))
            dstep(V.tensor_reduce(edge_c[:, 0:1], on_c[:, :], AX_X, ALU.min))
            dstep(V.tensor_copy(edge_c[:, 2:3], s3a[:, 0:1]))
            assert dc[0] == D_SUM1
            dve.wait_ge(LD["ct"], 1)
            dstep(V.tensor_copy(top[0:1, :, 0:NC], bank[3][0:1, 0:128].rearrange("p (a b) -> p a b", a=2)[:, :, 0:NC]))
            dstep(V.memset(carry_r[:, :], 0.0))
            dstep(V.tensor_tensor_scan(carry_r[0:1, 0:NC][:, ::-1], top[0:1, 0, 0:NC][:, ::-1],
                                       top[0:1, 1, 0:NC][:, ::-1], 0.0, ALU.mult, ALU.add))
            assert dc[0] == D_CARRY1
            dve.wait_ge(LD["ct"], 2)
            dstep(V.tensor_copy(carry_c[:, 0:1], bank[3][0:NC, 128:129]))
            dstep(V.tensor_tensor_scan(s3a[:, ::-1], on_c[:, ::-1], er[:, ::-1], carry_c[:, 0:1], ALU.mult, ALU.add))
            dstep(V.tensor_tensor(s3b, el, s3a, ALU.add))
            dstep(V.scalar_tensor_tensor(el, s3b, 0.2, s3b, ALU.mult, ALU.max))
            dstep(V.tensor_scalar(er, keep_c[:, :], -1.0, BIG, ALU.add, ALU.mult))
            dstep(V.tensor_tensor_scan(s3a, er, el, -BIG, ALU.add, ALU.max))
            dstep(V.tensor_reduce(edge_c[:, 0:1], er, AX_X, ALU.min))
            dstep(V.tensor_copy(edge_c[:, 2:3], s3a[:, CH - 1:CH]))
            assert dc[0] == D_SUM2
            dve.wait_ge(LD["ct"], 3)
            dstep(V.tensor_copy(top[0:1, :, 0:NC], bank[3][0:1, 0:128].rearrange("p (a b) -> p a b", a=2)[:, :, 0:NC]))
            dstep(V.memset(carry_r[:, :], -BIG))
            dstep(V.tensor_tensor_scan(carry_r[0:1, 1:NC + 1], top[0:1, 0, 0:NC], top[0:1, 1, 0:NC], -BIG, ALU.add, ALU.max))
            assert dc[0] == D_CARRY2
            dve.wait_ge(LD["ct"], 4)
            dstep(V.tensor_copy(carry_c[:, 0:1], bank[3][0:NC, 128:129]))
            mx = dstf_c[:, 0:CH + 1]
            dstep(V.tensor_copy(mx[:, 0:1], carry_c[:, 0:1]))
            dstep(V.tensor_tensor_scan(mx[:, 1:CH + 1], er, el, carry_c[:, 0:1], ALU.add, ALU.max))
            dstep(V.tensor_tensor(s3a, mx[:, 0:CH], mx[:, 1:CH + 1], ALU.subtract))
            dstep(V.tensor_scalar(s3a, s3a, 0.0, None, ALU.min))
            dstep(V.tensor_tensor(s3b, el, mx[:, 1:CH + 1], ALU.subtract))
            assert dc[0] == D_EXP
            dve.wait_ge(LD["ca"], 1)
            dstep(V.tensor_tensor(s2_c[:, 0, :], s2_c[:, 0, :], keep_c[:, :], ALU.mult))
            assert dc[0] == D_ROWS

            AT65 = AT[0:R, :].rearrange("p (k f) -> p k f", f=128)

            def slot_g(at):
                if c := at(2):
                    k, q, h, p = c
                    at_least(dve, LE["aggT"], k + 1)
                    at_least(dve, LE["t1"], k)
                    V.tensor_scalar(lden[:, :], AT65[:, :, D], 1e-30, None, ALU.max).then_inc(LE["den"].sem, 1)
                if c := at(3):
                    k, q, h, p = c
                    at_least(dve, LE["sq"], k + 1)
                    V.tensor_reduce(lss[:, :], v4(lsq[:, :]), AX_X, ALU.add).then_inc(LE["ssum"].sem, 1)
                if c := at(2):
                    k, q, h, p = c
                    at_least(dve, LE["den"], k + 1)
                    V.reciprocal(lrden[:, :], lden[:, :]).then_inc(LE["rden"].sem, 1)
                if c := at(2):
                    k, q, h, p = c
                    at_least(dve, LE["rden"], k + 1)
                    at_least(dve, LE["t2"], k)
                    V.tensor_tensor(v4(v_r[:, :]), AT65[:, :, 0:D], spread(lrden[:, :], TC), ALU.mult).then_inc(LE["t1"].sem, 1)
                if c := at(0):
                    k, q, h, p = c
                    at_least(dve, LE["aggT"], k - 1)
                    at_least(dve, LE["msg"], k + 1)
                    at_least(dve, G_ld[q], h * 64 + 64)
                    init = 0.0 if isinstance(k, int) and k == 0 else agg[(q - 1) % 2][0:D + 1, CH - 1:CH]
                    at_least(dve, LE["agg"], k)
                    V.tensor_tensor_scan(agg[q % 2][0:D + 1, :], l_k[q][0:D + 1, :], l_m[q][:, :], init,
                                         ALU.mult, ALU.add).then_inc(LE["agg"].sem, 1)
                if c := at(3):
                    k, q, h, p = c
                    at_least(dve, LE["std"], k + 1)
                    V.reciprocal(lrs[:, :], lsd[:, :]).then_inc(LE["rstd"].sem, 1)
                if c := at(2):
                    k, q, h, p = c
                    at_least(dve, LE["t1"], k + 1)
                    at_least(dve, LE["rows"], k - 1)
                    V.tensor_tensor(w_rs[p][:, :], v_r[:, :], l_b[q][:, :], ALU.add).then_inc(LE["t2"].sem, 1)
                if c := at(3):
                    k, q, h, p = c
                    at_least(dve, LE["rstd"], k + 1)
                    at_least(dve, G_st[q], h * 16)
                    V.tensor_tensor(v4(n_r[q][:, :]), v4(w_rs[p][:, :]), spread(lrs[:, :], TC), ALU.mult)\
                     .then_inc(LE["rows"].sem, 1)
            first, rest = [beside(lambda mode, part=part: chain(WITH_G, mode)[part]) for part in (1, 2)]
            shared_slots(slot_g, rest, WITH_G, dve, 3, before=first)
            at_least(dve, LE["rows"], NC)

            def slot_m(at):
                if c := at(0):
                    k, q, h, p = c
                    at_least(dve, M_ld[q], h * 48 + 48)
                    at_least(dve, LG["srcT"], k - 3)
                    g_right = g_row[q][:, :].rearrange("p (k f) -> p k f", f=128)[:, :, D:128]
                    V.tensor_tensor(g_right, half(l_a[q]), tile_scalar(last_t, mirror(dve, k)), ALU.mult)\
                     .then_inc(LG["live"].sem, 1)
                if c := at(1):
                    k, q, h, p = c
                    at_least(dve, LG["msg"], k + 1)
                    at_least(dve, LG["agg"], k)
                    at_least(dve, LG["up2"], k - 3)
                    init = 0.0 if isinstance(k, int) and k == 0 else l_up[(q - 1) % 4][0:D, 0:1]
                    V.tensor_tensor_scan(l_up[q][0:D, ::-1], l_k[q][0:D, ::-1], l_m[q][0:D, ::-1], init,
                                         ALU.mult, ALU.add).then_inc(LG["agg"].sem, 1)
                if c := at(2):
                    k, q, h, p = c
                    at_least(dve, LG["dn2"], k + 1)
                    at_least(dve, LG["rows"], k - 1)
                    V.tensor_tensor(v4(w_rs[p][:, :]), OTv, row_bias(3, TC), ALU.add).then_inc(LG["t1"].sem, 1)
                    at_least(dve, LG["sq"], k + 1)
                    V.tensor_reduce(lss[:, :], v4(lsq[:, :]), AX_X, ALU.add).then_inc(LG["ssum"].sem, 1)
                if c := at(0):
                    k, q, h, p = c
                    at_least(dve, LG["scol"], k + 1)
                    at_least(dve, LG["fill"], k)
                    init = 0.0 if isinstance(k, int) and k == 0 else l_in[(q - 1) % 4][D:128, 0:1]
                    V.tensor_tensor_scan(l_in[q][D:128, ::-1], l_k[q][D:128, ::-1], MT[D:128, 0:CH][:, ::-1], init,
                                         ALU.mult, ALU.add).then_inc(LG["fill"].sem, 1)
                if c := at(2):
                    k, q, h, p = c
                    at_least(dve, LG["std"], k + 1)
                    V.reciprocal(lrs[:, :], lsd[:, :]).then_inc(LG["rstd"].sem, 1)
                    at_least(dve, LG["rstd"], k + 1)
                    if isinstance(k, int):
                        at_least(dve, M_sc[p], 64 * ((k - 4) // 2 + 1))
                    else:
                        at_least(dve, M_sc[p], h * 128 + ((q // 2) * 64 - 64))
                    V.tensor_tensor(v4(n_r[q][:, :]), v4(w_rs[p][:, :]), spread(lrs[:, :], TC), ALU.mult)\
                     .then_inc(LG["rows"].sem, 1)
            lagged_slots(slot_m, dve, 2)


C_ROWS = 4
C_SUM = 10
C_CARRY = 13
C_DD = 18
C_DINV = 25
C_INFO = 34
C_ALL = 41
PREP_TWO = 37
PREP_ALL = 44
D_SUM1, D_CARRY1, D_SUM2, D_CARRY2, D_EXP, D_ROWS = 4, 7, 15, 18, 24, 25

_INS = ["x", "dst", "edge_weight",
        "L0_gnn_W1", "L0_gnn_b1", "L0_gnn_W2", "L0_gnn_b2", "L1_gnn_W1", "L1_gnn_b1", "L1_gnn_W2", "L1_gnn_b2",
        "L2_gnn_W", "L2_gnn_attn_l", "L2_gnn_attn_r", "L2_gnn_bias", "L3_gnn_mW1", "L3_gnn_mb1", "L3_gnn_mW2",
        "L3_gnn_mb2", "L3_gnn_uW1", "L3_gnn_ub1", "L3_gnn_uW2", "L3_gnn_ub2"]


def kernel(**inputs):
    import numpy as _np
    import concourse.bacc as _bacc
    from concourse import mybir as _mybir
    from concourse.bass_utils import run_bass_kernel_spmd as _run

    given = {n: _np.asarray(inputs[n]) for n in _INS}
    for n, name in (("src", "src_by_tile"), ("dst", "dst_by_tile"), ("edge_weight", "edge_weight_by_tile")):
        given[name] = _np.asarray(inputs[n]).reshape(NT, R).T
    given["x_cols"] = given["x"].reshape(NB, R, TC, 2, D).transpose(0, 3, 4, 2, 1).reshape(NB, 128, CH)
    given["edge_attr_cols"] = _np.asarray(inputs["edge_attr_32"]).T
    nc = _bacc.Bacc("TRN2", target_bir_lowering=False, num_devices=1)
    arrays, t = {}, {}
    for name, a in given.items():
        a = _np.ascontiguousarray(a)
        arrays[f"in_{name}"] = a
        t[name] = nc.dram_tensor(f"in_{name}", a.shape, _mybir.dt.from_np(a.dtype), kind="ExternalInput").ap()
    out = nc.dram_tensor("out_rows", (N, D), F32, kind="ExternalOutput").ap()
    build(nc, t, out)
    r = _run(nc, [arrays], core_ids=[0])
    return r.results[0]["out_rows"]
```
